# Optimizing a Trainium2 kernel written in Bass

```python
import numpy as np
import jax
import jax.numpy as jnp

def _softmax(x, axis=-1):
    return jax.nn.softmax(x, axis=axis)

def _gelu(x):
    return jax.nn.gelu(x, approximate=True)

def _silu(x):
    return jax.nn.silu(x)

def _sigmoid(x):
    return jax.nn.sigmoid(x)

def _layernorm(x, axis=-1, eps=1e-05):
    m = jnp.mean(x, axis=axis, keepdims=True)
    v = jnp.var(x, axis=axis, keepdims=True)
    return (x - m) / jnp.sqrt(v + eps)

def _scatter_add(tgt, idx, src, axis=0):
    return tgt.at[idx].add(src)

def _segment_sum(src, seg, n):
    return jax.ops.segment_sum(src, seg, n)
kernel_name = 'mk_gnn_ffn_d2_gnn_r8_ba3697'

def setup_inputs(seed: int=0):
    np.random.seed(seed)
    _w = jnp.asarray

    def _rec_inputs():
        import jax
        import jax.numpy as jnp
        _gk = jax.random.key(seed)
        x = -0.0002117 + 1 * jax.random.normal(jax.random.fold_in(_gk, 1), (1250, 512), jnp.float32)
        src = jax.random.randint(jax.random.fold_in(_gk, 2), (40000,), 0, 1250, jnp.int32)
        dst = jnp.minimum((1250 * jax.random.uniform(jax.random.fold_in(_gk, 3), (40000,)) ** 2.0).astype(jnp.int32), 9999)
        _o = jnp.argsort(dst, stable=True)
        src = src[_o]
        dst = dst[_o]
        edge_type_4 = jax.random.randint(jax.random.fold_in(_gk, 12), (40000,), 0, 4, jnp.int32)
        edge_type_8 = jax.random.randint(jax.random.fold_in(_gk, 13), (40000,), 0, 8, jnp.int32)
        edge_weight = jax.random.uniform(jax.random.fold_in(_gk, 14), (40000,), jnp.float32, 0.0, 0.999999)
        return (x, src, dst, edge_type_4, edge_type_8, edge_weight)
    x, src, dst, edge_type_4, edge_type_8, edge_weight = _rec_inputs()

    def _L0_gnn_setup():
        import jax, jax.numpy as jnp
        import numpy as np
        N, IN_DIM, H, D, E = (6250, 512, 8, 64, 100000)
        NEG_SLOPE = 0.2
        LN_EPS = 1e-05
        key = jax.random.key(seed)
        ks = jax.random.split(key, 8)
        x = jax.random.normal(ks[0], (N, IN_DIM), dtype=jnp.float32)
        edge_index = jax.random.randint(ks[1], (2, E), 0, N, dtype=jnp.int64)
        edge_type = jax.random.randint(ks[2], (E,), 0, 8, dtype=jnp.int64)
        edge_weight = jax.random.uniform(ks[3], (E,), dtype=jnp.float32)
        W = jax.random.normal(ks[4], (H * D, IN_DIM), dtype=jnp.float32) * (1.0 / np.sqrt(IN_DIM))
        a_src = jax.random.normal(ks[5], (H, D), dtype=jnp.float32) * (1.0 / np.sqrt(D))
        a_dst = jax.random.normal(ks[6], (H, D), dtype=jnp.float32) * (1.0 / np.sqrt(D))
        et_emb = jax.random.normal(ks[7], (8, H), dtype=jnp.float32)
        ln_gamma = jnp.ones((H * D,), dtype=jnp.float32)
        ln_beta = jnp.zeros((H * D,), dtype=jnp.float32)
        return {'x': x, 'edge_index': edge_index, 'edge_type': edge_type, 'edge_weight': edge_weight, 'W': W, 'a_src': a_src, 'a_dst': a_dst, 'et_emb': et_emb, 'ln_gamma': ln_gamma, 'ln_beta': ln_beta}
    _L0_gnn_all = _L0_gnn_setup()
    _L0_gnn_in = {k: v for k, v in _L0_gnn_all.items() if k in ('W', 'a_src', 'a_dst', 'et_emb', 'ln_gamma', 'ln_beta')}
    del _L0_gnn_all

    def _L0_ffn_setup():
        import jax, jax.numpy as jnp
        import numpy as np
        EPS = 1e-05
        TOP_K = 2

        def layer_norm(x, g, b):
            m = x.mean(-1, keepdims=True)
            v = ((x - m) ** 2).mean(-1, keepdims=True)
            return (x - m) / jnp.sqrt(v + EPS) * g + b
        key = jax.random.key(seed)
        ks = jax.random.split(key, 8)
        B, S, D, E, H = (8, 512, 512, 8, 256)
        x = jax.random.normal(ks[0], (B, S, D), dtype=jnp.float32)
        Wg = jax.random.normal(ks[1], (D, E), dtype=jnp.float32) * 0.02
        W1 = jax.random.normal(ks[2], (E, D, H), dtype=jnp.float32) * 0.02
        b1 = jnp.zeros((E, H), dtype=jnp.float32)
        W2 = jax.random.normal(ks[3], (E, H, D), dtype=jnp.float32) * 0.02
        b2 = jnp.zeros((E, D), dtype=jnp.float32)
        ln_g = jnp.ones((D,), dtype=jnp.float32)
        ln_b = jnp.zeros((D,), dtype=jnp.float32)
        out_g = jnp.ones((D,), dtype=jnp.float32)
        out_b = jnp.zeros((D,), dtype=jnp.float32)
        return {'x': x, 'Wg': Wg, 'W1': W1, 'b1': b1, 'W2': W2, 'b2': b2, 'ln_g': ln_g, 'ln_b': ln_b, 'out_g': out_g, 'out_b': out_b}
    _L0_ffn_all = _L0_ffn_setup()
    _L0_ffn_in = {k: v for k, v in _L0_ffn_all.items() if k in ('Wg', 'W1', 'b1', 'W2', 'b2', 'ln_g', 'ln_b', 'out_g', 'out_b')}
    del _L0_ffn_all

    def _L1_gnn_setup():
        import jax, jax.numpy as jnp
        import numpy as np
        N = 1250
        E = 20000
        DIM = 512
        R = 4
        EPS = 1e-05

        def layer_norm(h, w, b):
            mu = jnp.mean(h, axis=-1, keepdims=True)
            var = jnp.mean((h - mu) ** 2, axis=-1, keepdims=True)
            return (h - mu) * jax.lax.rsqrt(var + EPS) * w + b
        key = jax.random.key(seed)
        ks = jax.random.split(key, 12)
        s = 0.02
        inp = {'x': jax.random.normal(ks[0], (N, DIM), dtype=jnp.float32), 'edge_index': jax.random.randint(ks[1], (2, E), 0, N, dtype=jnp.int64), 'edge_type': jax.random.randint(ks[2], (E,), 0, R, dtype=jnp.int64), 'self_W': jax.random.normal(ks[3], (DIM, DIM), dtype=jnp.float32) * s, 'self_b': jnp.zeros((DIM,), dtype=jnp.float32), 'rel_W': jax.random.normal(ks[4], (R, DIM, DIM), dtype=jnp.float32) * s, 'rel_b': jnp.zeros((R, DIM), dtype=jnp.float32), 'ln1_w': jnp.ones((DIM,), dtype=jnp.float32), 'ln1_b': jnp.zeros((DIM,), dtype=jnp.float32), 'W1': jax.random.normal(ks[5], (DIM, 2 * DIM), dtype=jnp.float32) * s, 'b1': jnp.zeros((2 * DIM,), dtype=jnp.float32), 'W2': jax.random.normal(ks[6], (2 * DIM, DIM), dtype=jnp.float32) * s, 'b2': jnp.zeros((DIM,), dtype=jnp.float32), 'ln2_w': jnp.ones((DIM,), dtype=jnp.float32), 'ln2_b': jnp.zeros((DIM,), dtype=jnp.float32)}
        return inp
    _L1_gnn_all = _L1_gnn_setup()
    _L1_gnn_in = {k: v for k, v in _L1_gnn_all.items() if k in ('self_W', 'self_b', 'rel_W', 'rel_b', 'ln1_w', 'ln1_b', 'W1', 'b1', 'W2', 'b2', 'ln2_w', 'ln2_b')}
    del _L1_gnn_all

    def _L1_ffn_setup():
        import jax, jax.numpy as jnp
        import numpy as np
        MARK_AX, OP_ADD, OP_SUB = (0, 1, 2)
        ALU_LO, ALU_HI = (16, 32)
        AX_CARRY_LO, AX_CARRY_HI = (48, 64)
        OPCODE_BASE = 80
        OUTPUT_LO, OUTPUT_HI, CARRY = (128, 144, 160)
        NIB_A, NIB_B, OP_START = (0, 1, 10)
        RESULT, CARRY_OUT = (100, 101)
        GE_POS, GE_DIM = (8, 160)
        OPC_ADD, OPC_SUB = (25, 26)
        B, S, D = (8, 512, 512)

        def _decode_nibble(x, base):
            return jnp.argmax(x[..., base:base + 16] > 0.5, axis=-1).astype(x.dtype)

        def _pipeline(h, W, b):
            for i in range(3):
                h = jnp.einsum('bspd,od->bspo', h, W[i]) + b[i]
                if i < 2:
                    h = jax.nn.relu(h)
            return h
        key = jax.random.key(seed)
        kx, k1, k2, k3, k4 = jax.random.split(key, 5)
        x_bd = jax.random.uniform(kx, (B, S, D), dtype=jnp.float32)
        Wa = jax.random.normal(k1, (3, GE_DIM, GE_DIM), dtype=jnp.float32) * 0.05
        ba = jax.random.normal(k2, (3, GE_DIM), dtype=jnp.float32) * 0.05
        Ws = jax.random.normal(k3, (3, GE_DIM, GE_DIM), dtype=jnp.float32) * 0.05
        bs = jax.random.normal(k4, (3, GE_DIM), dtype=jnp.float32) * 0.05
        return {'x_bd': x_bd, 'Wa': Wa, 'ba': ba, 'Ws': Ws, 'bs': bs}
    _L1_ffn_all = _L1_ffn_setup()
    _L1_ffn_in = {k: v for k, v in _L1_ffn_all.items() if k in ('Wa', 'ba', 'Ws', 'bs')}
    del _L1_ffn_all
    return {'x': x, 'src': src, 'dst': dst, 'edge_type_4': edge_type_4, 'edge_type_8': edge_type_8, 'edge_weight': edge_weight, 'L0_gnn_W': _L0_gnn_in['W'], 'L0_gnn_a_src': _L0_gnn_in['a_src'], 'L0_gnn_a_dst': _L0_gnn_in['a_dst'], 'L0_gnn_et_emb': _L0_gnn_in['et_emb'], 'L0_gnn_ln_gamma': _L0_gnn_in['ln_gamma'], 'L0_gnn_ln_beta': _L0_gnn_in['ln_beta'], 'L0_ffn_Wg': _L0_ffn_in['Wg'], 'L0_ffn_W1': _L0_ffn_in['W1'], 'L0_ffn_b1': _L0_ffn_in['b1'], 'L0_ffn_W2': _L0_ffn_in['W2'], 'L0_ffn_b2': _L0_ffn_in['b2'], 'L0_ffn_ln_g': _L0_ffn_in['ln_g'], 'L0_ffn_ln_b': _L0_ffn_in['ln_b'], 'L0_ffn_out_g': _L0_ffn_in['out_g'], 'L0_ffn_out_b': _L0_ffn_in['out_b'], 'L1_gnn_self_W': _L1_gnn_in['self_W'], 'L1_gnn_self_b': _L1_gnn_in['self_b'], 'L1_gnn_rel_W': _L1_gnn_in['rel_W'], 'L1_gnn_rel_b': _L1_gnn_in['rel_b'], 'L1_gnn_ln1_w': _L1_gnn_in['ln1_w'], 'L1_gnn_ln1_b': _L1_gnn_in['ln1_b'], 'L1_gnn_W1': _L1_gnn_in['W1'], 'L1_gnn_b1': _L1_gnn_in['b1'], 'L1_gnn_W2': _L1_gnn_in['W2'], 'L1_gnn_b2': _L1_gnn_in['b2'], 'L1_gnn_ln2_w': _L1_gnn_in['ln2_w'], 'L1_gnn_ln2_b': _L1_gnn_in['ln2_b'], 'L1_ffn_Wa': _L1_ffn_in['Wa'], 'L1_ffn_ba': _L1_ffn_in['ba'], 'L1_ffn_Ws': _L1_ffn_in['Ws'], 'L1_ffn_bs': _L1_ffn_in['bs']}

def reference(x, src, dst, edge_type_4, edge_type_8, edge_weight, L0_gnn_W, L0_gnn_a_src, L0_gnn_a_dst, L0_gnn_et_emb, L0_gnn_ln_gamma, L0_gnn_ln_beta, L0_ffn_Wg, L0_ffn_W1, L0_ffn_b1, L0_ffn_W2, L0_ffn_b2, L0_ffn_ln_g, L0_ffn_ln_b, L0_ffn_out_g, L0_ffn_out_b, L1_gnn_self_W, L1_gnn_self_b, L1_gnn_rel_W, L1_gnn_rel_b, L1_gnn_ln1_w, L1_gnn_ln1_b, L1_gnn_W1, L1_gnn_b1, L1_gnn_W2, L1_gnn_b2, L1_gnn_ln2_w, L1_gnn_ln2_b, L1_ffn_Wa, L1_ffn_ba, L1_ffn_Ws, L1_ffn_bs):
    import jax
    import jax.numpy as jnp

    def _L0_gnn_ref(x, edge_index, edge_type, edge_weight, W, a_src, a_dst, et_emb, ln_gamma, ln_beta):
        import jax, jax.numpy as jnp
        import numpy as np
        N, IN_DIM, H, D, E = (6250, 512, 8, 64, 100000)
        NEG_SLOPE = 0.2
        LN_EPS = 1e-05
        n, h_, d_ = (x.shape[0], a_src.shape[0], a_src.shape[1])
        h = (x @ W.T).reshape(n, h_, d_)
        src, dst = (edge_index[0], edge_index[1])
        h_src = h[src]
        e_src = jnp.einsum('ehd,hd->eh', h_src, a_src)
        e_dst = jnp.einsum('ehd,hd->eh', h[dst], a_dst)
        e = jax.nn.leaky_relu(e_src + e_dst, NEG_SLOPE)
        e = e * (1.0 + et_emb[edge_type])
        e = e * edge_weight[:, None]
        e_max = jnp.zeros((n, h_), x.dtype).at[dst].max(e)
        e = jnp.exp(e - e_max[dst])
        e_sum = jnp.zeros((n, h_), x.dtype).at[dst].add(e)
        alpha = e / (e_sum[dst] + 1e-10)
        msg = h_src * alpha[:, :, None]
        out = jnp.zeros((n, h_, d_), x.dtype).at[dst].add(msg).reshape(n, h_ * d_)
        out = out + x
        mu = jnp.mean(out, axis=-1, keepdims=True)
        var = jnp.var(out, axis=-1, keepdims=True)
        return (out - mu) / jnp.sqrt(var + LN_EPS) * ln_gamma + ln_beta

    def _L0_ffn_ref(x, Wg, W1, b1, W2, b2, ln_g, ln_b, out_g, out_b):
        import jax, jax.numpy as jnp
        import numpy as np
        EPS = 1e-05
        TOP_K = 2

        def layer_norm(x, g, b):
            m = x.mean(-1, keepdims=True)
            v = ((x - m) ** 2).mean(-1, keepdims=True)
            return (x - m) / jnp.sqrt(v + EPS) * g + b
        xn = layer_norm(x, ln_g, ln_b)
        logits = jnp.einsum('bsd,de->bse', xn, Wg)
        probs = jax.nn.softmax(logits, axis=-1)
        top_p, top_i = jax.lax.top_k(probs, TOP_K)
        conf = top_p / top_p.sum(-1, keepdims=True)
        h = jax.nn.gelu(jnp.einsum('bsd,edh->bseh', xn, W1) + b1)
        o = jnp.einsum('bseh,ehd->bsed', h, W2) + b2
        sel = jnp.take_along_axis(o, top_i[..., None], axis=2)
        combined = jnp.einsum('bskd,bsk->bsd', sel, conf)
        return layer_norm(x + combined, out_g, out_b)

    def _L1_gnn_ref(x, edge_index, edge_type, self_W, self_b, rel_W, rel_b, ln1_w, ln1_b, W1, b1, W2, b2, ln2_w, ln2_b):
        import jax, jax.numpy as jnp
        import numpy as np
        N = 1250
        E = 20000
        DIM = 512
        R = 4
        EPS = 1e-05

        def layer_norm(h, w, b):
            mu = jnp.mean(h, axis=-1, keepdims=True)
            var = jnp.mean((h - mu) ** 2, axis=-1, keepdims=True)
            return (h - mu) * jax.lax.rsqrt(var + EPS) * w + b
        n = x.shape[0]
        src, dst = (edge_index[0], edge_index[1])
        h_all = jnp.einsum('nd,rdf->nrf', x, rel_W) + rel_b
        msg = h_all[src, edge_type]
        agg = jax.ops.segment_sum(msg, dst, num_segments=n)
        deg = jax.ops.segment_sum(jnp.ones_like(dst, dtype=x.dtype), dst, num_segments=n)
        agg = agg / jnp.maximum(deg, 1.0)[:, None]
        h = x @ self_W + self_b + agg
        x1 = layer_norm(x + h, ln1_w, ln1_b)
        f = jax.nn.gelu(x1 @ W1 + b1, approximate=False) @ W2 + b2
        out = layer_norm(x1 + f, ln2_w, ln2_b)
        return out

    def _L1_ffn_ref(x_bd, Wa, ba, Ws, bs):
        import jax, jax.numpy as jnp
        import numpy as np
        MARK_AX, OP_ADD, OP_SUB = (0, 1, 2)
        ALU_LO, ALU_HI = (16, 32)
        AX_CARRY_LO, AX_CARRY_HI = (48, 64)
        OPCODE_BASE = 80
        OUTPUT_LO, OUTPUT_HI, CARRY = (128, 144, 160)
        NIB_A, NIB_B, OP_START = (0, 1, 10)
        RESULT, CARRY_OUT = (100, 101)
        GE_POS, GE_DIM = (8, 160)
        OPC_ADD, OPC_SUB = (25, 26)
        B, S, D = (8, 512, 512)

        def _decode_nibble(x, base):
            return jnp.argmax(x[..., base:base + 16] > 0.5, axis=-1).astype(x.dtype)

        def _pipeline(h, W, b):
            for i in range(3):
                h = jnp.einsum('bspd,od->bspo', h, W[i]) + b[i]
                if i < 2:
                    h = jax.nn.relu(h)
            return h
        x = x_bd
        Bsz, seq, _ = x.shape
        x_ge = jnp.zeros((Bsz, seq, GE_POS, GE_DIM), dtype=x.dtype)
        x_ge = x_ge.at[..., 0, NIB_A].set(_decode_nibble(x, ALU_LO))
        x_ge = x_ge.at[..., 1, NIB_A].set(_decode_nibble(x, ALU_HI))
        x_ge = x_ge.at[..., 0, NIB_B].set(_decode_nibble(x, AX_CARRY_LO))
        x_ge = x_ge.at[..., 1, NIB_B].set(_decode_nibble(x, AX_CARRY_HI))
        x_ge = x_ge.at[..., :, OP_START + OPC_ADD].set(x[..., OPCODE_BASE + OPC_ADD][..., None])
        x_ge = x_ge.at[..., :, OP_START + OPC_SUB].set(x[..., OPCODE_BASE + OPC_SUB][..., None])
        mark = x[..., MARK_AX] > 0.5
        m_add = mark & (x[..., OP_ADD] > 0.5)
        m_sub = mark & ~(x[..., OP_ADD] > 0.5) & (x[..., OP_SUB] > 0.5)
        active = (m_add | m_sub).astype(x.dtype)
        y_add = _pipeline(x_ge, Wa, ba)
        y_sub = _pipeline(x_ge, Ws, bs)
        y = jnp.where(m_add[..., None, None], y_add, jnp.where(m_sub[..., None, None], y_sub, x_ge))
        res_lo = jnp.clip(jnp.round(y[..., 0, RESULT]), 0, 15).astype(jnp.int32)
        res_hi = jnp.clip(jnp.round(y[..., 1, RESULT]), 0, 15).astype(jnp.int32)
        oh_lo = jax.nn.one_hot(res_lo, 16, dtype=x.dtype) * active[..., None]
        oh_hi = jax.nn.one_hot(res_hi, 16, dtype=x.dtype) * active[..., None]
        carry = (jnp.round(y[..., 1, CARRY_OUT]) > 0.5).astype(x.dtype) * active
        out = x
        out = out.at[..., OUTPUT_LO:OUTPUT_LO + 16].add(2.0 * oh_lo)
        out = out.at[..., OUTPUT_HI:OUTPUT_HI + 16].add(2.0 * oh_hi)
        out = out.at[..., CARRY].add(carry)
        return out
    edge_index = jnp.stack([src, dst])
    x = x + _L0_gnn_ref(_layernorm(x, axis=-1), edge_index, edge_type_8, edge_weight, L0_gnn_W, L0_gnn_a_src, L0_gnn_a_dst, L0_gnn_et_emb, L0_gnn_ln_gamma, L0_gnn_ln_beta)
    x = x + _L0_ffn_ref(_layernorm(x, axis=-1)[None], L0_ffn_Wg, L0_ffn_W1, L0_ffn_b1, L0_ffn_W2, L0_ffn_b2, L0_ffn_ln_g, L0_ffn_ln_b, L0_ffn_out_g, L0_ffn_out_b)[0]
    x = x + _L1_gnn_ref(_layernorm(x, axis=-1), edge_index, edge_type_4, L1_gnn_self_W, L1_gnn_self_b, L1_gnn_rel_W, L1_gnn_rel_b, L1_gnn_ln1_w, L1_gnn_ln1_b, L1_gnn_W1, L1_gnn_b1, L1_gnn_W2, L1_gnn_b2, L1_gnn_ln2_w, L1_gnn_ln2_b)
    x = x + _L1_ffn_ref(_layernorm(x, axis=-1)[None], L1_ffn_Wa, L1_ffn_ba, L1_ffn_Ws, L1_ffn_bs)[0]
    return x

_drawn_inputs = setup_inputs


def setup_inputs(seed=0):
    import zlib

    import numpy as np

    out = dict(_drawn_inputs(seed))
    spreads = {'L0_gnn_ln_gamma': (1.0, 0.2),
     'L0_gnn_ln_beta': (0.0, 0.1),
     'L0_ffn_b1': (0.0, 0.8),
     'L0_ffn_b2': (0.0, 0.32),
     'L0_ffn_ln_g': (1.0, 0.6),
     'L0_ffn_ln_b': (0.0, 0.746),
     'L0_ffn_out_g': (1.0, 0.2),
     'L0_ffn_out_b': (0.0, 0.1),
     'L1_gnn_self_b': (0.0, 0.339),
     'L1_gnn_rel_b': (0.0, 0.616),
     'L1_gnn_ln1_w': (1.0, 0.2),
     'L1_gnn_ln1_b': (0.0, 0.312),
     'L1_gnn_b1': (0.0, 0.8),
     'L1_gnn_b2': (0.0, 0.307),
     'L1_gnn_ln2_w': (1.0, 0.2),
     'L1_gnn_ln2_b': (0.0, 0.313)}
    factors = {'L0_ffn_W1': 2.733, 'L1_gnn_rel_W': 2.826}
    for name, (base, spread) in spreads.items():
        noise = np.random.default_rng([zlib.crc32(name.encode()), seed]).standard_normal(out[name].shape)
        drawn = base * np.exp(spread * noise) if base else spread * noise
        out[name] = jnp.asarray(drawn.astype(out[name].dtype))
    for name, factor in factors.items():
        out[name] = (out[name] * factor).astype(out[name].dtype)
    return out
```

```python
from contextlib import ExitStack

import concourse.bass as bass
import numpy as np
from concourse import mybir

ALU = mybir.AluOpType
ACT = mybir.ActivationFunctionType
AX = mybir.AxisListType
F32, F16, BF16 = mybir.dt.float32, mybir.dt.float16, mybir.dt.bfloat16
I32, U32 = mybir.dt.int32, mybir.dt.uint32

P = 128
N = 1250
D = 512
E = 40000
NT = -(-N // P)
NP = NT * P
LAST = N - (NT - 1) * P
KD = D // P
H, HD = 8, 64
NREL = 4
NTYPE = 8
NEXP, HID = 8, 256
FF = 1024
GT = 2
NG = NT // GT
W2N = GT * P

C = -(-E // P)
EP = C * P
CG = 16
NCG = -(-C // CG)
CP = NCG * CG
TAIL = E - (P - 1) * C
CHUNK = 512
CJ = CHUNK // P
STEPS = (EP + NT * (CHUNK - 1)) // CHUNK
RING = 4
R0 = 2 + H + 1
R1 = 2
PARTS = 3
EPS = 1e-5
NEG_SLOPE = 0.2
PAD_DST = NP - 1
ROUND = 12582912.0
GE = 160
ONE = 1
WBYTES = 64 * 1024

ROW_NAMES = ["L0_gnn_ln_gamma", "L0_gnn_ln_beta", "L0_ffn_ln_g", "L0_ffn_ln_b", "L0_ffn_out_g",
             "L0_ffn_out_b", "L1_gnn_self_b", "L1_gnn_ln1_w", "L1_gnn_ln1_b", "L1_gnn_b2",
             "L1_gnn_ln2_w", "L1_gnn_ln2_b"]


class Shared:
    pass


def tile(ap, i):
    return ap[:, bass.ds(i, 1), :].rearrange("p a d -> p (a d)")


def over_heads(ap):
    return ap.unsqueeze(2).to_broadcast((P, H, HD))


def build(nc, t):
    with ExitStack() as ctx:
        m = Shared()
        m.t = t

        def sb(name, shape, dt=F32):
            return ctx.enter_context(nc.sbuf_tensor(name, shape, dt))

        def sem(name):
            return ctx.enter_context(nc.semaphore(name))

        def dram(name, shape, dt=F32):
            return nc.dram_tensor(name, shape, dt, kind="Internal").ap()

        m.sb, m.sem = sb, sem
        m.h_rows = dram("h_rows", [NP, D])
        m.rel_rows = dram("rel_rows", [NP * NREL, D])
        m.rec0 = dram("rec0", [EP + CHUNK, R0])
        m.rec1 = dram("rec1", [EP + CHUNK, R1])
        m.src_cp = dram("src_cp", [CP, P], F16)
        m.dst_cp = dram("dst_cp", [CP, P], F16)

        m.X = sb("X", [P, NT, D])
        m.ACC = sb("ACC", [P, NT, D])
        m.ASUM = sb("ASUM", [P, NT, H + 1])
        m.RES = sb("RES", [P, NT, D])
        m.XS = sb("XS", [P, GT, D])
        m.XT = sb("XT", [P, KD, W2N])
        m.U = sb("U", [P, GT, D])
        m.ident = sb("ident", [P, P])
        m.iota_f = sb("iota_f", [P, P])
        m.iota_k = sb("iota_k", [P, NT])
        m.ones = sb("ones", [P, P])
        m.eps = sb("eps", [P, 1])
        m.ROWS = sb("ROWS", [P, len(ROW_NAMES), D])
        m.rows = {name: m.ROWS[:, n, :] for n, name in enumerate(ROW_NAMES)}
        m.stats = sb("stats", [P, NT, 6])
        m.mv = sb("mv", [P, NT, 2])
        m.sd = sb("sd", [P, NT])
        m.rstd = sb("rstd", [P, NT])
        m.TAB = sb("TAB", [P, 2, NT, PARTS, H], BF16)
        m.woff = sb("woff", [P, STEPS])
        m.step_off = sb("step_off", [P, STEPS], I32)
        m.step_win = sb("step_win", [P, STEPS], I32)
        m.arena_words = 26 * 1024 + 512
        m.arena = sb("arena", [P, m.arena_words])
        m.PS = [ctx.enter_context(nc.psum_tensor(f"PS{i}", [P, 512], F32)) for i in range(8)]

        node_scores(nc, m)
        edge_weights(nc, m)
        messages(nc, m, "m0", m.rec0, R0, m.h_rows, True, load_experts)
        experts(nc, m)
        relations(nc, m)
        messages(nc, m, "m1", m.rec1, R1, m.rel_rows, False, load_ffn)
        ffn(nc, m)
        nibbles(nc, m)


def carver(m, start=0):
    at = [start]

    def take(words):
        at[0] += words
        assert at[0] <= m.arena_words, at
        return m.arena[:, at[0] - words:at[0]]
    return take


def node_scores(nc, m):
    t, PS, sem = m.t, m.PS, m.sem
    take = carver(m)
    WT = take(KD * D).rearrange("p (k d) -> p k d", k=KD)
    WR = take(KD * D).rearrange("p (k d) -> p k d", k=KD)
    WA = take(KD * 2 * H).rearrange("p (k d) -> p k d", k=KD)
    AB = take(KD * 2 * H).rearrange("p (k d) -> p k d", k=KD)
    STG = take(GT * D).rearrange("p (j d) -> p j d", j=GT)
    SV = take(NT * 2 * H).rearrange("p (t s) -> p t s", t=NT)
    SR = take(NT * 2 * H).rearrange("p (t s) -> p t s", t=NT)

    x_ld, w_ld, a_ld, row_ld, x_zero, ab_zero, consts, wa_ps, wa_sb = (sem("s1_" + n) for n in (
        "x_ld", "w_ld", "a_ld", "row_ld", "x_zero", "ab_zero", "consts", "wa_ps", "wa_sb"))
    mv_ready, sd_ready, xs_ready, xt_ps, xt_sb, res_sb, h_ps, h_sb, h_dr = (sem("s1_" + n) for n in (
        "mv_ready", "sd_ready", "xs_ready", "xt_ps", "xt_sb", "res_sb", "h_ps", "h_sb", "h_dr"))

    with nc.Block() as block:
        @block.sync
        def _(sp):
            sp.sem_inc(h_dr, ONE)
            sp.wait_ge(x_zero, 1)
            sp.dma_start(m.X[:, 0:NT - 1, :], t["x"][0:(NT - 1) * P, :].rearrange("(t p) d -> p t d", p=P)).then_inc(x_ld, 16)
            sp.dma_start(m.X[0:LAST, NT - 1, :], t["x"][(NT - 1) * P:N, :]).then_inc(x_ld, 16)
            sp.dma_start(WR, t["L0_gnn_W"].rearrange("(k p) d -> p k d", p=P)).then_inc(w_ld, 16)
            sp.dma_start(WT, t["L0_gnn_WT"].rearrange("(k p) d -> p k d", p=P)).then_inc(w_ld, 16)
            for name in ROW_NAMES:
                sp.dma_start(m.rows[name], t[name].partition_broadcast(P)).then_inc(row_ld, 16)
            with sp.Fori(0, NG) as g:
                sp.wait_ge(h_sb, ONE + g * GT + GT)
                sp.dma_start(m.h_rows[bass.ds(g * W2N, W2N), :].rearrange("(j p) d -> p j d", p=P), STG).then_inc(h_dr, 16)
            sp.wait_ge(h_dr, ONE + 16 * NG)
            sp.wait_ge(row_ld, 16 * len(ROW_NAMES))

        @block.gpsimd
        def _(pool):
            pool.memset(m.X[:, NT - 1, :], 0.0).then_inc(x_zero, 1)
            pool.memset(AB, 0.0).then_inc(ab_zero, 1)
            pool.memset(m.eps[:, :], EPS)
            pool.memset(m.ones[:, :], 1.0)
            pool.memset(m.ident[:, :], 0.0)
            pool.iota(m.iota_f[:, :], [[1, P]], base=0, channel_multiplier=0, allow_small_or_imprecise_dtypes=True)
            pool.iota(m.iota_k[:, :], [[P, NT]], base=0, channel_multiplier=1, allow_small_or_imprecise_dtypes=True)
            pool.drain()
            pool.affine_select(out=m.ident[:, :], in_=m.ident[:, :], compare_op=ALU.not_equal, fill=1.0, base=0,
                               pattern=[[-1, P]], channel_multiplier=1).then_inc(consts, 1)
            pool.wait_ge(ab_zero, 1)
            for h in range(H):
                lo = (h * HD) % P
                for s, name in enumerate(("L0_gnn_a_src", "L0_gnn_a_dst")):
                    pool.dma_start(AB[lo:lo + HD, h * HD // P, s * H + h:s * H + h + 1],
                                   t[name][h:h + 1, :].rearrange("a d -> d a")).then_inc(a_ld, 16)
            pool.wait_ge(a_ld, 16 * 2 * H)

        @block.vector
        def _(dve):
            dve.sem_inc(h_sb, ONE)
            dve.memset(m.ACC[:, :, :], 0.0)
            dve.memset(m.ASUM[:, :, :], 0.0)
            dve.wait_ge(x_ld, 32)
            for i in range(NT):
                dve.bn_stats(m.stats[:, i, :], m.X[:, i, :])
            dve.drain()
            for i in range(NT):
                dve.bn_aggr(m.mv[:, i, :], m.stats[:, i, :])
            dve.drain().then_inc(mv_ready, 1)
            dve.wait_ge(wa_ps, 1)
            dve.tensor_copy(WA, PS[7][:, 0:KD * 2 * H].rearrange("p (k d) -> p k d", k=KD)).then_inc(wa_sb, 1)
            dve.wait_ge(sd_ready, 1)
            dve.reciprocal(m.rstd[:, :], m.sd[:, :])
            dve.drain()
            with dve.Fori(0, NG) as g:
                dve.wait_ge(xt_ps, ONE + g * GT)
                dve.wait_ge(res_sb, ONE + g * GT)
                for j in range(GT):
                    dve.tensor_scalar(m.XS[:, j, :], tile(m.X, g * GT + j), tile(m.mv, g * GT + j)[:, 0:1],
                                      m.rstd[:, bass.ds(g * GT + j, 1)], ALU.subtract, ALU.mult).then_inc(xs_ready, 1)
                dve.wait_ge(h_dr, ONE + g * 16)
                for j in range(GT):
                    dve.wait_ge(h_ps, ONE + g * GT + j + 1)
                    dve.tensor_copy(STG[:, j, :], PS[4 + j][:, :])
                    dve.tensor_copy(tile(SV, g * GT + j), PS[2 + j][:, 0:2 * H])
                    dve.drain().then_inc(h_sb, 1)
            for s in range(2):
                left = SV[:, :, s * H:(s + 1) * H]
                for part in range(PARTS):
                    dve.tensor_copy(m.TAB[:, s, :, part, :], left)
                    dve.drain()
                    if part < PARTS - 1:
                        rest = SR[:, :, part * H:(part + 1) * H]
                        dve.tensor_tensor(rest, left, m.TAB[:, s, :, part, :], ALU.subtract)
                        dve.drain()
                        left = rest

        @block.scalar
        def _(act):
            act.sem_inc(res_sb, ONE)
            act.sem_inc(xt_sb, ONE)
            act.wait_ge(consts, 1)
            act.wait_ge(mv_ready, 1)
            act.activation(m.sd[:, :], m.mv[:, :, 1], ACT.Sqrt, bias=m.eps[:, 0:1]).then_inc(sd_ready, 1)
            with act.Fori(0, NG) as g:
                for j in range(GT):
                    act.wait_ge(xs_ready, g * GT + j + 1)
                    act.copy(tile(m.RES, g * GT + j), m.XS[:, j, :]).then_inc(res_sb, 1)
                act.wait_ge(h_ps, ONE + g * GT)
                for j in range(GT):
                    act.wait_ge(xt_ps, ONE + g * GT + j + 1)
                    act.copy(m.XT[:, :, j * P:(j + 1) * P], PS[j][:, :].rearrange("p (k n) -> p k n", k=KD)).then_inc(xt_sb, 1)

        @block.tensor
        def _(pe):
            pe.sem_inc(xt_ps, ONE)
            pe.sem_inc(h_ps, ONE)
            pe.wait_ge(consts, 1)
            pe.wait_ge(w_ld, 32)
            pe.wait_ge(a_ld, 16 * 2 * H)
            for k in range(KD):
                for b in range(KD):
                    ins = pe.matmul(PS[7][:, k * 2 * H:(k + 1) * 2 * H], WR[:, b, k * P:(k + 1) * P], AB[:, b, :],
                                    start=(b == 0), stop=(b == KD - 1))
            ins.then_inc(wa_ps, 1)
            pe.wait_ge(wa_sb, 1)
            with pe.Fori(0, NG) as g:
                pe.wait_ge(xt_sb, ONE + g * GT)
                for j in range(GT):
                    pe.wait_ge(xs_ready, g * GT + j + 1)
                    for k in range(KD):
                        ins = pe.transpose(PS[j][:, k * P:(k + 1) * P], m.XS[:, j, k * P:(k + 1) * P], m.ident[:, :])
                    ins.then_inc(xt_ps, 1)
                pe.wait_ge(h_sb, ONE + g * GT)
                for j in range(GT):
                    pe.wait_ge(xt_sb, ONE + g * GT + j + 1)
                    for k in range(KD):
                        pe.matmul(PS[2 + j][:, 0:2 * H], m.XT[:, k, j * P:(j + 1) * P], WA[:, k, :],
                                  start=(k == 0), stop=(k == KD - 1))
                    for k in range(KD):
                        ins = pe.matmul(PS[4 + j][:, :], m.XT[:, k, j * P:(j + 1) * P], WT[:, k, :],
                                        start=(k == 0), stop=(k == KD - 1))
                    ins.then_inc(h_ps, 1)


def edge_weights(nc, m):
    t, PS, sem = m.t, m.PS, m.sem
    NOT = 2 * NT
    OTS = 4
    take = carver(m)
    BC = take(2 * 2 * CG * P // 2).bitcast(F16).rearrange("p (r s e) -> p r s e", r=2, s=2)
    OT = take(OTS * CG * P // 2).bitcast(BF16).rearrange("p (r e) -> p r e", r=OTS)
    SC = take(H * CP).rearrange("p (h c) -> p h c", h=H)
    MUL = take(H * CP).rearrange("p (h c) -> p h c", h=H)
    FW = take(H * CP).rearrange("p (h c) -> p h c", h=H)
    EDG = take(10 * CP).rearrange("p (n c) -> p n c", n=10)
    src_i, dst_i, t4_i, t8_i = (EDG[:, n, :].bitcast(I32) for n in range(4))
    ew, src_f, dst_f, t8_f, mask, same = (EDG[:, n, :] for n in range(4, 10))
    REC0 = take(C * R0).rearrange("p (c r) -> p c r", r=R0)
    REC1 = take(C * R1).rearrange("p (c r) -> p c r", r=R1)
    emb = take(NTYPE * H)
    cp16 = take(2 * 3 * P // 2).bitcast(F16).rearrange("p (s b e) -> p s b e", s=2, b=3)
    cnt, tot, sst = take(NT + 1), take(NT + 1), take(NT + 1)
    nst, nst_i, adj, dadj = take(NT), take(NT).bitcast(I32), take(NT), take(NT)
    iota_s, stmp, off_f = take(STEPS), take(STEPS), take(STEPS)
    lv_in = take(4 * H).rearrange("p (n h) -> p n h", n=4)
    lv = take(4 * 2 * P).rearrange("p (n e s) -> p n e s", n=4, e=P)
    lv_same = take(2 * P + 1)[0:H, :]
    g_first, g_last = take(H), take(H)
    tail = take(CJ * R0).rearrange("p (c r) -> p c r", r=R0)

    init, tails, e_ld, e_ready, cp_ps, cp_sb, cp_dr, tot_ps = (sem("s2_" + n) for n in (
        "init", "tails", "e_ld", "e_ready", "cp_ps", "cp_sb", "cp_dr", "tot_ps"))
    bc_ld = [sem(f"s2_bc_ld{i}") for i in range(2)]
    bc_free, ot_ready, ot_free, sc_free = (sem("s2_" + n) for n in ("bc_free", "ot_ready", "ot_free", "sc_free"))
    lv_ready, lv_ps, lv_done, gb_ps, diff, rec_ready, rec_dr = (sem("s2_" + n) for n in (
        "lv_ready", "lv_ps", "lv_done", "gb_ps", "diff", "rec_ready", "rec_dr"))

    with nc.Block() as block:
        @block.sync
        def _(sp):
            sp.wait_ge(init, 1)
            full = (P - 1) * C
            for dst, name in ((src_i, "src"), (dst_i, "dst"), (t4_i, "edge_type_4"), (t8_i, "edge_type_8"), (ew, "edge_weight")):
                sp.dma_start(dst[0:P - 1, 0:C], t[name][0:full].rearrange("(p c) -> p c", c=C)).then_inc(e_ld, 16)
                sp.dma_start(dst[P - 1:P, 0:TAIL], t[name][full:E].unsqueeze(0)).then_inc(e_ld, 16)
            sp.dma_start(emb, t["L0_gnn_et_emb"].rearrange("t h -> (t h)").partition_broadcast(P)).then_inc(e_ld, 16)
            sp.wait_ge(cp_sb, 2)
            for s, cp in enumerate((m.src_cp, m.dst_cp)):
                sp.dma_start(cp[0:2 * P, :].rearrange("(b c) p -> c b p", c=P), cp16[:, s, 0:2, :]).then_inc(cp_dr, 16)
                sp.dma_start(cp[2 * P:CP, :], cp16[0:CP - 2 * P, s, 2, :]).then_inc(cp_dr, 16)
            sp.wait_ge(cp_dr, 64)
            with sp.Fori(0, NCG // 2) as i:
                for r in range(2):
                    sp.wait_ge(bc_free, i * 2 + r + 1)
                    for s, cp in enumerate((m.src_cp, m.dst_cp)):
                        sp.dma_start(BC[:, r, s, :], cp[bass.ds((i * 2 + r) * CG, CG), :].rearrange("c p -> (c p)").partition_broadcast(P)).then_inc(bc_ld[r], 16)
            sp.wait_ge(rec_ready, 1)
            sp.dma_start(m.rec0[0:EP, :].rearrange("(p c) r -> p (c r)", c=C), REC0.rearrange("p c r -> p (c r)")).then_inc(rec_dr, 16)
            sp.dma_start(m.rec1[0:EP, :].rearrange("(p c) r -> p (c r)", c=C), REC1.rearrange("p c r -> p (c r)")).then_inc(rec_dr, 16)
            sp.wait_ge(tails, 1)
            sp.dma_start(m.rec0[EP:EP + CHUNK, :].rearrange("(p c) r -> p c r", c=CJ), tail).then_inc(rec_dr, 16)
            sp.dma_start(m.rec1[EP:EP + CHUNK, :].rearrange("(p c) r -> p c r", c=CJ), tail[:, :, 0:R1]).then_inc(rec_dr, 16)
            sp.wait_ge(rec_dr, 64)

        @block.gpsimd
        def _(pool):
            pool.memset(EDG, 0.0)
            pool.drain()
            pool.memset(dst_i, PAD_DST)
            pool.drain().then_inc(init, 1)
            pool.memset(tail, 0.0)
            pool.memset(cp16, 0.0)
            pool.iota(iota_s, [[1, STEPS]], base=0, channel_multiplier=0, allow_small_or_imprecise_dtypes=True)
            pool.drain()
            pool.memset(tail[:, :, 1:2], -1.0).then_inc(tails, 1)

        @block.vector
        def _(dve):
            dve.sem_inc(bc_free, 2)
            dve.sem_inc(sc_free, 2)
            dve.wait_ge(e_ld, 176)
            dve.wait_ge(tails, 1)
            dve.tensor_copy(src_f, src_i)
            dve.tensor_copy(dst_f, dst_i)
            dve.tensor_copy(t8_f, t8_i)
            dve.memset(MUL, 0.0)
            dve.memset(cnt[:, 0:1], 0.0)
            dve.tensor_scalar(emb, emb, 1.0, None, ALU.add)
            dve.drain()
            for w in range(1, NT + 1):
                dve.tensor_scalar(mask[:, 0:C], dst_f[:, 0:C], float(P * w), 0.0, ALU.is_lt, ALU.add, accum_out=cnt[:, w:w + 1])
                dve.drain()
            dve.drain().then_inc(e_ready, 1)
            dve.scalar_tensor_tensor(REC1[:, :, 0].bitcast(I32), src_f[:, 0:C], float(NREL), t4_i[:, 0:C], ALU.mult, ALU.add)
            dve.tensor_copy(REC1[:, :, 1], dst_f[:, 0:C])
            dve.tensor_copy(REC0[:, :, 0].bitcast(I32), src_i[:, 0:C])
            dve.tensor_copy(REC0[:, :, 1], dst_f[:, 0:C])
            dve.memset(REC0[:, :, R0 - 1], 1.0)
            dve.memset(same[:, 0:1], 1.0)
            dve.tensor_tensor(same[:, 1:C], dst_f[:, 1:C], dst_f[:, 0:C - 1], ALU.is_equal)
            dve.memset(same[:, C:C + 1], 1.0)
            for s in range(2):
                dve.wait_ge(cp_ps, s + 1)
                dve.tensor_copy(cp16[:, s, 0:2, :], PS[s][:, 0:2 * P].rearrange("p (b c) -> p b c", b=2))
                dve.tensor_copy(cp16[0:C - 2 * P, s, 2, :], PS[s][0:C - 2 * P, 2 * P:3 * P])
                dve.drain().then_inc(cp_sb, 1)
            for ty in range(NTYPE):
                dve.tensor_scalar(mask, t8_f, float(ty), None, ALU.is_equal)
                dve.drain()
                for h in range(H):
                    dve.scalar_tensor_tensor(MUL[:, h, :], mask, emb[:, ty * H + h:ty * H + h + 1], MUL[:, h, :], ALU.mult, ALU.add)
                dve.drain()
            for h in range(H):
                dve.tensor_tensor(MUL[:, h, :], MUL[:, h, :], ew, ALU.mult)
            dve.wait_ge(tot_ps, 1)
            dve.tensor_copy(tot, PS[2][:, 0:NT + 1])
            dve.drain()
            dve.tensor_tensor(nst, tot[:, 1:NT + 1], tot[:, 0:NT], ALU.subtract)
            dve.drain()
            dve.tensor_scalar(nst_i, nst, float(CHUNK - 1), None, ALU.add)
            dve.drain()
            dve.tensor_scalar(nst_i, nst_i, CHUNK.bit_length() - 1, None, ALU.arith_shift_right)
            dve.drain()
            dve.tensor_copy(nst, nst_i)
            dve.memset(sst, 0.0)
            dve.drain()
            for w in range(NT):
                dve.tensor_tensor(sst[:, w + 1:w + 2], sst[:, w:w + 1], nst[:, w:w + 1], ALU.add)
                dve.drain()
            dve.scalar_tensor_tensor(adj, sst[:, 0:NT], -float(CHUNK), tot[:, 0:NT], ALU.mult, ALU.add)
            dve.drain()
            dve.tensor_tensor(dadj[:, 1:NT], adj[:, 1:NT], adj[:, 0:NT - 1], ALU.subtract)
            dve.tensor_scalar(off_f, iota_s, float(CHUNK), None, ALU.mult)
            dve.memset(m.woff[:, :], 0.0)
            dve.drain()
            for w in range(1, NT):
                dve.tensor_scalar(stmp, iota_s, sst[:, w:w + 1], None, ALU.is_ge)
                dve.drain()
                dve.scalar_tensor_tensor(off_f, stmp, dadj[:, w:w + 1], off_f, ALU.mult, ALU.add)
                dve.tensor_tensor(m.woff[:, :], m.woff[:, :], stmp, ALU.add)
                dve.drain()
            dve.tensor_scalar(m.step_off[:, :], off_f, float(EP), None, ALU.min)
            dve.tensor_copy(m.step_win[:, :], m.woff[:, :])
            dve.drain()
            dve.tensor_scalar(m.woff[:, :], m.woff[:, :], float(P), None, ALU.mult)
            with dve.Fori(0, NCG // 2) as i:
                for r in range(2):
                    dve.wait_ge(bc_ld[r], i * 32 + 32)
                    for s in range(2):
                        for k in range(NT):
                            n = s * NT + k
                            dve.wait_ge(ot_free, (i * 2 + r) * NOT + n + 1)
                            dve.tensor_scalar(OT[:, n % OTS, :], BC[:, r, s, :], m.iota_k[:, k:k + 1], None, ALU.is_equal).then_inc(ot_ready, 1)
                    dve.drain().then_inc(bc_free, 1)
                    dve.wait_ge(ot_free, OTS + (i * 2 + r + 1) * NOT)
                    dve.tensor_reduce(SC[:, :, bass.ds((i * 2 + r) * CG, CG)].rearrange("p h c -> p c h"),
                                      PS[4 + r][:, 0:CG * PARTS * H].rearrange("p (c b h) -> p c h b", c=CG, b=PARTS),
                                      AX.X, ALU.add).then_inc(sc_free, 1)
            dve.drain()
            dve.scalar_tensor_tensor(SC, SC, NEG_SLOPE, SC, ALU.mult, ALU.max)
            dve.drain()
            dve.tensor_tensor(SC, SC, MUL, ALU.mult)
            dve.drain()

            def segment_max(first, last):
                for h in range(H):
                    dve.tensor_tensor_scan(FW[:, h, 0:C], same[:, 0:C], SC[:, h, 0:C], first(h), ALU.mult, ALU.max)
                dve.drain()
                for h in range(H):
                    dve.tensor_tensor_scan(MUL[:, h, 0:C][:, ::-1], same[:, 1:C + 1][:, ::-1], FW[:, h, 0:C][:, ::-1],
                                           last(h), ALU.mult, ALU.max)
                dve.drain()

            segment_max(lambda h: 0.0, lambda h: 0.0)
            dve.tensor_copy(lv_in[:, 0, :], MUL[:, :, 0])
            dve.tensor_copy(lv_in[:, 1, :], FW[:, :, C - 1])
            dve.tensor_copy(lv_in[:, 2, :], dst_f[:, 0:1].to_broadcast((P, H)))
            dve.tensor_copy(lv_in[:, 3, :], dst_f[:, C - 1:C].to_broadcast((P, H)))
            dve.memset(lv_same, 0.0)
            dve.drain().then_inc(lv_ready, 1)
            dve.wait_ge(lv_ps, 1)
            for n in range(4):
                dve.tensor_copy(lv[0:H, n // 2, :, n % 2], PS[3][0:H, n * P:(n + 1) * P])
            dve.drain()
            val, key, fwd, bwd = (lv[0:H, n, :, :].rearrange("h e s -> h (e s)") for n in range(4))
            dve.tensor_tensor(lv_same[:, 1:2 * P], key[:, 1:2 * P], key[:, 0:2 * P - 1], ALU.is_equal)
            dve.drain()
            dve.tensor_tensor_scan(fwd, lv_same[:, 0:2 * P], val, 0.0, ALU.mult, ALU.max)
            dve.drain()
            dve.tensor_tensor_scan(bwd[:, ::-1], lv_same[:, 1:2 * P + 1][:, ::-1], fwd[:, ::-1], 0.0, ALU.mult, ALU.max).then_inc(lv_done, 1)
            dve.wait_ge(gb_ps, 1)
            dve.tensor_copy(g_first, PS[2][:, 0:H])
            dve.tensor_copy(g_last, PS[2][:, H:2 * H])
            dve.drain()
            segment_max(lambda h: g_first[:, h:h + 1], lambda h: g_last[:, h:h + 1])
            dve.tensor_tensor(FW, SC, MUL, ALU.subtract)
            dve.drain().then_inc(diff, 1)

        @block.scalar
        def _(act):
            act.wait_ge(diff, 1)
            act.activation(REC0[:, :, 2:2 + H].rearrange("p c h -> p h c"), FW[:, :, 0:C], ACT.Exp).then_inc(rec_ready, 1)

        @block.tensor
        def _(pe):
            pe.sem_inc(ot_free, OTS)
            pe.wait_ge(e_ready, 1)
            for s, v in enumerate((src_f, dst_f)):
                for b in range(3):
                    n = min(P, C - b * P)
                    ins = pe.transpose(PS[s][0:n, b * P:(b + 1) * P], v[:, b * P:b * P + n], m.ident[:, :])
                ins.then_inc(cp_ps, 1)
            pe.matmul(PS[2][:, 0:NT + 1], m.ones[:, :], cnt, start=True, stop=True).then_inc(tot_ps, 1)
            with pe.Fori(0, NCG // 2) as i:
                for r in range(2):
                    pe.wait_ge(sc_free, i * 2 + r + 1)
                    for n in range(NOT):
                        pe.wait_ge(ot_ready, (i * 2 + r) * NOT + n + 1)
                        for c in range(CG):
                            ins = pe.matmul(PS[4 + r][:, c * PARTS * H:(c + 1) * PARTS * H], OT[:, n % OTS, c * P:(c + 1) * P],
                                            m.TAB[:, n // NT, n % NT, :, :].rearrange("p b h -> p (b h)"),
                                            start=(n == 0 and c == 0), stop=(n == NOT - 1), skip_group_check=True)
                        ins.then_inc(ot_free, 1)
            pe.wait_ge(lv_ready, 1)
            for n in range(4):
                ins = pe.transpose(PS[3][0:H, n * P:(n + 1) * P], lv_in[:, n, :], m.ident[:, :])
            ins.then_inc(lv_ps, 1)
            pe.wait_ge(lv_done, 1)
            for n in range(2):
                ins = pe.transpose(PS[2][:, n * H:(n + 1) * H], lv[0:H, 3, :, n], m.ident[0:H, 0:H])
            ins.then_inc(gb_ps, 1)


def messages(nc, m, tag, rec, R, table, weighted, load_next):
    PS, sem = m.PS, m.sem
    take = carver(m, WBYTES // 4)
    G = take(RING * CJ * D).rearrange("p (r j d) -> p r j d", r=RING, j=CJ)
    OH = take(2 * CJ * P).rearrange("p (r j d) -> p r j d", r=2, j=CJ)
    RC = take(RING * CJ * R).rearrange("p (r j c) -> p r j c", r=RING, j=CJ)
    DR = take(2 * CJ).rearrange("p (r j) -> p r j", r=2)
    rec_ld = [sem(f"{tag}_rec_ld{i}") for i in range(RING)]
    g_ld = [sem(f"{tag}_g_ld{i}") for i in range(RING)]
    msg_ready, slot_free, oh_ready, ps_free = (sem(f"{tag}_{n}") for n in ("msg_ready", "slot_free", "oh_ready", "ps_free"))
    next_ld = sem(f"{tag}_next_ld")
    gather_steps = sem(f"{tag}_gather_steps")
    ROUNDS = STEPS // RING
    assert STEPS % RING == 0

    with nc.Block() as block:
        @block.sync
        def _(sp):
            with sp.Fori(0, ROUNDS) as i:
                for r in range(RING):
                    off = sp.value_load(m.step_off[0:1, bass.ds(i * RING + r, 1)], min_val=0, max_val=EP)
                    sp.wait_ge(slot_free, i * RING + r + 1)
                    sp.dma_start(RC[:, r, :, :].rearrange("p j c -> p (j c)"),
                                 rec[bass.ds(off, CHUNK), :].rearrange("(p j) c -> p (j c)", j=CJ)).then_inc(rec_ld[r], 16)

        @block.gpsimd
        def _(pool):
            with pool.Fori(0, ROUNDS) as i:
                for r in range(RING):
                    pool.wait_ge(rec_ld[r], i * 16 + 16)
                    pool.sem_inc(gather_steps, 1)
                    for j in range(CJ):
                        pool.indirect_dma_start(G[:, r, j, :], None, table,
                                                bass.IndirectOffsetOnAxis(ap=RC[:, r, j, 0:1].bitcast(I32), axis=0)).then_inc(g_ld[r], 16)

        @block.vector
        def _(dve):
            def front(i, r):
                dve.wait_ge(slot_free, i * RING + r + RING - 1)
                dve.wait_ge(rec_ld[r], i * 16 + 16)
                dve.tensor_scalar(DR[:, r % 2, :], RC[:, r, :, 1], m.woff[:, bass.ds(i * RING + r, 1)], None, ALU.subtract)
                dve.drain()
                dve.tensor_tensor(OH[:, r % 2, :, :], m.iota_f[:, :].unsqueeze(1).to_broadcast((P, CJ, P)),
                                  DR[:, r % 2, :].unsqueeze(2).to_broadcast((P, CJ, P)), ALU.is_equal).then_inc(oh_ready, 1)
                if weighted:
                    dve.wait_ge(g_ld[r], i * 16 * CJ + 16 * CJ)
                    for j in range(CJ):
                        g = G[:, r, j, :].rearrange("p (h d) -> p h d", h=H)
                        dve.tensor_tensor(g, g, over_heads(RC[:, r, j, 2:2 + H]), ALU.mult)
                    dve.drain().then_inc(msg_ready, 1)

            def back(i, r):
                win = dve.value_load(m.step_win[0:1, bass.ds(i * RING + r, 1)], min_val=0, max_val=NT - 1)
                dve.wait_ge(slot_free, i * RING + r + RING + 1)
                dve.tensor_tensor(tile(m.ACC, win), tile(m.ACC, win), PS[r % 2][:, :], ALU.add)
                if weighted:
                    dve.tensor_tensor(tile(m.ASUM, win), tile(m.ASUM, win), PS[2 + r % 2][:, 0:H + 1], ALU.add)
                dve.drain().then_inc(ps_free, 1)

            dve.sem_inc(ps_free, 2)
            front(0, 0)
            with dve.Fori(0, ROUNDS - 1) as i:
                for r in range(RING):
                    front(i + (r + 1) // RING, (r + 1) % RING)
                    back(i, r)
            for r in range(RING):
                if r + 1 < RING:
                    front(ROUNDS - 1, r + 1)
                back(ROUNDS - 1, r)

        @block.scalar
        def _(act):
            load_next(m, act, next_ld)

        @block.tensor
        def _(pe):
            pe.sem_inc(slot_free, RING)
            with pe.Fori(0, ROUNDS) as i:
                for r in range(RING):
                    pe.wait_ge(oh_ready, i * RING + r + 1)
                    if weighted:
                        pe.wait_ge(msg_ready, i * RING + r + 1)
                    else:
                        pe.wait_ge(g_ld[r], i * 16 * CJ + 16 * CJ)
                    pe.wait_ge(ps_free, i * RING + r + 1)
                    for j in range(CJ):
                        if weighted:
                            pe.matmul(PS[2 + r % 2][:, 0:H + 1], OH[:, r % 2, j, :], RC[:, r, j, 2:R], start=(j == 0), stop=(j == CJ - 1))
                        ins = pe.matmul(PS[r % 2][:, :], OH[:, r % 2, j, :], G[:, r, j, :], start=(j == 0), stop=(j == CJ - 1))
                    ins.then_inc(slot_free, 1)


class Norms:

    def __init__(self, m, tag, per):
        self.m, self.per = m, per
        self.var_ready, self.sd_ready = m.sem(tag + "_var_ready"), m.sem(tag + "_sd_ready")

    def stats(self, dve, g, k, tiles):
        m = self.m
        for j, x in enumerate(tiles):
            dve.bn_stats(m.stats[:, j, :], x)
        dve.drain()
        for j in range(len(tiles)):
            dve.bn_aggr(m.mv[:, j, :], m.stats[:, j, :])
        dve.drain().then_inc(self.var_ready, 1)
        dve.wait_ge(self.sd_ready, g * self.per + k + 1)
        dve.reciprocal(m.rstd[:, 0:GT], m.sd[:, 0:GT])
        dve.drain()

    def apply(self, dve, out, x, j):
        m = self.m
        return dve.tensor_scalar(out, x, m.mv[:, j, 0:1], m.rstd[:, j:j + 1], ALU.subtract, ALU.mult)

    def root(self, act, g, k):
        m = self.m
        act.wait_ge(self.var_ready, g * self.per + k + 1)
        act.activation(m.sd[:, 0:GT], m.mv[:, 0:GT, 1], ACT.Sqrt, bias=m.eps[:, 0:1]).then_inc(self.sd_ready, 1)


def affine(dve, x, scale, shift):
    for a in x:
        dve.tensor_tensor(a, a, scale, ALU.mult)
    dve.drain()
    for a in x:
        dve.tensor_tensor(a, a, shift, ALU.add)
    dve.drain()


def expert_weights(m):
    take = carver(m)
    W1 = take(KD * NEXP * HID).rearrange("p (k n) -> p k n", k=KD)
    W2 = take(NEXP * HID // P * D).rearrange("p (k n) -> p k n", n=D)
    return W1, W2


def load_experts(m, eng, s):
    W1, W2 = expert_weights(m)
    for k in range(KD):
        eng.dma_start(W1[:, k, :].rearrange("p (e h) -> p e h", e=NEXP),
                      m.t["L0_ffn_W1"].rearrange("e (k p) h -> k p e h", p=P)[k]).then_inc(s, 16)
    eng.dma_start(W2, m.t["L0_ffn_W2"].rearrange("e (k p) n -> p (e k) n", p=P)).then_inc(s, 16)
    eng.wait_ge(s, 16 * (KD + 1))


def experts(nc, m):
    t, PS, sem = m.t, m.PS, m.sem
    MH = HID // P
    W1, W2 = expert_weights(m)
    take = carver(m, WBYTES // 4)
    HS = take(2 * MH * W2N).rearrange("p (r b n) -> p r b n", r=2, b=MH)
    WG = take(KD * NEXP).rearrange("p (k e) -> p k e", k=KD)
    B1 = take(NEXP * MH)
    B2 = take(D)[0:NEXP, :]
    O = take(GT * D).rearrange("p (j d) -> p j d", j=GT)
    lg = take(GT * NEXP).rearrange("p (j e) -> p j e", j=GT)
    pr = take(GT * NEXP).rearrange("p (j e) -> p j e", j=GT)
    top = take(GT * NEXP).rearrange("p (j e) -> p j e", j=GT)
    top_i = take(GT * NEXP).bitcast(U32).rearrange("p (j e) -> p j e", j=GT)
    idx = take(GT * NEXP).rearrange("p (j e) -> p j e", j=GT)
    hot = take(GT * NEXP).rearrange("p (j e) -> p j e", j=GT)
    conf = take(GT * NEXP).rearrange("p (j e) -> p j e", j=GT)
    conf_t = take(W2N)[0:NEXP, :]
    red = take(GT * 4).rearrange("p (j e) -> p j e", j=GT)
    rs = take(GT * H).rearrange("p (j e) -> p j e", j=GT)

    ld, xs_ready, xt_ps, xt_sb, lg_ps, lg_ready, pr_ready, conf_ready, ct_ps, ct_sb = (sem("s4_" + n) for n in (
        "ld", "xs_ready", "xt_ps", "xt_sb", "lg_ps", "lg_ready", "pr_ready", "conf_ready", "ct_ps", "ct_sb"))
    h_ps, h_sb, o_ps, o_used = (sem("s4_" + n) for n in ("h_ps", "h_sb", "o_ps", "o_used"))
    norms = Norms(m, "s4", 4)
    PO = NEXP + 1

    with nc.Block() as block:
        @block.sync
        def _(sp):
            sp.dma_start(WG, t["L0_ffn_Wg"].rearrange("(k p) e -> p k e", p=P)).then_inc(ld, 16)
            sp.dma_start(B1, t["L0_ffn_b1_cols"]).then_inc(ld, 16)
            sp.dma_start(B2, t["L0_ffn_b2"]).then_inc(ld, 16)
            sp.wait_ge(ld, 48)

        @block.vector
        def _(dve):
            dve.sem_inc(o_used, ONE)
            def front(g):
                Y, U, S = ([b[:, j, :] for j in range(GT)] for b in (O, m.U, m.XS))
                for j in range(GT):
                    dve.tensor_scalar(rs[:, j, :], tile(m.ASUM, g * GT + j)[:, 0:H], 1e-10, None, ALU.add)
                dve.drain()
                dve.reciprocal(rs, rs)
                dve.drain()
                for j in range(GT):
                    a = tile(m.ACC, g * GT + j).rearrange("p (h d) -> p h d", h=H)
                    dve.tensor_tensor(a, a, over_heads(rs[:, j, :]), ALU.mult)
                dve.drain()
                for j in range(GT):
                    dve.tensor_tensor(Y[j], tile(m.ACC, g * GT + j), tile(m.RES, g * GT + j), ALU.add)
                dve.drain()
                norms.stats(dve, g, 0, Y)
                for j in range(GT):
                    norms.apply(dve, Y[j], Y[j], j)
                dve.drain()
                affine(dve, Y, m.rows["L0_gnn_ln_gamma"], m.rows["L0_gnn_ln_beta"])
                for j in range(GT):
                    dve.tensor_tensor(tile(m.X, g * GT + j), tile(m.X, g * GT + j), Y[j], ALU.add)
                dve.drain()
                norms.stats(dve, g, 1, [tile(m.X, g * GT + j) for j in range(GT)])
                for j in range(GT):
                    norms.apply(dve, U[j], tile(m.X, g * GT + j), j)
                dve.drain()
                norms.stats(dve, g, 2, U)
                dve.wait_ge(xt_ps, ONE + g * GT)
                for j in range(GT):
                    norms.apply(dve, S[j], U[j], j)
                dve.drain()
                affine(dve, S, m.rows["L0_ffn_ln_g"], m.rows["L0_ffn_ln_b"])
                dve.drain().then_inc(xs_ready, 1)

            def route(g):
                dve.wait_ge(lg_ps, g + 1)
                dve.tensor_reduce(red[:, :, 0:1], PS[0][:, 0:GT * NEXP].rearrange("p (j e) -> p j e", j=GT), AX.X, ALU.max)
                dve.drain()
                dve.tensor_tensor(lg, PS[0][:, 0:GT * NEXP].rearrange("p (j e) -> p j e", j=GT),
                                  red[:, :, 0:1].to_broadcast((P, GT, NEXP)), ALU.subtract)
                dve.drain().then_inc(lg_ready, 1)
                dve.wait_ge(pr_ready, g + 1)
                dve.tensor_reduce(red[:, :, 1:2], pr, AX.X, ALU.add)
                dve.drain()
                dve.reciprocal(red[:, :, 2:3], red[:, :, 1:2])
                dve.drain()
                dve.tensor_tensor(pr, pr, red[:, :, 2:3].to_broadcast((P, GT, NEXP)), ALU.mult)
                dve.drain()
                for j in range(GT):
                    dve.max(top[:, j, :], pr[:, j, :])
                dve.drain()
                for j in range(GT):
                    dve.max_index(top_i[:, j, :], top[:, j, :], pr[:, j, :])
                dve.tensor_reduce(red[:, :, 0:1], top[:, :, 0:2], AX.X, ALU.add)
                dve.drain()
                dve.reciprocal(red[:, :, 1:2], red[:, :, 0:1])
                dve.tensor_copy(idx, top_i)
                dve.drain()
                dve.tensor_tensor(top[:, :, 0:2], top[:, :, 0:2], red[:, :, 1:2].to_broadcast((P, GT, 2)), ALU.mult)
                dve.drain()
                for j in range(GT):
                    dve.tensor_scalar(conf[:, j, :], m.iota_f[:, 0:NEXP], idx[:, j, 0:1], top[:, j, 0:1], ALU.is_equal, ALU.mult)
                    dve.tensor_scalar(hot[:, j, :], m.iota_f[:, 0:NEXP], idx[:, j, 1:2], top[:, j, 1:2], ALU.is_equal, ALU.mult)
                dve.drain()
                dve.tensor_tensor(conf, conf, hot, ALU.add)
                dve.drain().then_inc(conf_ready, 1)
                dve.wait_ge(ct_ps, g + 1)
                dve.tensor_copy(conf_t, PS[1][0:NEXP, 0:W2N]).then_inc(ct_sb, 1)

            with dve.Fori(0, NG) as g:
                front(g)
                route(g)
                for e in range(PO):
                    dve.wait_ge(o_ps, ONE + g * PO + e + 1)
                    for j in range(GT):
                        ps = PS[4 + 2 * (e % 2) + j][:, :]
                        if e < NEXP:
                            dve.scalar_tensor_tensor(O[:, j, :], ps, conf[:, j, e:e + 1], m.U[:, j, :] if e == 0 else O[:, j, :], ALU.mult, ALU.add)
                        else:
                            dve.tensor_tensor(O[:, j, :], O[:, j, :], ps, ALU.add)
                    dve.drain().then_inc(o_used, 1)
                out = [O[:, j, :] for j in range(GT)]
                norms.stats(dve, g, 3, out)
                for j in range(GT):
                    norms.apply(dve, out[j], out[j], j)
                dve.drain()
                affine(dve, out, m.rows["L0_ffn_out_g"], m.rows["L0_ffn_out_b"])
                for j in range(GT):
                    dve.tensor_tensor(tile(m.X, g * GT + j), tile(m.X, g * GT + j), out[j], ALU.add)
                dve.drain()

        @block.scalar
        def _(act):
            act.sem_inc(h_sb, ONE)
            act.wait_ge(ld, 48)
            with act.Fori(0, NG) as g:
                for k in range(3):
                    norms.root(act, g, k)
                act.wait_ge(xt_ps, ONE + g * GT + GT)
                for j in range(GT):
                    act.copy(m.XT[:, :, j * P:(j + 1) * P], PS[j][:, :].rearrange("p (k n) -> p k n", k=KD))
                act.drain().then_inc(xt_sb, 1)
                act.wait_ge(lg_ready, g + 1)
                act.activation(pr, lg, ACT.Exp).then_inc(pr_ready, 1)
                for e in range(NEXP):
                    act.wait_ge(h_ps, g * NEXP + e + 1)
                    act.wait_ge(o_ps, ONE + g * PO + max(e - 1, 0))
                    for b in range(MH):
                        act.activation(HS[:, e % 2, b, :], PS[2 + e % 2][:, b * W2N:(b + 1) * W2N], ACT.Gelu_apprx_tanh,
                                       bias=B1[:, e * MH + b:e * MH + b + 1])
                    act.drain().then_inc(h_sb, 1)
                norms.root(act, g, 3)

        @block.tensor
        def _(pe):
            pe.sem_inc(xt_ps, ONE)
            pe.sem_inc(o_ps, ONE)
            pe.wait_ge(ld, 48)

            def hidden(g, e):
                pe.wait_ge(h_sb, ONE + g * NEXP + max(e - 1, 0))
                for b in range(MH):
                    for k in range(KD):
                        at = e * HID + b * P
                        ins = pe.matmul(PS[2 + e % 2][:, b * W2N:(b + 1) * W2N], W1[:, k, at:at + P], m.XT[:, k, :],
                                        start=(k == 0), stop=(k == KD - 1))
                ins.then_inc(h_ps, 1)

            def output(g, e):
                pe.wait_ge(h_sb, ONE + g * NEXP + e + 1)
                pe.wait_ge(o_used, ONE + g * PO + max(e - 1, 0))
                for j in range(GT):
                    for b in range(MH):
                        ins = pe.matmul(PS[4 + 2 * (e % 2) + j][:, :], HS[:, e % 2, b, j * P:(j + 1) * P], W2[:, e * MH + b, :],
                                        start=(b == 0), stop=(b == MH - 1))
                ins.then_inc(o_ps, 1)

            with pe.Fori(0, NG) as g:
                pe.wait_ge(xs_ready, g + 1)
                for j in range(GT):
                    for k in range(KD):
                        ins = pe.transpose(PS[j][:, k * P:(k + 1) * P], m.XS[:, j, k * P:(k + 1) * P], m.ident[:, :])
                    ins.then_inc(xt_ps, 1)
                pe.wait_ge(xt_sb, g + 1)
                for j in range(GT):
                    for k in range(KD):
                        ins = pe.matmul(PS[0][:, j * NEXP:(j + 1) * NEXP], m.XT[:, k, j * P:(j + 1) * P], WG[:, k, :],
                                        start=(k == 0), stop=(k == KD - 1))
                ins.then_inc(lg_ps, 1)
                hidden(g, 0)
                for e in range(NEXP):
                    if e + 1 < NEXP:
                        hidden(g, e + 1)
                    if e == 1:
                        pe.wait_ge(conf_ready, g + 1)
                        for j in range(GT):
                            ins = pe.transpose(PS[1][0:NEXP, j * P:(j + 1) * P], conf[:, j, :], m.ident[:, :])
                        ins.then_inc(ct_ps, 1)
                    output(g, e)
                pe.wait_ge(ct_sb, g + 1)
                pe.wait_ge(o_used, ONE + g * PO + NEXP - 1)
                for j in range(GT):
                    ins = pe.matmul(PS[4 + j][:, :], conf_t[:, j * P:(j + 1) * P], B2, start=True, stop=True)
                ins.then_inc(o_ps, 1)


def relations(nc, m):
    t, PS, sem = m.t, m.PS, m.sem
    take = carver(m)
    WR = take(KD * NREL * D).rearrange("p (k n) -> p k n", k=KD)
    WS = take(KD * D).rearrange("p (k n) -> p k n", k=KD)
    RB = take(NREL * D)
    STG = take(GT * NREL * D).rearrange("p (j n) -> p j n", j=GT)
    ld, xs_ready, xt_ps, xt_sb, ps_ready, ps_used, rows_dr = (sem("s5_" + n) for n in (
        "ld", "xs_ready", "xt_ps", "xt_sb", "ps_ready", "ps_used", "rows_dr"))
    norms = Norms(m, "s5", 1)
    PJ = NREL + 1

    with nc.Block() as block:
        @block.sync
        def _(sp):
            sp.sem_inc(rows_dr, ONE)
            for k in range(KD):
                sp.dma_start(WR[:, k, :].rearrange("p (r f) -> p r f", r=NREL),
                             t["L1_gnn_rel_W"].rearrange("r (k p) f -> k p r f", p=P)[k]).then_inc(ld, 16)
            sp.dma_start(WS, t["L1_gnn_self_W"].rearrange("(k p) f -> p k f", p=P)).then_inc(ld, 16)
            sp.dma_start(RB, t["L1_gnn_rel_b"].rearrange("r f -> (r f)").partition_broadcast(P)).then_inc(ld, 16)
            with sp.Fori(0, NG) as g:
                for j in range(GT):
                    sp.wait_ge(ps_used, ONE + (g * GT + j + 1) * PJ)
                    sp.dma_start(m.rel_rows[bass.ds((g * GT + j) * P * NREL, P * NREL), :].rearrange("(p r) f -> p (r f)", r=NREL),
                                 STG[:, j, :]).then_inc(rows_dr, 16)
            sp.wait_ge(rows_dr, ONE + 16 * NT)

        @block.vector
        def _(dve):
            dve.sem_inc(ps_used, ONE)
            dve.memset(m.ACC[:, :, :], 0.0)
            dve.wait_ge(ld, 16 * (KD + 2))
            with dve.Fori(0, NG) as g:
                norms.stats(dve, g, 0, [tile(m.X, g * GT + j) for j in range(GT)])
                dve.wait_ge(xt_ps, ONE + g)
                for j in range(GT):
                    norms.apply(dve, m.XS[:, j, :], tile(m.X, g * GT + j), j)
                dve.drain().then_inc(xs_ready, 1)
                for j in range(GT):
                    dve.tensor_tensor(tile(m.RES, g * GT + j), m.XS[:, j, :], m.rows["L1_gnn_self_b"], ALU.add)
                dve.drain()
                dve.wait_ge(rows_dr, ONE + g * 16 * GT)
                for j in range(GT):
                    for r in range(PJ):
                        n = j * PJ + r
                        dve.wait_ge(ps_ready, ONE + g * GT * PJ + n + 1)
                        ps = PS[2 + n % 4][:, :]
                        if r < NREL:
                            dve.tensor_tensor(STG[:, j, r * D:(r + 1) * D], ps, RB[:, r * D:(r + 1) * D], ALU.add).then_inc(ps_used, 1)
                        else:
                            dve.tensor_tensor(tile(m.RES, g * GT + j), tile(m.RES, g * GT + j), ps, ALU.add).then_inc(ps_used, 1)

        @block.scalar
        def _(act):
            with act.Fori(0, NG) as g:
                norms.root(act, g, 0)
                act.wait_ge(xt_ps, ONE + g + 1)
                act.wait_ge(ps_ready, ONE + g * GT * PJ)
                for j in range(GT):
                    act.copy(m.XT[:, :, j * P:(j + 1) * P], PS[j][:, :].rearrange("p (k n) -> p k n", k=KD))
                act.drain().then_inc(xt_sb, 1)

        @block.tensor
        def _(pe):
            pe.sem_inc(xt_ps, ONE)
            pe.sem_inc(ps_ready, ONE)
            pe.wait_ge(ld, 16 * (KD + 2))
            with pe.Fori(0, NG) as g:
                pe.wait_ge(xs_ready, g + 1)
                for j in range(GT):
                    for k in range(KD):
                        ins = pe.transpose(PS[j][:, k * P:(k + 1) * P], m.XS[:, j, k * P:(k + 1) * P], m.ident[:, :])
                ins.then_inc(xt_ps, 1)
                pe.wait_ge(xt_sb, g + 1)
                for j in range(GT):
                    for r in range(PJ):
                        n = j * PJ + r
                        pe.wait_ge(ps_used, ONE + g * GT * PJ + max(n - 3, 0))
                        for k in range(KD):
                            w = WR[:, k, r * D:(r + 1) * D] if r < NREL else WS[:, k, :]
                            ins = pe.matmul(PS[2 + n % 4][:, :], m.XT[:, k, j * P:(j + 1) * P], w, start=(k == 0), stop=(k == KD - 1))
                        ins.then_inc(ps_ready, 1)


def ffn_weights(m):
    take = carver(m)
    W1 = take(KD * FF).rearrange("p (k n) -> p k n", k=KD)
    W2 = take(FF // P * D).rearrange("p (k n) -> p k n", n=D)
    return W1, W2


def load_ffn(m, eng, s):
    W1, W2 = ffn_weights(m)
    eng.dma_start(W1, m.t["L1_gnn_W1"].rearrange("(k p) n -> p k n", p=P)).then_inc(s, 16)
    eng.dma_start(W2, m.t["L1_gnn_W2"].rearrange("(k p) n -> p k n", p=P)).then_inc(s, 16)
    eng.wait_ge(s, 32)


def ffn(nc, m):
    t, PS, sem = m.t, m.PS, m.sem
    MB = 2
    NQ = FF // P // MB
    W1, W2 = ffn_weights(m)
    take = carver(m, WBYTES // 4)
    HS = take(2 * MB * W2N).rearrange("p (r b n) -> p r b n", r=2, b=MB)
    B1 = take(FF // P)
    deg = take(NT)
    Y = take(GT * D).rearrange("p (j d) -> p j d", j=GT)
    ld, xs_ready, xt_ps, xt_sb, h_ps, h_sb, o_ps, o_used = (sem("s7_" + n) for n in (
        "ld", "xs_ready", "xt_ps", "xt_sb", "h_ps", "h_sb", "o_ps", "o_used"))
    norms = Norms(m, "s7", 2)

    with nc.Block() as block:
        @block.sync
        def _(sp):
            sp.dma_start(B1, t["L1_gnn_b1_cols"]).then_inc(ld, 16)
            sp.wait_ge(ld, 16)

        @block.vector
        def _(dve):
            dve.sem_inc(o_used, ONE)
            dve.tensor_scalar(deg, m.ASUM[:, :, H], 1.0, None, ALU.max)
            dve.drain()
            dve.reciprocal(deg, deg)
            dve.drain()
            with dve.Fori(0, NG) as g:
                S = [m.XS[:, j, :] for j in range(GT)]
                O = [Y[:, j, :] for j in range(GT)]
                dve.wait_ge(xt_ps, ONE + g)
                for j in range(GT):
                    dve.scalar_tensor_tensor(S[j], tile(m.ACC, g * GT + j), deg[:, bass.ds(g * GT + j, 1)], tile(m.RES, g * GT + j), ALU.mult, ALU.add)
                dve.drain()
                norms.stats(dve, g, 0, S)
                for j in range(GT):
                    norms.apply(dve, S[j], S[j], j)
                dve.drain()
                affine(dve, S, m.rows["L1_gnn_ln1_w"], m.rows["L1_gnn_ln1_b"])
                dve.drain().then_inc(xs_ready, 1)
                for j in range(GT):
                    dve.tensor_tensor(O[j], S[j], m.rows["L1_gnn_b2"], ALU.add)
                dve.drain()
                dve.wait_ge(o_ps, g + 1)
                for j in range(GT):
                    dve.tensor_tensor(O[j], O[j], PS[4 + j][:, :], ALU.add)
                dve.drain().then_inc(o_used, 1)
                norms.stats(dve, g, 1, O)
                for j in range(GT):
                    norms.apply(dve, O[j], O[j], j)
                dve.drain()
                affine(dve, O, m.rows["L1_gnn_ln2_w"], m.rows["L1_gnn_ln2_b"])
                for j in range(GT):
                    dve.tensor_tensor(tile(m.X, g * GT + j), tile(m.X, g * GT + j), O[j], ALU.add)
                dve.drain()

        @block.scalar
        def _(act):
            act.sem_inc(h_sb, ONE)
            act.wait_ge(ld, 16)
            with act.Fori(0, NG) as g:
                norms.root(act, g, 0)
                act.wait_ge(xt_ps, ONE + g + 1)
                for j in range(GT):
                    act.copy(m.XT[:, :, j * P:(j + 1) * P], PS[j][:, :].rearrange("p (k n) -> p k n", k=KD))
                act.drain().then_inc(xt_sb, 1)
                for q in range(NQ):
                    act.wait_ge(h_ps, g * NQ + q + 1)
                    for b in range(MB):
                        act.activation(HS[:, q % 2, b, :], PS[2 + q % 2][:, b * W2N:(b + 1) * W2N], ACT.Gelu,
                                       bias=B1[:, q * MB + b:q * MB + b + 1])
                    act.drain().then_inc(h_sb, 1)
                norms.root(act, g, 1)

        @block.tensor
        def _(pe):
            pe.sem_inc(xt_ps, ONE)
            def hidden(g, q):
                pe.wait_ge(h_sb, ONE + g * NQ + max(q - 1, 0))
                for b in range(MB):
                    at = (q * MB + b) * P
                    for k in range(KD):
                        ins = pe.matmul(PS[2 + q % 2][:, b * W2N:(b + 1) * W2N], W1[:, k, at:at + P], m.XT[:, k, :],
                                        start=(k == 0), stop=(k == KD - 1))
                ins.then_inc(h_ps, 1)

            with pe.Fori(0, NG) as g:
                pe.wait_ge(xs_ready, g + 1)
                for j in range(GT):
                    for k in range(KD):
                        ins = pe.transpose(PS[j][:, k * P:(k + 1) * P], m.XS[:, j, k * P:(k + 1) * P], m.ident[:, :])
                ins.then_inc(xt_ps, 1)
                pe.wait_ge(xt_sb, g + 1)
                hidden(g, 0)
                pe.wait_ge(o_used, ONE + g)
                hidden(g, 1)
                for q in range(NQ):
                    pe.wait_ge(h_sb, ONE + g * NQ + q + 1)
                    for b in range(MB):
                        for j in range(GT):
                            ins = pe.matmul(PS[4 + j][:, :], HS[:, q % 2, b, j * P:(j + 1) * P], W2[:, q * MB + b, :],
                                            start=(q == 0 and b == 0), stop=(q == NQ - 1 and b == MB - 1))
                    if q + 2 < NQ:
                        hidden(g, q + 2)
                ins.then_inc(o_ps, 1)


ALU_LO, ALU_HI, AX_LO, AX_HI = 16, 32, 48, 64
OPC_ADD, OPC_SUB, OPCODE_BASE, OP_START = 25, 26, 80, 10
OUTPUT_LO, OUTPUT_HI, CARRY = 128, 144, 160
NF = 4
MARK_AX, OP_ADD, OP_SUB = 0, 1, 2


def nibbles(nc, m):
    t, PS, sem = m.t, m.PS, m.sem
    take = carver(m)
    REM = GE - P
    W0 = take(2 * GE)[0:NF, :].rearrange("p (a n) -> p a n", a=2)
    W1a = take(2 * GE).rearrange("p (a n) -> p a n", a=2)
    W1b = take(2 * GE)[0:REM, :].rearrange("p (a n) -> p a n", a=2)
    W2a = take(2 * 2).rearrange("p (a n) -> p a n", a=2)
    W2b = take(2 * 2)[0:REM, :].rearrange("p (a n) -> p a n", a=2)
    Ba = take(2 * 2).rearrange("p (a n) -> p a n", a=2)
    Bb = take(2 * 2)[0:REM, :].rearrange("p (a n) -> p a n", a=2)
    BO = take(2 * 2).rearrange("p (a n) -> p a n", a=2)
    Y = take(GT * D).rearrange("p (j d) -> p j d", j=GT)
    desc = take(16)
    gt = take(GT * 64).rearrange("p (j n) -> p j n", j=GT)
    nib = take(GT * 4).rearrange("p (j n) -> p j n", j=GT)
    msk = take(GT * 4).rearrange("p (j n) -> p j n", j=GT)
    FT = take(2 * GT * NF).rearrange("p (s j f) -> p s j f", s=2, j=GT)
    mk = take(GT * 8).rearrange("p (j n) -> p j n", j=GT)
    FS = take(2 * W2N)[0:NF, :]
    H1a = take(2 * 2 * W2N).rearrange("p (a n) -> p a n", a=2)
    H1b = take(2 * 2 * W2N)[0:REM, :].rearrange("p (a n) -> p a n", a=2)
    H2a = take(2 * 2 * W2N).rearrange("p (a n) -> p a n", a=2)
    H2b = take(2 * 2 * W2N)[0:REM, :].rearrange("p (a n) -> p a n", a=2)
    res = take(GT * 8).rearrange("p (j s a n) -> p j s a n", j=GT, s=2, a=2)
    y = take(GT * 4).rearrange("p (j s n) -> p j s n", j=GT, s=2)
    y2 = take(GT * 4).rearrange("p (j s n) -> p j s n", j=GT, s=2)
    oh = take(GT * 32).rearrange("p (j s n) -> p j s n", j=GT, s=2)

    ld, desc_ready, f_ready, f_ps, f_sb, h1_ps, h1_sb, h2_ps, h2_sb, y_ps, y_used, out_ready, out_dr = (sem("s8_" + n) for n in (
        "ld", "desc_ready", "f_ready", "f_ps", "f_sb", "h1_ps", "h1_sb", "h2_ps", "h2_sb", "y_ps", "y_used", "out_ready", "out_dr"))
    norms = Norms(m, "s8", 1)

    with nc.Block() as block:
        @block.sync
        def _(sp):
            for a, (w, b) in enumerate((("L1_ffn_Wa", "L1_ffn_ba"), ("L1_ffn_Ws", "L1_ffn_bs"))):
                wt, bc = t[w + "_T"], t[b + "_cols"]
                sp.dma_start(W0[0:2, a, :], wt[0, 0:2, :]).then_inc(ld, 16)
                sp.dma_start(W0[2:4, a, :], wt[0, OP_START + OPC_ADD:OP_START + OPC_SUB + 1, :]).then_inc(ld, 16)
                sp.dma_start(W1a[:, a, :], wt[1, 0:P, :]).then_inc(ld, 16)
                sp.dma_start(W1b[:, a, :], wt[1, P:GE, :]).then_inc(ld, 16)
                sp.dma_start(W2a[:, a, :], wt[2, 0:P, 100:102]).then_inc(ld, 16)
                sp.dma_start(W2b[:, a, :], wt[2, P:GE, 100:102]).then_inc(ld, 16)
                sp.dma_start(Ba[:, a, :], bc[0:P, 0:2]).then_inc(ld, 16)
                sp.dma_start(Bb[:, a, :], bc[P:GE, 0:2]).then_inc(ld, 16)
                sp.dma_start(BO[:, a, :], t[b][2, 100:102].partition_broadcast(P)).then_inc(ld, 16)
            with sp.Fori(0, NG - 1) as g:
                sp.wait_ge(out_ready, g + 1)
                sp.dma_start(t["out"][bass.ds(g * W2N, W2N), :].rearrange("(j p) d -> p j d", p=P), m.X[:, bass.ds(g * GT, GT), :]).then_inc(out_dr, 16)
            sp.wait_ge(out_ready, NG)
            sp.dma_start(t["out"][(NT - 2) * P:(NT - 1) * P, :], m.X[:, NT - 2, :]).then_inc(out_dr, 16)
            sp.dma_start(t["out"][(NT - 1) * P:N, :], m.X[0:LAST, NT - 1, :]).then_inc(out_dr, 16)
            sp.wait_ge(out_dr, 16 * (NG + 1))

        @block.gpsimd
        def _(pool):
            pool.iota(desc, [[-1, 16]], base=16, channel_multiplier=0, allow_small_or_imprecise_dtypes=True).then_inc(desc_ready, 1)

        @block.vector
        def _(dve):
            dve.sem_inc(y_used, ONE)
            dve.wait_ge(desc_ready, 1)
            dve.wait_ge(ld, 16 * 18)
            with dve.Fori(0, NG) as g:
                norms.stats(dve, g, 0, [tile(m.X, g * GT + j) for j in range(GT)])
                for j in range(GT):
                    norms.apply(dve, Y[:, j, :], tile(m.X, g * GT + j), j)
                dve.drain()
                dve.tensor_scalar(gt, Y[:, :, ALU_LO:ALU_LO + 64], 0.5, None, ALU.is_gt)
                dve.tensor_scalar(mk[:, :, 0:3], Y[:, :, 0:3], 0.5, None, ALU.is_gt)
                dve.drain()
                for j in range(GT):
                    q = gt[:, j, :].rearrange("p (q n) -> p q n", q=4)
                    dve.tensor_tensor(q, q, desc.unsqueeze(1).to_broadcast((P, 4, 16)), ALU.mult)
                dve.drain()
                dve.tensor_reduce(nib, gt.rearrange("p j (q n) -> p j q n", q=4), AX.X, ALU.max)
                dve.drain()
                dve.tensor_scalar(msk, nib, 0.0, None, ALU.is_gt)
                dve.tensor_scalar(nib, nib, -1.0, 16.0, ALU.mult, ALU.add)
                dve.drain()
                dve.tensor_tensor(nib, nib, msk, ALU.mult)
                dve.tensor_tensor(mk[:, :, 3:4], mk[:, :, 0:1], mk[:, :, 1:2], ALU.mult)
                dve.tensor_tensor(mk[:, :, 5:6], mk[:, :, 0:1], mk[:, :, 2:3], ALU.mult)
                dve.drain()
                dve.tensor_tensor(mk[:, :, 6:7], mk[:, :, 5:6], mk[:, :, 1:2], ALU.mult)
                for s in range(2):
                    dve.tensor_copy(FT[:, s, :, 0:1], nib[:, :, s:s + 1])
                    dve.tensor_copy(FT[:, s, :, 1:2], nib[:, :, 2 + s:3 + s])
                    dve.tensor_copy(FT[:, s, :, 2:4], Y[:, :, OPCODE_BASE + OPC_ADD:OPCODE_BASE + OPC_SUB + 1])
                dve.drain().then_inc(f_ready, 1)
                dve.tensor_tensor(mk[:, :, 4:5], mk[:, :, 5:6], mk[:, :, 6:7], ALU.subtract)
                dve.drain()
                dve.tensor_tensor(mk[:, :, 7:8], mk[:, :, 3:4], mk[:, :, 4:5], ALU.add)
                dve.wait_ge(f_ps, g + 1)
                dve.tensor_copy(FS, PS[0][0:NF, 0:2 * W2N])
                dve.drain().then_inc(f_sb, 1)
                dve.wait_ge(y_ps, g + 1)
                dve.tensor_tensor(res.rearrange("p j s a n -> p (j s) (a n)"),
                                  PS[7][:, 0:GT * 8].rearrange("p (q n) -> p q n", n=4),
                                  BO.rearrange("p a n -> p (a n)").unsqueeze(1).to_broadcast((P, 2 * GT, 4)), ALU.add)
                dve.drain().then_inc(y_used, 1)
                for j in range(GT):
                    dve.tensor_scalar(y[:, j, :, :], res[:, j, :, 0, :], mk[:, j, 3:4], None, ALU.mult)
                    dve.tensor_scalar(y2[:, j, :, :], res[:, j, :, 1, :], mk[:, j, 4:5], None, ALU.mult)
                dve.drain()
                dve.tensor_tensor(y, y, y2, ALU.add)
                dve.drain()
                dve.tensor_scalar(y, y, ROUND, ROUND, ALU.add, ALU.subtract)
                dve.drain()
                dve.tensor_scalar(y[:, :, :, 0:1], y[:, :, :, 0:1], 0.0, 15.0, ALU.max, ALU.min)
                dve.tensor_scalar(y2[:, :, 1:2, 1:2], y[:, :, 1:2, 1:2], 0.5, None, ALU.is_gt)
                dve.tensor_scalar(mk[:, :, 6:7], mk[:, :, 7:8], 2.0, None, ALU.mult)
                dve.drain()
                for j in range(GT):
                    for s in range(2):
                        dve.tensor_scalar(oh[:, j, s, :], m.iota_f[:, 0:16], y[:, j, s, 0:1], mk[:, j, 6:7], ALU.is_equal, ALU.mult)
                    dve.tensor_tensor(y2[:, j, 1, 1:2], y2[:, j, 1, 1:2], mk[:, j, 7:8], ALU.mult)
                dve.drain()
                for j in range(GT):
                    dve.tensor_tensor(Y[:, j, OUTPUT_LO:CARRY], Y[:, j, OUTPUT_LO:CARRY], oh[:, j, :, :].rearrange("p s n -> p (s n)"), ALU.add)
                    dve.tensor_tensor(Y[:, j, CARRY:CARRY + 1], Y[:, j, CARRY:CARRY + 1], y2[:, j, 1, 1:2], ALU.add)
                dve.drain()
                for j in range(GT):
                    dve.tensor_tensor(tile(m.X, g * GT + j), tile(m.X, g * GT + j), Y[:, j, :], ALU.add)
                dve.drain().then_inc(out_ready, 1)

        @block.scalar
        def _(act):
            act.wait_ge(ld, 16 * 18)
            with act.Fori(0, NG) as g:
                norms.root(act, g, 0)
                for layer, (ps, sbuf, Ha, Hb) in enumerate(((h1_ps, h1_sb, H1a, H1b), (h2_ps, h2_sb, H2a, H2b))):
                    for a in range(2):
                        act.wait_ge(ps, g * 2 + a + 1)
                        act.activation(Ha[:, a, :], PS[1 + a][:, :], ACT.Relu, bias=Ba[:, a, layer:layer + 1])
                        act.activation(Hb[:, a, :], PS[3 + a][0:REM, :], ACT.Relu, bias=Bb[:, a, layer:layer + 1])
                        act.drain().then_inc(sbuf, 1)

        @block.tensor
        def _(pe):
            pe.wait_ge(ld, 16 * 18)
            with pe.Fori(0, NG) as g:
                pe.wait_ge(f_ready, g + 1)
                for s in range(2):
                    for j in range(GT):
                        ins = pe.transpose(PS[0][0:NF, (s * GT + j) * P:(s * GT + j + 1) * P], FT[:, s, j, :], m.ident[:, :])
                ins.then_inc(f_ps, 1)
                pe.wait_ge(f_sb, g + 1)
                for a in range(2):
                    pe.matmul(PS[1 + a][:, :], W0[:, a, 0:P], FS, start=True, stop=True)
                    pe.matmul(PS[3 + a][0:REM, :], W0[:, a, P:GE], FS, start=True, stop=True).then_inc(h1_ps, 1)
                for a in range(2):
                    pe.wait_ge(h1_sb, g * 2 + a + 1)
                    for ps, lo, hi in ((PS[1 + a][:, :], 0, P), (PS[3 + a][0:REM, :], P, GE)):
                        pe.matmul(ps, W1a[:, a, lo:hi], H1a[:, a, :], start=True, stop=False)
                        ins = pe.matmul(ps, W1b[:, a, lo:hi], H1b[:, a, :], start=False, stop=True)
                    ins.then_inc(h2_ps, 1)
                pe.wait_ge(y_used, ONE + g)
                pe.wait_ge(h2_sb, g * 2 + 2)
                for j in range(GT):
                    for s in range(2):
                        for a in range(2):
                            at = ((j * 2 + s) * 2 + a) * 2
                            q = (s * GT + j) * P
                            pe.matmul(PS[7][:, at:at + 2], H2a[:, a, q:q + P], W2a[:, a, :], start=True, stop=False)
                            ins = pe.matmul(PS[7][:, at:at + 2], H2b[:, a, q:q + P], W2b[:, a, :], start=False, stop=True)
                ins.then_inc(y_ps, 1)


_PLAIN = ["x", "src", "dst", "edge_type_4", "edge_type_8", "edge_weight", "L0_gnn_W", "L0_gnn_a_src", "L0_gnn_a_dst",
          "L0_gnn_et_emb", "L0_ffn_Wg", "L0_ffn_W1", "L0_ffn_W2", "L0_ffn_b2", "L1_gnn_self_W", "L1_gnn_rel_W",
          "L1_gnn_rel_b", "L1_gnn_W1", "L1_gnn_W2", "L1_ffn_ba", "L1_ffn_bs"] + ROW_NAMES


def kernel(**inputs):
    import concourse.bacc as _bacc
    from concourse.bass_utils import run_bass_kernel_spmd as _run

    a = {name: np.ascontiguousarray(inputs[name]) for name in _PLAIN}
    a["L0_gnn_WT"] = np.ascontiguousarray(np.asarray(inputs["L0_gnn_W"]).T)
    a["L0_ffn_b1_cols"] = np.ascontiguousarray(np.asarray(inputs["L0_ffn_b1"]).reshape(-1, P).T)
    a["L1_gnn_b1_cols"] = np.ascontiguousarray(np.asarray(inputs["L1_gnn_b1"]).reshape(-1, P).T)
    for w, b in (("L1_ffn_Wa", "L1_ffn_ba"), ("L1_ffn_Ws", "L1_ffn_bs")):
        a[w + "_T"] = np.ascontiguousarray(np.asarray(inputs[w]).transpose(0, 2, 1))
        a[b + "_cols"] = np.ascontiguousarray(np.asarray(inputs[b]).T)

    nc = _bacc.Bacc("TRN2", target_bir_lowering=False, num_devices=1)
    t = {name: nc.dram_tensor("in_" + name, v.shape, mybir.dt.from_np(v.dtype), kind="ExternalInput").ap() for name, v in a.items()}
    t["out"] = nc.dram_tensor("out", (N, D), F32, kind="ExternalOutput").ap()
    build(nc, t)
    r = _run(nc, [{"in_" + name: v for name, v in a.items()}], core_ids=[0])
    return r.results[0]["out"]
```

```python
from contextlib import ExitStack

import concourse.bass as bass
import numpy as np
from concourse import mybir

ALU = mybir.AluOpType
ACT = mybir.ActivationFunctionType
AX = mybir.AxisListType
F32, F16, BF16 = mybir.dt.float32, mybir.dt.float16, mybir.dt.bfloat16
I32, U32 = mybir.dt.int32, mybir.dt.uint32

P = 128
N = 1250
D = 512
E = 40000
NT = -(-N // P)
NP = NT * P
LAST = N - (NT - 1) * P
KD = D // P
H, HD = 8, 64
NREL = 4
NTYPE = 8
NEXP, HID = 8, 256
FF = 1024
GT = 2
NG = NT // GT
W2N = GT * P

C = -(-E // P)
EP = C * P
CG = 16
NCG = -(-C // CG)
CP = NCG * CG
TAIL = E - (P - 1) * C
CHUNK = 512
CJ = CHUNK // P
STEPS = (EP + NT * (CHUNK - 1)) // CHUNK
RING = 4
R0 = 2 + H + 1
R1 = 2
PARTS = 3
EPS = 1e-5
NEG_SLOPE = 0.2
PAD_DST = NP - 1
ROUND = 12582912.0
GE = 160
ONE = 1
WBYTES = 64 * 1024

ROW_NAMES = ["L0_gnn_ln_gamma", "L0_gnn_ln_beta", "L0_ffn_ln_g", "L0_ffn_ln_b", "L0_ffn_out_g",
             "L0_ffn_out_b", "L1_gnn_self_b", "L1_gnn_ln1_w", "L1_gnn_ln1_b", "L1_gnn_b2",
             "L1_gnn_ln2_w", "L1_gnn_ln2_b"]


class Shared:
    pass


def tile(ap, i):
    return ap[:, bass.ds(i, 1), :].rearrange("p a d -> p (a d)")


def over_heads(ap):
    return ap.unsqueeze(2).to_broadcast((P, H, HD))


def build(nc, t):
    with ExitStack() as ctx:
        m = Shared()
        m.t = t

        def sb(name, shape, dt=F32):
            return ctx.enter_context(nc.sbuf_tensor(name, shape, dt))

        def sem(name):
            return ctx.enter_context(nc.semaphore(name))

        def dram(name, shape, dt=F32):
            return nc.dram_tensor(name, shape, dt, kind="Internal").ap()

        m.sb, m.sem = sb, sem
        m.h_rows = dram("h_rows", [NP, D])
        m.rel_rows = dram("rel_rows", [NP * NREL, D])
        m.rec0 = dram("rec0", [EP + CHUNK, R0])
        m.rec1 = dram("rec1", [EP + CHUNK, R1])
        m.src_cp = dram("src_cp", [CP, P], F16)
        m.dst_cp = dram("dst_cp", [CP, P], F16)

        m.X = sb("X", [P, NT, D])
        m.ACC = sb("ACC", [P, NT, D])
        m.ASUM = sb("ASUM", [P, NT, H + 1])
        m.RES = sb("RES", [P, NT, D])
        m.XS = sb("XS", [P, GT, D])
        m.XT = sb("XT", [P, KD, W2N])
        m.U = sb("U", [P, GT, D])
        m.ident = sb("ident", [P, P])
        m.iota_f = sb("iota_f", [P, P])
        m.iota_k = sb("iota_k", [P, NT])
        m.ones = sb("ones", [P, P])
        m.eps = sb("eps", [P, 1])
        m.ROWS = sb("ROWS", [P, len(ROW_NAMES), D])
        m.rows = {name: m.ROWS[:, n, :] for n, name in enumerate(ROW_NAMES)}
        m.stats = sb("stats", [P, NT, 6])
        m.mv = sb("mv", [P, NT, 2])
        m.sd = sb("sd", [P, NT])
        m.rstd = sb("rstd", [P, NT])
        m.TAB = sb("TAB", [P, 2, NT, PARTS, H], BF16)
        m.woff = sb("woff", [P, STEPS])
        m.step_off = sb("step_off", [P, STEPS], I32)
        m.step_win = sb("step_win", [P, STEPS], I32)
        m.arena_words = 26 * 1024 + 512
        m.arena = sb("arena", [P, m.arena_words])
        m.PS = [ctx.enter_context(nc.psum_tensor(f"PS{i}", [P, 512], F32)) for i in range(8)]

        node_scores(nc, m)
        load_edges(nc, m)
        sort_edges(nc, m)
        edge_weights(nc, m)
        messages(nc, m, "m0", m.rec0, R0, m.h_rows, True, load_experts)
        experts(nc, m)
        relations(nc, m)
        messages(nc, m, "m1", m.rec1, R1, m.rel_rows, False, load_ffn)
        ffn(nc, m)
        nibbles(nc, m)


def carver(m, start=0):
    at = [start]

    def take(words):
        at[0] += words
        assert at[0] <= m.arena_words, at
        return m.arena[:, at[0] - words:at[0]]
    return take


def node_scores(nc, m):
    t, PS, sem = m.t, m.PS, m.sem
    take = carver(m)
    WT = take(KD * D).rearrange("p (k d) -> p k d", k=KD)
    WR = take(KD * D).rearrange("p (k d) -> p k d", k=KD)
    WA = take(KD * 2 * H).rearrange("p (k d) -> p k d", k=KD)
    AB = take(KD * 2 * H).rearrange("p (k d) -> p k d", k=KD)
    STG = take(GT * D).rearrange("p (j d) -> p j d", j=GT)
    SV = take(NT * 2 * H).rearrange("p (t s) -> p t s", t=NT)
    SR = take(NT * 2 * H).rearrange("p (t s) -> p t s", t=NT)

    x_ld, w_ld, a_ld, row_ld, x_zero, ab_zero, consts, wa_ps, wa_sb = (sem("s1_" + n) for n in (
        "x_ld", "w_ld", "a_ld", "row_ld", "x_zero", "ab_zero", "consts", "wa_ps", "wa_sb"))
    mv_ready, sd_ready, xs_ready, xt_ps, xt_sb, res_sb, h_ps, h_sb, h_dr = (sem("s1_" + n) for n in (
        "mv_ready", "sd_ready", "xs_ready", "xt_ps", "xt_sb", "res_sb", "h_ps", "h_sb", "h_dr"))

    with nc.Block() as block:
        @block.sync
        def _(sp):
            sp.sem_inc(h_dr, ONE)
            sp.wait_ge(x_zero, 1)
            sp.dma_start(m.X[:, 0:NT - 1, :], t["x"][0:(NT - 1) * P, :].rearrange("(t p) d -> p t d", p=P)).then_inc(x_ld, 16)
            sp.dma_start(m.X[0:LAST, NT - 1, :], t["x"][(NT - 1) * P:N, :]).then_inc(x_ld, 16)
            sp.dma_start(WR, t["L0_gnn_W"].rearrange("(k p) d -> p k d", p=P)).then_inc(w_ld, 16)
            sp.dma_start(WT, t["L0_gnn_WT"].rearrange("(k p) d -> p k d", p=P)).then_inc(w_ld, 16)
            for name in ROW_NAMES:
                sp.dma_start(m.rows[name], t[name].partition_broadcast(P)).then_inc(row_ld, 16)
            with sp.Fori(0, NG) as g:
                sp.wait_ge(h_sb, ONE + g * GT + GT)
                sp.dma_start(m.h_rows[bass.ds(g * W2N, W2N), :].rearrange("(j p) d -> p j d", p=P), STG).then_inc(h_dr, 16)
            sp.wait_ge(h_dr, ONE + 16 * NG)
            sp.wait_ge(row_ld, 16 * len(ROW_NAMES))

        @block.gpsimd
        def _(pool):
            pool.memset(m.X[:, NT - 1, :], 0.0).then_inc(x_zero, 1)
            pool.memset(AB, 0.0).then_inc(ab_zero, 1)
            pool.memset(m.eps[:, :], EPS)
            pool.memset(m.ones[:, :], 1.0)
            pool.memset(m.ident[:, :], 0.0)
            pool.iota(m.iota_f[:, :], [[1, P]], base=0, channel_multiplier=0, allow_small_or_imprecise_dtypes=True)
            pool.iota(m.iota_k[:, :], [[P, NT]], base=0, channel_multiplier=1, allow_small_or_imprecise_dtypes=True)
            pool.drain()
            pool.affine_select(out=m.ident[:, :], in_=m.ident[:, :], compare_op=ALU.not_equal, fill=1.0, base=0,
                               pattern=[[-1, P]], channel_multiplier=1).then_inc(consts, 1)
            pool.wait_ge(ab_zero, 1)
            for h in range(H):
                lo = (h * HD) % P
                for s, name in enumerate(("L0_gnn_a_src", "L0_gnn_a_dst")):
                    pool.dma_start(AB[lo:lo + HD, h * HD // P, s * H + h:s * H + h + 1],
                                   t[name][h:h + 1, :].rearrange("a d -> d a")).then_inc(a_ld, 16)
            pool.wait_ge(a_ld, 16 * 2 * H)

        @block.vector
        def _(dve):
            dve.sem_inc(h_sb, ONE)
            dve.memset(m.ACC[:, :, :], 0.0)
            dve.memset(m.ASUM[:, :, :], 0.0)
            dve.wait_ge(x_ld, 32)
            for i in range(NT):
                dve.bn_stats(m.stats[:, i, :], m.X[:, i, :])
            dve.drain()
            for i in range(NT):
                dve.bn_aggr(m.mv[:, i, :], m.stats[:, i, :])
            dve.drain().then_inc(mv_ready, 1)
            dve.wait_ge(wa_ps, 1)
            dve.tensor_copy(WA, PS[7][:, 0:KD * 2 * H].rearrange("p (k d) -> p k d", k=KD)).then_inc(wa_sb, 1)
            dve.wait_ge(sd_ready, 1)
            dve.reciprocal(m.rstd[:, :], m.sd[:, :])
            dve.drain()
            with dve.Fori(0, NG) as g:
                dve.wait_ge(xt_ps, ONE + g * GT)
                dve.wait_ge(res_sb, ONE + g * GT)
                for j in range(GT):
                    dve.tensor_scalar(m.XS[:, j, :], tile(m.X, g * GT + j), tile(m.mv, g * GT + j)[:, 0:1],
                                      m.rstd[:, bass.ds(g * GT + j, 1)], ALU.subtract, ALU.mult).then_inc(xs_ready, 1)
                dve.wait_ge(h_dr, ONE + g * 16)
                for j in range(GT):
                    dve.wait_ge(h_ps, ONE + g * GT + j + 1)
                    dve.tensor_copy(STG[:, j, :], PS[4 + j][:, :])
                    dve.tensor_copy(tile(SV, g * GT + j), PS[2 + j][:, 0:2 * H])
                    dve.drain().then_inc(h_sb, 1)
            for s in range(2):
                left = SV[:, :, s * H:(s + 1) * H]
                for part in range(PARTS):
                    dve.tensor_copy(m.TAB[:, s, :, part, :], left)
                    dve.drain()
                    if part < PARTS - 1:
                        rest = SR[:, :, part * H:(part + 1) * H]
                        dve.tensor_tensor(rest, left, m.TAB[:, s, :, part, :], ALU.subtract)
                        dve.drain()
                        left = rest

        @block.scalar
        def _(act):
            act.sem_inc(res_sb, ONE)
            act.sem_inc(xt_sb, ONE)
            act.wait_ge(consts, 1)
            act.wait_ge(mv_ready, 1)
            act.activation(m.sd[:, :], m.mv[:, :, 1], ACT.Sqrt, bias=m.eps[:, 0:1]).then_inc(sd_ready, 1)
            with act.Fori(0, NG) as g:
                for j in range(GT):
                    act.wait_ge(xs_ready, g * GT + j + 1)
                    act.copy(tile(m.RES, g * GT + j), m.XS[:, j, :]).then_inc(res_sb, 1)
                act.wait_ge(h_ps, ONE + g * GT)
                for j in range(GT):
                    act.wait_ge(xt_ps, ONE + g * GT + j + 1)
                    act.copy(m.XT[:, :, j * P:(j + 1) * P], PS[j][:, :].rearrange("p (k n) -> p k n", k=KD)).then_inc(xt_sb, 1)

        @block.tensor
        def _(pe):
            pe.sem_inc(xt_ps, ONE)
            pe.sem_inc(h_ps, ONE)
            pe.wait_ge(consts, 1)
            pe.wait_ge(w_ld, 32)
            pe.wait_ge(a_ld, 16 * 2 * H)
            for k in range(KD):
                for b in range(KD):
                    ins = pe.matmul(PS[7][:, k * 2 * H:(k + 1) * 2 * H], WR[:, b, k * P:(k + 1) * P], AB[:, b, :],
                                    start=(b == 0), stop=(b == KD - 1))
            ins.then_inc(wa_ps, 1)
            pe.wait_ge(wa_sb, 1)
            with pe.Fori(0, NG) as g:
                pe.wait_ge(xt_sb, ONE + g * GT)
                for j in range(GT):
                    pe.wait_ge(xs_ready, g * GT + j + 1)
                    for k in range(KD):
                        ins = pe.transpose(PS[j][:, k * P:(k + 1) * P], m.XS[:, j, k * P:(k + 1) * P], m.ident[:, :])
                    ins.then_inc(xt_ps, 1)
                pe.wait_ge(h_sb, ONE + g * GT)
                for j in range(GT):
                    pe.wait_ge(xt_sb, ONE + g * GT + j + 1)
                    for k in range(KD):
                        pe.matmul(PS[2 + j][:, 0:2 * H], m.XT[:, k, j * P:(j + 1) * P], WA[:, k, :],
                                  start=(k == 0), stop=(k == KD - 1))
                    for k in range(KD):
                        ins = pe.matmul(PS[4 + j][:, :], m.XT[:, k, j * P:(j + 1) * P], WT[:, k, :],
                                        start=(k == 0), stop=(k == KD - 1))
                    ins.then_inc(h_ps, 1)


FIELDS = ("src", "dst", "edge_type_4", "edge_type_8", "edge_weight")


def edge_arrays(m):
    top = m.arena[:, m.arena_words - 12 * CP:]
    EDG = top.rearrange("p (n c) -> p n c", n=12)
    return EDG, [EDG[:, n, :].bitcast(I32) for n in range(4)] + [EDG[:, 4, :]], EDG[:, 10, :].bitcast(I32), EDG[:, 11, :]


def load_edges(nc, m):
    t, PS, sem = m.t, m.PS, m.sem
    EDG, fields, next_i, down = edge_arrays(m)
    m.flag = m.sb("flag", [P, 1], I32)
    down_n = m.sb("down_n", [P, 1])
    init, e_ld, down_ready, down_ps = (sem("s2a_" + n) for n in ("init", "e_ld", "down_ready", "down_ps"))

    with nc.Block() as block:
        @block.gpsimd
        def _(pool):
            pool.memset(EDG, 0.0)
            pool.drain()
            pool.memset(fields[1], PAD_DST)
            pool.memset(next_i, PAD_DST)
            pool.drain().then_inc(init, 1)

        @block.sync
        def _(sp):
            sp.wait_ge(init, 1)
            full = (P - 1) * C
            for dst, name in zip(fields, FIELDS):
                sp.dma_start(dst[0:P - 1, 0:C], t[name][0:full].rearrange("(p c) -> p c", c=C)).then_inc(e_ld, 16)
                sp.dma_start(dst[P - 1:P, 0:TAIL], t[name][full:E].unsqueeze(0)).then_inc(e_ld, 16)
            sp.dma_start(next_i[0:P - 1, 0:C], t["dst"][1:full + 1].rearrange("(p c) -> p c", c=C)).then_inc(e_ld, 16)
            sp.dma_start(next_i[P - 1:P, 0:TAIL - 1], t["dst"][full + 1:E].unsqueeze(0)).then_inc(e_ld, 16)
            sp.wait_ge(e_ld, 32 * (len(FIELDS) + 1))

        @block.vector
        def _(dve):
            dve.wait_ge(e_ld, 32 * (len(FIELDS) + 1))
            dve.tensor_tensor(down, next_i, fields[1], ALU.is_lt)
            dve.drain()
            dve.tensor_reduce(down_n[:, :], down[:, 0:C], AX.X, ALU.add)
            dve.drain().then_inc(down_ready, 1)
            dve.wait_ge(down_ps, 1)
            dve.tensor_copy(m.flag[:, :], PS[0][:, 0:1])
            dve.drain()

        @block.tensor
        def _(pe):
            pe.wait_ge(down_ready, 1)
            pe.matmul(PS[0][:, 0:1], m.ones[:, :], down_n[:, :], start=True, stop=True).then_inc(down_ps, 1)


def sort_edges(nc, m):
    PS, sem = m.PS, m.sem
    take = carver(m)
    EDG, fields, _, _ = edge_arrays(m)
    REC5 = take(C * 5).rearrange("p (c f) -> p c f", f=5)
    REC5_i = REC5.bitcast(I32)
    iota_n = take(NP)
    OHD = take(NP // 2).bitcast(BF16)
    prod = take(NP)
    starts = take(NP)
    rank, add, pos = take(CP), take(CP), take(CP)
    dst_f = take(CP)
    pos_i = take(CP).bitcast(I32)
    BEFORE = take(P // 2).bitcast(BF16)
    OTHERS = take(P // 2).bitcast(BF16)
    ZERO = take(P // 2).bitcast(BF16)
    ones_n = take(NP)
    idx1 = take(1).bitcast(I32)
    rec_1 = take(5)
    sorted5 = nc.dram_tensor("sorted5", [EP, 5], F32, kind="Internal").ap()
    ready, oh_ready, before_ps, rank_read, all_ps, pos_ready, staged, scattered, back = (sem("s2b_" + n) for n in (
        "ready", "oh_ready", "before_ps", "rank_read", "all_ps", "pos_ready", "staged", "scattered", "back"))
    SPAN = [(0, 512), (512, 1024), (1024, NP)]

    def out_of_order(eng):
        return eng.value_load(m.flag[0:1, 0:1], min_val=0, max_val=E)

    with nc.Block() as block:
        @block.vector
        def _(dve):
            with dve.If(out_of_order(dve) > 0):
                dve.wait_ge(ready, 1)
                dve.tensor_copy(dst_f, fields[1])
                for f in range(4):
                    dve.tensor_copy(REC5_i[:, :, f], fields[f][:, 0:C])
                dve.tensor_copy(REC5[:, :, 4], fields[4][:, 0:C])
                dve.tensor_scalar(BEFORE, m.iota_f[:, :], m.iota_k[:, 0:1], None, ALU.is_gt)
                dve.tensor_scalar(OTHERS, m.iota_f[:, :], m.iota_k[:, 0:1], None, ALU.is_le)
                dve.memset(ZERO, 0.0)
                dve.memset(ones_n, 1.0)
                dve.drain()
                dve.tensor_scalar(OHD, iota_n, dst_f[:, 0:1], None, ALU.is_equal)
                dve.drain().then_inc(oh_ready, 1)
                with dve.Fori(0, C) as c:
                    dve.wait_ge(before_ps, c + 1)
                    for b, (lo, hi) in enumerate(SPAN):
                        dve.tensor_tensor(prod[:, lo:hi], OHD[:, lo:hi], PS[b][:, 0:hi - lo], ALU.mult)
                    dve.drain()
                    dve.tensor_reduce(rank[:, bass.ds(c, 1)], prod, AX.X, ALU.add)
                    dve.drain().then_inc(rank_read, 1)
                    dve.wait_ge(all_ps, c + 1)
                    dve.tensor_scalar(OHD, iota_n, dst_f[:, bass.ds(c + 1, 1)], None, ALU.is_equal)
                    dve.drain().then_inc(oh_ready, 1)
                for b, (lo, hi) in enumerate(SPAN):
                    dve.tensor_copy(prod[:, lo:hi], PS[b][:, 0:hi - lo])
                dve.drain()
                dve.tensor_tensor_scan(starts, ones_n, prod, 0.0, ALU.mult, ALU.add)
                dve.drain()
                dve.tensor_tensor(starts, starts, prod, ALU.subtract)
                dve.drain()
                with dve.Fori(0, C) as c:
                    dve.tensor_scalar(OHD, iota_n, dst_f[:, bass.ds(c, 1)], None, ALU.is_equal)
                    dve.drain()
                    dve.tensor_tensor(prod, OHD, starts, ALU.mult)
                    dve.drain()
                    dve.tensor_reduce(add[:, bass.ds(c, 1)], prod, AX.X, ALU.add)
                    dve.drain()
                dve.tensor_tensor(pos_i[:, 0:C], rank[:, 0:C], add[:, 0:C], ALU.add)
                dve.drain().then_inc(pos_ready, 1)
                dve.wait_ge(back, 16)
                for f in range(4):
                    dve.tensor_copy(fields[f][:, 0:C], REC5_i[:, :, f])
                dve.tensor_copy(fields[4][:, 0:C], REC5[:, :, 4])
                dve.drain()

        @block.gpsimd
        def _(pool):
            with pool.If(out_of_order(pool) > 0):
                pool.iota(iota_n, [[1, NP]], base=0, channel_multiplier=0, allow_small_or_imprecise_dtypes=True)
                pool.drain().then_inc(ready, 1)
                pool.wait_ge(pos_ready, 1)
                with pool.Fori(0, C) as c:
                    pool.tensor_copy(idx1, pos_i[:, bass.ds(c, 1)])
                    pool.tensor_copy(rec_1, tile(REC5, c))
                    pool.drain().then_inc(staged, 1)
                    pool.wait_ge(staged, c + 1)
                    pool.sem_inc(pos_ready, 1)
                    pool.indirect_dma_start(sorted5, bass.IndirectOffsetOnAxis(ap=idx1, axis=0), rec_1, None).then_inc(scattered, 16)
                    pool.wait_ge(scattered, c * 16 + 16)
                pool.dma_start(REC5.rearrange("p c f -> p (c f)"), sorted5.rearrange("(p c) f -> p (c f)", c=C)).then_inc(back, 16)

        @block.tensor
        def _(pe):
            with pe.If(out_of_order(pe) > 0):
                pe.wait_ge(oh_ready, 1)
                for b, (lo, hi) in enumerate(SPAN):
                    pe.matmul(PS[b][:, 0:hi - lo], ZERO, OHD[:, lo:hi], start=True, stop=False, skip_group_check=True)
                with pe.Fori(0, C) as c:
                    pe.wait_ge(oh_ready, c + 1)
                    for b, (lo, hi) in enumerate(SPAN):
                        ins = pe.matmul(PS[b][:, 0:hi - lo], BEFORE, OHD[:, lo:hi], start=False, stop=False, skip_group_check=True)
                    ins.then_inc(before_ps, 1)
                    pe.wait_ge(rank_read, c + 1)
                    for b, (lo, hi) in enumerate(SPAN):
                        ins = pe.matmul(PS[b][:, 0:hi - lo], OTHERS, OHD[:, lo:hi], start=False, stop=False, skip_group_check=True)
                    ins.then_inc(all_ps, 1)


def edge_weights(nc, m):
    t, PS, sem = m.t, m.PS, m.sem
    NOT = 2 * NT
    OTS = 4
    take = carver(m)
    BC = take(2 * 2 * CG * P // 2).bitcast(F16).rearrange("p (r s e) -> p r s e", r=2, s=2)
    OT = take(OTS * CG * P // 2).bitcast(BF16).rearrange("p (r e) -> p r e", r=OTS)
    SC = take(H * CP).rearrange("p (h c) -> p h c", h=H)
    MUL = take(H * CP).rearrange("p (h c) -> p h c", h=H)
    FW = take(H * CP).rearrange("p (h c) -> p h c", h=H)
    EDG, (src_i, dst_i, t4_i, t8_i, ew), _, _ = edge_arrays(m)
    src_f, dst_f, t8_f, mask, same = (EDG[:, n, :] for n in range(5, 10))
    REC0 = take(C * R0).rearrange("p (c r) -> p c r", r=R0)
    REC1 = take(C * R1).rearrange("p (c r) -> p c r", r=R1)
    emb = take(NTYPE * H)
    cp16 = take(2 * 3 * P // 2).bitcast(F16).rearrange("p (s b e) -> p s b e", s=2, b=3)
    cnt, tot, sst = take(NT + 1), take(NT + 1), take(NT + 1)
    nst, nst_i, adj, dadj = take(NT), take(NT).bitcast(I32), take(NT), take(NT)
    iota_s, stmp, off_f = take(STEPS), take(STEPS), take(STEPS)
    lv_in = take(4 * H).rearrange("p (n h) -> p n h", n=4)
    lv = take(4 * 2 * P).rearrange("p (n e s) -> p n e s", n=4, e=P)
    lv_same = take(2 * P + 1)[0:H, :]
    g_first, g_last = take(H), take(H)
    tail = take(CJ * R0).rearrange("p (c r) -> p c r", r=R0)

    tails, e_ld, e_ready, cp_ps, cp_sb, cp_dr, tot_ps = (sem("s2_" + n) for n in (
        "tails", "e_ld", "e_ready", "cp_ps", "cp_sb", "cp_dr", "tot_ps"))
    bc_ld = [sem(f"s2_bc_ld{i}") for i in range(2)]
    bc_free, ot_ready, ot_free, sc_free = (sem("s2_" + n) for n in ("bc_free", "ot_ready", "ot_free", "sc_free"))
    lv_ready, lv_ps, lv_done, gb_ps, diff, rec_ready, rec_dr = (sem("s2_" + n) for n in (
        "lv_ready", "lv_ps", "lv_done", "gb_ps", "diff", "rec_ready", "rec_dr"))

    with nc.Block() as block:
        @block.sync
        def _(sp):
            sp.dma_start(emb, t["L0_gnn_et_emb"].rearrange("t h -> (t h)").partition_broadcast(P)).then_inc(e_ld, 16)
            sp.wait_ge(cp_sb, 2)
            for s, cp in enumerate((m.src_cp, m.dst_cp)):
                sp.dma_start(cp[0:2 * P, :].rearrange("(b c) p -> c b p", c=P), cp16[:, s, 0:2, :]).then_inc(cp_dr, 16)
                sp.dma_start(cp[2 * P:CP, :], cp16[0:CP - 2 * P, s, 2, :]).then_inc(cp_dr, 16)
            sp.wait_ge(cp_dr, 64)
            with sp.Fori(0, NCG // 2) as i:
                for r in range(2):
                    sp.wait_ge(bc_free, i * 2 + r + 1)
                    for s, cp in enumerate((m.src_cp, m.dst_cp)):
                        sp.dma_start(BC[:, r, s, :], cp[bass.ds((i * 2 + r) * CG, CG), :].rearrange("c p -> (c p)").partition_broadcast(P)).then_inc(bc_ld[r], 16)
            sp.wait_ge(rec_ready, 1)
            sp.dma_start(m.rec0[0:EP, :].rearrange("(p c) r -> p (c r)", c=C), REC0.rearrange("p c r -> p (c r)")).then_inc(rec_dr, 16)
            sp.dma_start(m.rec1[0:EP, :].rearrange("(p c) r -> p (c r)", c=C), REC1.rearrange("p c r -> p (c r)")).then_inc(rec_dr, 16)
            sp.wait_ge(tails, 1)
            sp.dma_start(m.rec0[EP:EP + CHUNK, :].rearrange("(p c) r -> p c r", c=CJ), tail).then_inc(rec_dr, 16)
            sp.dma_start(m.rec1[EP:EP + CHUNK, :].rearrange("(p c) r -> p c r", c=CJ), tail[:, :, 0:R1]).then_inc(rec_dr, 16)
            sp.wait_ge(rec_dr, 64)

        @block.gpsimd
        def _(pool):
            pool.memset(tail, 0.0)
            pool.memset(cp16, 0.0)
            pool.iota(iota_s, [[1, STEPS]], base=0, channel_multiplier=0, allow_small_or_imprecise_dtypes=True)
            pool.drain()
            pool.memset(tail[:, :, 1:2], -1.0).then_inc(tails, 1)

        @block.vector
        def _(dve):
            dve.sem_inc(bc_free, 2)
            dve.sem_inc(sc_free, 2)
            dve.wait_ge(e_ld, 16)
            dve.wait_ge(tails, 1)
            dve.tensor_copy(src_f, src_i)
            dve.tensor_copy(dst_f, dst_i)
            dve.tensor_copy(t8_f, t8_i)
            dve.memset(MUL, 0.0)
            dve.memset(cnt[:, 0:1], 0.0)
            dve.tensor_scalar(emb, emb, 1.0, None, ALU.add)
            dve.drain()
            for w in range(1, NT + 1):
                dve.tensor_scalar(mask[:, 0:C], dst_f[:, 0:C], float(P * w), 0.0, ALU.is_lt, ALU.add, accum_out=cnt[:, w:w + 1])
                dve.drain()
            dve.drain().then_inc(e_ready, 1)
            dve.scalar_tensor_tensor(REC1[:, :, 0].bitcast(I32), src_f[:, 0:C], float(NREL), t4_i[:, 0:C], ALU.mult, ALU.add)
            dve.tensor_copy(REC1[:, :, 1], dst_f[:, 0:C])
            dve.tensor_copy(REC0[:, :, 0].bitcast(I32), src_i[:, 0:C])
            dve.tensor_copy(REC0[:, :, 1], dst_f[:, 0:C])
            dve.memset(REC0[:, :, R0 - 1], 1.0)
            dve.memset(same[:, 0:1], 1.0)
            dve.tensor_tensor(same[:, 1:C], dst_f[:, 1:C], dst_f[:, 0:C - 1], ALU.is_equal)
            dve.memset(same[:, C:C + 1], 1.0)
            for s in range(2):
                dve.wait_ge(cp_ps, s + 1)
                dve.tensor_copy(cp16[:, s, 0:2, :], PS[s][:, 0:2 * P].rearrange("p (b c) -> p b c", b=2))
                dve.tensor_copy(cp16[0:C - 2 * P, s, 2, :], PS[s][0:C - 2 * P, 2 * P:3 * P])
                dve.drain().then_inc(cp_sb, 1)
            for ty in range(NTYPE):
                dve.tensor_scalar(mask, t8_f, float(ty), None, ALU.is_equal)
                dve.drain()
                for h in range(H):
                    dve.scalar_tensor_tensor(MUL[:, h, :], mask, emb[:, ty * H + h:ty * H + h + 1], MUL[:, h, :], ALU.mult, ALU.add)
                dve.drain()
            for h in range(H):
                dve.tensor_tensor(MUL[:, h, :], MUL[:, h, :], ew, ALU.mult)
            dve.wait_ge(tot_ps, 1)
            dve.tensor_copy(tot, PS[2][:, 0:NT + 1])
            dve.drain()
            dve.tensor_tensor(nst, tot[:, 1:NT + 1], tot[:, 0:NT], ALU.subtract)
            dve.drain()
            dve.tensor_scalar(nst_i, nst, float(CHUNK - 1), None, ALU.add)
            dve.drain()
            dve.tensor_scalar(nst_i, nst_i, CHUNK.bit_length() - 1, None, ALU.arith_shift_right)
            dve.drain()
            dve.tensor_copy(nst, nst_i)
            dve.memset(sst, 0.0)
            dve.drain()
            for w in range(NT):
                dve.tensor_tensor(sst[:, w + 1:w + 2], sst[:, w:w + 1], nst[:, w:w + 1], ALU.add)
                dve.drain()
            dve.scalar_tensor_tensor(adj, sst[:, 0:NT], -float(CHUNK), tot[:, 0:NT], ALU.mult, ALU.add)
            dve.drain()
            dve.tensor_tensor(dadj[:, 1:NT], adj[:, 1:NT], adj[:, 0:NT - 1], ALU.subtract)
            dve.tensor_scalar(off_f, iota_s, float(CHUNK), None, ALU.mult)
            dve.memset(m.woff[:, :], 0.0)
            dve.drain()
            for w in range(1, NT):
                dve.tensor_scalar(stmp, iota_s, sst[:, w:w + 1], None, ALU.is_ge)
                dve.drain()
                dve.scalar_tensor_tensor(off_f, stmp, dadj[:, w:w + 1], off_f, ALU.mult, ALU.add)
                dve.tensor_tensor(m.woff[:, :], m.woff[:, :], stmp, ALU.add)
                dve.drain()
            dve.tensor_scalar(m.step_off[:, :], off_f, float(EP), None, ALU.min)
            dve.tensor_copy(m.step_win[:, :], m.woff[:, :])
            dve.drain()
            dve.tensor_scalar(m.woff[:, :], m.woff[:, :], float(P), None, ALU.mult)
            with dve.Fori(0, NCG // 2) as i:
                for r in range(2):
                    dve.wait_ge(bc_ld[r], i * 32 + 32)
                    for s in range(2):
                        for k in range(NT):
                            n = s * NT + k
                            dve.wait_ge(ot_free, (i * 2 + r) * NOT + n + 1)
                            dve.tensor_scalar(OT[:, n % OTS, :], BC[:, r, s, :], m.iota_k[:, k:k + 1], None, ALU.is_equal).then_inc(ot_ready, 1)
                    dve.drain().then_inc(bc_free, 1)
                    dve.wait_ge(ot_free, OTS + (i * 2 + r + 1) * NOT)
                    dve.tensor_reduce(SC[:, :, bass.ds((i * 2 + r) * CG, CG)].rearrange("p h c -> p c h"),
                                      PS[4 + r][:, 0:CG * PARTS * H].rearrange("p (c b h) -> p c h b", c=CG, b=PARTS),
                                      AX.X, ALU.add).then_inc(sc_free, 1)
            dve.drain()
            dve.scalar_tensor_tensor(SC, SC, NEG_SLOPE, SC, ALU.mult, ALU.max)
            dve.drain()
            dve.tensor_tensor(SC, SC, MUL, ALU.mult)
            dve.drain()

            def segment_max(first, last):
                for h in range(H):
                    dve.tensor_tensor_scan(FW[:, h, 0:C], same[:, 0:C], SC[:, h, 0:C], first(h), ALU.mult, ALU.max)
                dve.drain()
                for h in range(H):
                    dve.tensor_tensor_scan(MUL[:, h, 0:C][:, ::-1], same[:, 1:C + 1][:, ::-1], FW[:, h, 0:C][:, ::-1],
                                           last(h), ALU.mult, ALU.max)
                dve.drain()

            segment_max(lambda h: 0.0, lambda h: 0.0)
            dve.tensor_copy(lv_in[:, 0, :], MUL[:, :, 0])
            dve.tensor_copy(lv_in[:, 1, :], FW[:, :, C - 1])
            dve.tensor_copy(lv_in[:, 2, :], dst_f[:, 0:1].to_broadcast((P, H)))
            dve.tensor_copy(lv_in[:, 3, :], dst_f[:, C - 1:C].to_broadcast((P, H)))
            dve.memset(lv_same, 0.0)
            dve.drain().then_inc(lv_ready, 1)
            dve.wait_ge(lv_ps, 1)
            for n in range(4):
                dve.tensor_copy(lv[0:H, n // 2, :, n % 2], PS[3][0:H, n * P:(n + 1) * P])
            dve.drain()
            val, key, fwd, bwd = (lv[0:H, n, :, :].rearrange("h e s -> h (e s)") for n in range(4))
            dve.tensor_tensor(lv_same[:, 1:2 * P], key[:, 1:2 * P], key[:, 0:2 * P - 1], ALU.is_equal)
            dve.drain()
            dve.tensor_tensor_scan(fwd, lv_same[:, 0:2 * P], val, 0.0, ALU.mult, ALU.max)
            dve.drain()
            dve.tensor_tensor_scan(bwd[:, ::-1], lv_same[:, 1:2 * P + 1][:, ::-1], fwd[:, ::-1], 0.0, ALU.mult, ALU.max).then_inc(lv_done, 1)
            dve.wait_ge(gb_ps, 1)
            dve.tensor_copy(g_first, PS[2][:, 0:H])
            dve.tensor_copy(g_last, PS[2][:, H:2 * H])
            dve.drain()
            segment_max(lambda h: g_first[:, h:h + 1], lambda h: g_last[:, h:h + 1])
            dve.tensor_tensor(FW, SC, MUL, ALU.subtract)
            dve.drain().then_inc(diff, 1)

        @block.scalar
        def _(act):
            act.wait_ge(diff, 1)
            act.activation(REC0[:, :, 2:2 + H].rearrange("p c h -> p h c"), FW[:, :, 0:C], ACT.Exp).then_inc(rec_ready, 1)

        @block.tensor
        def _(pe):
            pe.sem_inc(ot_free, OTS)
            pe.wait_ge(e_ready, 1)
            for s, v in enumerate((src_f, dst_f)):
                for b in range(3):
                    n = min(P, C - b * P)
                    ins = pe.transpose(PS[s][0:n, b * P:(b + 1) * P], v[:, b * P:b * P + n], m.ident[:, :])
                ins.then_inc(cp_ps, 1)
            pe.matmul(PS[2][:, 0:NT + 1], m.ones[:, :], cnt, start=True, stop=True).then_inc(tot_ps, 1)
            with pe.Fori(0, NCG // 2) as i:
                for r in range(2):
                    pe.wait_ge(sc_free, i * 2 + r + 1)
                    for n in range(NOT):
                        pe.wait_ge(ot_ready, (i * 2 + r) * NOT + n + 1)
                        for c in range(CG):
                            ins = pe.matmul(PS[4 + r][:, c * PARTS * H:(c + 1) * PARTS * H], OT[:, n % OTS, c * P:(c + 1) * P],
                                            m.TAB[:, n // NT, n % NT, :, :].rearrange("p b h -> p (b h)"),
                                            start=(n == 0 and c == 0), stop=(n == NOT - 1), skip_group_check=True)
                        ins.then_inc(ot_free, 1)
            pe.wait_ge(lv_ready, 1)
            for n in range(4):
                ins = pe.transpose(PS[3][0:H, n * P:(n + 1) * P], lv_in[:, n, :], m.ident[:, :])
            ins.then_inc(lv_ps, 1)
            pe.wait_ge(lv_done, 1)
            for n in range(2):
                ins = pe.transpose(PS[2][:, n * H:(n + 1) * H], lv[0:H, 3, :, n], m.ident[0:H, 0:H])
            ins.then_inc(gb_ps, 1)


def messages(nc, m, tag, rec, R, table, weighted, load_next):
    PS, sem = m.PS, m.sem
    take = carver(m, WBYTES // 4)
    G = take(RING * CJ * D).rearrange("p (r j d) -> p r j d", r=RING, j=CJ)
    OH = take(RING * CJ * P).rearrange("p (r j d) -> p r j d", r=RING, j=CJ)
    RC = take(RING * CJ * R).rearrange("p (r j c) -> p r j c", r=RING, j=CJ)
    DR = take(RING * CJ).rearrange("p (r j) -> p r j", r=RING)
    rec_ld = [sem(f"{tag}_rec_ld{i}") for i in range(RING)]
    g_ld = [sem(f"{tag}_g_ld{i}") for i in range(RING)]
    msg_ready, slot_free, oh_ready, ps_free = (sem(f"{tag}_{n}") for n in ("msg_ready", "slot_free", "oh_ready", "ps_free"))
    next_ld = sem(f"{tag}_next_ld")
    gather_steps = sem(f"{tag}_gather_steps")
    ROUNDS = STEPS // RING
    assert STEPS % RING == 0

    with nc.Block() as block:
        @block.sync
        def _(sp):
            with sp.Fori(0, ROUNDS) as i:
                for r in range(RING):
                    off = sp.value_load(m.step_off[0:1, bass.ds(i * RING + r, 1)], min_val=0, max_val=EP)
                    sp.wait_ge(slot_free, i * RING + r + 1)
                    sp.dma_start(RC[:, r, :, :].rearrange("p j c -> p (j c)"),
                                 rec[bass.ds(off, CHUNK), :].rearrange("(p j) c -> p (j c)", j=CJ)).then_inc(rec_ld[r], 16)

        @block.gpsimd
        def _(pool):
            with pool.Fori(0, ROUNDS) as i:
                for r in range(RING):
                    pool.wait_ge(rec_ld[r], i * 16 + 16)
                    pool.sem_inc(gather_steps, 1)
                    for j in range(CJ):
                        pool.indirect_dma_start(G[:, r, j, :], None, table,
                                                bass.IndirectOffsetOnAxis(ap=RC[:, r, j, 0:1].bitcast(I32), axis=0)).then_inc(g_ld[r], 16)

        @block.vector
        def _(dve):
            def front(i, r):
                dve.wait_ge(slot_free, i * RING + r + 1)
                dve.wait_ge(rec_ld[r], i * 16 + 16)
                dve.tensor_scalar(DR[:, r, :], RC[:, r, :, 1], m.woff[:, bass.ds(i * RING + r, 1)], None, ALU.subtract)
                dve.drain()
                dve.tensor_tensor(OH[:, r, :, :], m.iota_f[:, :].unsqueeze(1).to_broadcast((P, CJ, P)),
                                  DR[:, r, :].unsqueeze(2).to_broadcast((P, CJ, P)), ALU.is_equal).then_inc(oh_ready, 1)
                if weighted:
                    dve.wait_ge(g_ld[r], i * 16 * CJ + 16 * CJ)
                    g = G[:, r, :, :].rearrange("p j (h d) -> p j h d", h=H)
                    dve.tensor_tensor(g, g, RC[:, r, :, 2:2 + H].unsqueeze(3).to_broadcast((P, CJ, H, HD)), ALU.mult).then_inc(msg_ready, 1)

            def back(i, r):
                win = dve.value_load(m.step_win[0:1, bass.ds(i * RING + r, 1)], min_val=0, max_val=NT - 1)
                dve.wait_ge(slot_free, i * RING + r + RING + 1)
                dve.tensor_tensor(tile(m.ACC, win), tile(m.ACC, win), PS[r][:, :], ALU.add)
                if weighted:
                    dve.tensor_tensor(tile(m.ASUM, win), tile(m.ASUM, win), PS[RING + r][:, 0:H + 1], ALU.add)
                dve.drain().then_inc(ps_free, 1)

            LAG = 2
            dve.sem_inc(ps_free, RING)
            for r in range(LAG):
                front(0, r)
            with dve.Fori(0, ROUNDS - 1) as i:
                for r in range(RING):
                    front(i + (r + LAG) // RING, (r + LAG) % RING)
                    back(i, r)
            for r in range(RING):
                if r + LAG < RING:
                    front(ROUNDS - 1, r + LAG)
                back(ROUNDS - 1, r)

        @block.scalar
        def _(act):
            load_next(m, act, next_ld)

        @block.tensor
        def _(pe):
            pe.sem_inc(slot_free, RING)
            with pe.Fori(0, ROUNDS) as i:
                for r in range(RING):
                    pe.wait_ge(oh_ready, i * RING + r + 1)
                    if weighted:
                        pe.wait_ge(msg_ready, i * RING + r + 1)
                    else:
                        pe.wait_ge(g_ld[r], i * 16 * CJ + 16 * CJ)
                    pe.wait_ge(ps_free, i * RING + r + 1)
                    for j in range(CJ):
                        if weighted:
                            pe.matmul(PS[RING + r][:, 0:H + 1], OH[:, r, j, :], RC[:, r, j, 2:R], start=(j == 0), stop=(j == CJ - 1))
                        ins = pe.matmul(PS[r][:, :], OH[:, r, j, :], G[:, r, j, :], start=(j == 0), stop=(j == CJ - 1))
                    ins.then_inc(slot_free, 1)


class Norms:

    def __init__(self, m, tag):
        self.m = m
        self.var_ready, self.sd_ready = m.sem(tag + "_var_ready"), m.sem(tag + "_sd_ready")

    def stats(self, dve, n, tiles):
        m = self.m
        for j, x in enumerate(tiles):
            dve.bn_stats(m.stats[:, j, :], x)
        dve.drain()
        for j in range(len(tiles)):
            dve.bn_aggr(m.mv[:, j, :], m.stats[:, j, :])
        dve.drain().then_inc(self.var_ready, 1)
        dve.wait_ge(self.sd_ready, n + 1)
        dve.reciprocal(m.rstd[:, 0:GT], m.sd[:, 0:GT])
        dve.drain()

    def apply(self, dve, out, x):
        m = self.m
        for j in range(len(x)):
            dve.tensor_scalar(out[j], x[j], m.mv[:, j, 0:1], m.rstd[:, j:j + 1], ALU.subtract, ALU.mult)
        dve.drain()

    def root(self, act, n):
        m = self.m
        act.wait_ge(self.var_ready, n + 1)
        act.activation(m.sd[:, 0:GT], m.mv[:, 0:GT, 1], ACT.Sqrt, bias=m.eps[:, 0:1]).then_inc(self.sd_ready, 1)


def affine(dve, x, scale, shift):
    for a in x:
        dve.tensor_tensor(a, a, scale, ALU.mult)
    dve.drain()
    for a in x:
        dve.tensor_tensor(a, a, shift, ALU.add)
    dve.drain()


def expert_weights(m):
    take = carver(m)
    W1 = take(KD * NEXP * HID).rearrange("p (k n) -> p k n", k=KD)
    W2 = take(NEXP * HID // P * D).rearrange("p (k n) -> p k n", n=D)
    return W1, W2


def load_experts(m, eng, s):
    W1, W2 = expert_weights(m)
    for k in range(KD):
        eng.dma_start(W1[:, k, :].rearrange("p (e h) -> p e h", e=NEXP),
                      m.t["L0_ffn_W1"].rearrange("e (k p) h -> k p e h", p=P)[k]).then_inc(s, 16)
    eng.dma_start(W2, m.t["L0_ffn_W2"].rearrange("e (k p) n -> p (e k) n", p=P)).then_inc(s, 16)
    eng.wait_ge(s, 16 * (KD + 1))


def experts(nc, m):
    t, PS, sem = m.t, m.PS, m.sem
    MH = HID // P
    W1, W2 = expert_weights(m)
    take = carver(m, WBYTES // 4)
    HS = take(2 * MH * W2N).rearrange("p (r b n) -> p r b n", r=2, b=MH)
    WG = take(KD * NEXP).rearrange("p (k e) -> p k e", k=KD)
    B1 = take(NEXP * MH)
    B2 = take(D)[0:NEXP, :]
    O = take(GT * D).rearrange("p (j d) -> p j d", j=GT)
    lg = take(GT * NEXP).rearrange("p (j e) -> p j e", j=GT)
    pr = take(GT * NEXP).rearrange("p (j e) -> p j e", j=GT)
    top = take(GT * NEXP).rearrange("p (j e) -> p j e", j=GT)
    top_i = take(GT * NEXP).bitcast(U32).rearrange("p (j e) -> p j e", j=GT)
    idx = take(GT * NEXP).rearrange("p (j e) -> p j e", j=GT)
    hot = take(GT * NEXP).rearrange("p (j e) -> p j e", j=GT)
    conf = take(GT * NEXP).rearrange("p (j e) -> p j e", j=GT)
    conf_t = take(W2N)[0:NEXP, :]
    red = take(GT * 4).rearrange("p (j e) -> p j e", j=GT)
    rs = take(GT * H).rearrange("p (j e) -> p j e", j=GT)

    ld, xs_ready, xt_ps, xt_sb, lg_ps, lg_ready, pr_ready, conf_ready, ct_ps, ct_sb = (sem("s4_" + n) for n in (
        "ld", "xs_ready", "xt_ps", "xt_sb", "lg_ps", "lg_ready", "pr_ready", "conf_ready", "ct_ps", "ct_sb"))
    h_ps, h_sb, o_ps, o_used = (sem("s4_" + n) for n in ("h_ps", "h_sb", "o_ps", "o_used"))
    norms = Norms(m, "s4")
    PO = NEXP + 1

    with nc.Block() as block:
        @block.sync
        def _(sp):
            sp.dma_start(WG, t["L0_ffn_Wg"].rearrange("(k p) e -> p k e", p=P)).then_inc(ld, 16)
            sp.dma_start(B1, t["L0_ffn_b1_cols"]).then_inc(ld, 16)
            sp.dma_start(B2, t["L0_ffn_b2"]).then_inc(ld, 16)
            sp.wait_ge(ld, 48)

        FRONT = 3
        AFTER = (1, 3, 5)

        @block.vector
        def _(dve):
            dve.sem_inc(o_used, ONE)

            def tiles(b, g):
                return [tile(b, g * GT + j) for j in range(GT)]

            def front(g, part, n):
                A, R, X = tiles(m.ACC, g), tiles(m.RES, g), tiles(m.X, g)
                U, S = ([b[:, j, :] for j in range(GT)] for b in (m.U, m.XS))
                if part == 0:
                    for j in range(GT):
                        dve.tensor_scalar(rs[:, j, :], tile(m.ASUM, g * GT + j)[:, 0:H], 1e-10, None, ALU.add)
                    dve.drain()
                    dve.reciprocal(rs, rs)
                    dve.drain()
                    for j in range(GT):
                        a = A[j].rearrange("p (h d) -> p h d", h=H)
                        dve.tensor_tensor(a, a, over_heads(rs[:, j, :]), ALU.mult)
                    dve.drain()
                    for j in range(GT):
                        dve.tensor_tensor(A[j], A[j], R[j], ALU.add)
                    dve.drain()
                    norms.stats(dve, n, A)
                    norms.apply(dve, A, A)
                elif part == 1:
                    affine(dve, A, m.rows["L0_gnn_ln_gamma"], m.rows["L0_gnn_ln_beta"])
                    for j in range(GT):
                        dve.tensor_tensor(X[j], X[j], A[j], ALU.add)
                    dve.drain()
                    norms.stats(dve, n, X)
                    norms.apply(dve, U, X)
                else:
                    norms.stats(dve, n, U)
                    norms.apply(dve, S, U)
                    affine(dve, S, m.rows["L0_ffn_ln_g"], m.rows["L0_ffn_ln_b"])
                    dve.drain().then_inc(xs_ready, 1)

            def route(g):
                dve.wait_ge(lg_ps, g + 1)
                dve.tensor_reduce(red[:, :, 0:1], PS[0][:, 0:GT * NEXP].rearrange("p (j e) -> p j e", j=GT), AX.X, ALU.max)
                dve.drain()
                dve.tensor_tensor(lg, PS[0][:, 0:GT * NEXP].rearrange("p (j e) -> p j e", j=GT),
                                  red[:, :, 0:1].to_broadcast((P, GT, NEXP)), ALU.subtract)
                dve.drain().then_inc(lg_ready, 1)
                dve.wait_ge(pr_ready, g + 1)
                dve.tensor_reduce(red[:, :, 1:2], pr, AX.X, ALU.add)
                dve.drain()
                dve.reciprocal(red[:, :, 2:3], red[:, :, 1:2])
                dve.drain()
                dve.tensor_tensor(pr, pr, red[:, :, 2:3].to_broadcast((P, GT, NEXP)), ALU.mult)
                dve.drain()
                for j in range(GT):
                    dve.max(top[:, j, :], pr[:, j, :])
                dve.drain()
                for j in range(GT):
                    dve.max_index(top_i[:, j, :], top[:, j, :], pr[:, j, :])
                dve.tensor_reduce(red[:, :, 0:1], top[:, :, 0:2], AX.X, ALU.add)
                dve.drain()
                dve.reciprocal(red[:, :, 1:2], red[:, :, 0:1])
                dve.tensor_copy(idx, top_i)
                dve.drain()
                dve.tensor_tensor(top[:, :, 0:2], top[:, :, 0:2], red[:, :, 1:2].to_broadcast((P, GT, 2)), ALU.mult)
                dve.drain()
                for j in range(GT):
                    dve.tensor_scalar(conf[:, j, :], m.iota_f[:, 0:NEXP], idx[:, j, 0:1], top[:, j, 0:1], ALU.is_equal, ALU.mult)
                    dve.tensor_scalar(hot[:, j, :], m.iota_f[:, 0:NEXP], idx[:, j, 1:2], top[:, j, 1:2], ALU.is_equal, ALU.mult)
                dve.drain()
                dve.tensor_tensor(conf, conf, hot, ALU.add)
                dve.drain().then_inc(conf_ready, 1)
                dve.wait_ge(ct_ps, g + 1)
                dve.tensor_copy(conf_t, PS[1][0:NEXP, 0:W2N]).then_inc(ct_sb, 1)

            def group(g, n, last):
                route(g)
                out = [O[:, j, :] for j in range(GT)]
                for e in range(PO):
                    dve.wait_ge(o_ps, ONE + g * PO + e + 1)
                    for j in range(GT):
                        ps = PS[4 + 2 * (e % 2) + j][:, :]
                        if e < NEXP:
                            dve.scalar_tensor_tensor(out[j], ps, conf[:, j, e:e + 1], m.U[:, j, :] if e == 0 else out[j], ALU.mult, ALU.add)
                        else:
                            dve.tensor_tensor(out[j], out[j], ps, ALU.add)
                    dve.drain().then_inc(o_used, 1)
                    if e in AFTER and not last:
                        front(g + 1, AFTER.index(e), n + AFTER.index(e))
                norms.stats(dve, n + (0 if last else FRONT), out)
                norms.apply(dve, out, out)
                affine(dve, out, m.rows["L0_ffn_out_g"], m.rows["L0_ffn_out_b"])
                for x, o in zip(tiles(m.X, g), out):
                    dve.tensor_tensor(x, x, o, ALU.add)
                dve.drain()

            for part in range(FRONT):
                front(0, part, part)
            with dve.Fori(0, NG - 1) as g:
                group(g, FRONT + g * (FRONT + 1), False)
            group(NG - 1, FRONT + (NG - 1) * (FRONT + 1), True)

        @block.scalar
        def _(act):
            act.sem_inc(h_sb, ONE)
            act.wait_ge(ld, 48)

            def group(g, n, last):
                act.wait_ge(xt_ps, ONE + g * GT + GT)
                for j in range(GT):
                    act.copy(m.XT[:, :, j * P:(j + 1) * P], PS[j][:, :].rearrange("p (k n) -> p k n", k=KD))
                act.drain().then_inc(xt_sb, 1)
                act.wait_ge(lg_ready, g + 1)
                act.activation(pr, lg, ACT.Exp).then_inc(pr_ready, 1)
                for e in range(NEXP):
                    act.wait_ge(h_ps, g * NEXP + e + 1)
                    act.wait_ge(o_ps, ONE + g * PO + max(e - 1, 0))
                    for b in range(MH):
                        act.activation(HS[:, e % 2, b, :], PS[2 + e % 2][:, b * W2N:(b + 1) * W2N], ACT.Gelu_apprx_tanh,
                                       bias=B1[:, e * MH + b:e * MH + b + 1])
                    act.drain().then_inc(h_sb, 1)
                    if e - 2 in AFTER and not last:
                        norms.root(act, n + AFTER.index(e - 2))
                norms.root(act, n + (0 if last else FRONT))

            for part in range(FRONT):
                norms.root(act, part)
            with act.Fori(0, NG - 1) as g:
                group(g, FRONT + g * (FRONT + 1), False)
            group(NG - 1, FRONT + (NG - 1) * (FRONT + 1), True)

        @block.tensor
        def _(pe):
            pe.sem_inc(xt_ps, ONE)
            pe.sem_inc(o_ps, ONE)
            pe.wait_ge(ld, 48)

            def transposes(g):
                pe.wait_ge(xs_ready, g + 1)
                for j in range(GT):
                    for k in range(KD):
                        ins = pe.transpose(PS[j][:, k * P:(k + 1) * P], m.XS[:, j, k * P:(k + 1) * P], m.ident[:, :])
                    ins.then_inc(xt_ps, 1)

            def hidden(g, e):
                pe.wait_ge(h_sb, ONE + g * NEXP + max(e - 1, 0))
                for b in range(MH):
                    for k in range(KD):
                        at = e * HID + b * P
                        ins = pe.matmul(PS[2 + e % 2][:, b * W2N:(b + 1) * W2N], W1[:, k, at:at + P], m.XT[:, k, :],
                                        start=(k == 0), stop=(k == KD - 1))
                ins.then_inc(h_ps, 1)

            def output(g, e):
                pe.wait_ge(h_sb, ONE + g * NEXP + e + 1)
                pe.wait_ge(o_used, ONE + g * PO + max(e - 1, 0))
                for j in range(GT):
                    for b in range(MH):
                        ins = pe.matmul(PS[4 + 2 * (e % 2) + j][:, :], HS[:, e % 2, b, j * P:(j + 1) * P], W2[:, e * MH + b, :],
                                        start=(b == 0), stop=(b == MH - 1))
                ins.then_inc(o_ps, 1)

            def group(g, last):
                pe.wait_ge(xt_sb, g + 1)
                for j in range(GT):
                    for k in range(KD):
                        ins = pe.matmul(PS[0][:, j * NEXP:(j + 1) * NEXP], m.XT[:, k, j * P:(j + 1) * P], WG[:, k, :],
                                        start=(k == 0), stop=(k == KD - 1))
                ins.then_inc(lg_ps, 1)
                hidden(g, 0)
                for e in range(NEXP):
                    if e + 1 < NEXP:
                        hidden(g, e + 1)
                    if e == 1:
                        pe.wait_ge(conf_ready, g + 1)
                        for j in range(GT):
                            ins = pe.transpose(PS[1][0:NEXP, j * P:(j + 1) * P], conf[:, j, :], m.ident[:, :])
                        ins.then_inc(ct_ps, 1)
                    output(g, e)
                pe.wait_ge(ct_sb, g + 1)
                pe.wait_ge(o_used, ONE + g * PO + NEXP - 1)
                for j in range(GT):
                    ins = pe.matmul(PS[4 + j][:, :], conf_t[:, j * P:(j + 1) * P], B2, start=True, stop=True)
                ins.then_inc(o_ps, 1)
                if not last:
                    transposes(g + 1)

            transposes(0)
            with pe.Fori(0, NG - 1) as g:
                group(g, False)
            group(NG - 1, True)


def relations(nc, m):
    t, PS, sem = m.t, m.PS, m.sem
    take = carver(m)
    WR = take(KD * NREL * D).rearrange("p (k n) -> p k n", k=KD)
    WS = take(KD * D).rearrange("p (k n) -> p k n", k=KD)
    RB = take(NREL * D)
    STG = take(GT * NREL * D).rearrange("p (j n) -> p j n", j=GT)
    b_ld, xs_ready, xt_ps, xt_sb, ps_ready, ps_used, rows_dr = (sem("s5_" + n) for n in (
        "b_ld", "xs_ready", "xt_ps", "xt_sb", "ps_ready", "ps_used", "rows_dr"))
    norms = Norms(m, "s5")
    PJ = NREL + 1
    PB = 5
    w_ld = [sem(f"s5_w_ld{r}") for r in range(PJ)]

    with nc.Block() as block:
        @block.sync
        def _(sp):
            sp.sem_inc(rows_dr, ONE)
            for r in range(NREL):
                sp.dma_start(WR[:, :, r * D:(r + 1) * D], t["L1_gnn_rel_W"][r].rearrange("(k p) f -> p k f", p=P)).then_inc(w_ld[r], 16)
                if r == 0:
                    sp.dma_start(RB, t["L1_gnn_rel_b"].rearrange("r f -> (r f)").partition_broadcast(P)).then_inc(b_ld, 16)
            sp.dma_start(WS, t["L1_gnn_self_W"].rearrange("(k p) f -> p k f", p=P)).then_inc(w_ld[NREL], 16)
            with sp.Fori(0, NG) as g:
                for j in range(GT):
                    sp.wait_ge(ps_used, ONE + (g * GT + j + 1) * PJ)
                    sp.dma_start(m.rel_rows[bass.ds((g * GT + j) * P * NREL, P * NREL), :].rearrange("(p r) f -> p (r f)", r=NREL),
                                 STG[:, j, :]).then_inc(rows_dr, 16)
            sp.wait_ge(rows_dr, ONE + 16 * NT)

        @block.vector
        def _(dve):
            dve.sem_inc(ps_used, ONE)

            def front(g):
                X = [tile(m.X, g * GT + j) for j in range(GT)]
                norms.stats(dve, g, X)
                norms.apply(dve, [m.XS[:, j, :] for j in range(GT)], X)
                dve.drain().then_inc(xs_ready, 1)
                for j in range(GT):
                    dve.tensor_tensor(tile(m.RES, g * GT + j), m.XS[:, j, :], m.rows["L1_gnn_self_b"], ALU.add)
                dve.drain()

            def group(g, last):
                for j in range(GT):
                    dve.wait_ge(rows_dr, ONE + g * 16 * GT)
                    for r in range(PJ):
                        n = j * PJ + r
                        dve.wait_ge(ps_ready, ONE + g * GT * PJ + n + 1)
                        ps = PS[2 + n % PB][:, :]
                        if r < NREL:
                            dve.tensor_tensor(STG[:, j, r * D:(r + 1) * D], ps, RB[:, r * D:(r + 1) * D], ALU.add).then_inc(ps_used, 1)
                        else:
                            dve.tensor_tensor(tile(m.RES, g * GT + j), tile(m.RES, g * GT + j), ps, ALU.add).then_inc(ps_used, 1)
                    if j == 0 and not last:
                        front(g + 1)

            front(0)
            dve.memset(m.ACC[:, :, :], 0.0)
            dve.wait_ge(b_ld, 16)
            with dve.Fori(0, NG - 1) as g:
                group(g, False)
            group(NG - 1, True)

        @block.scalar
        def _(act):
            norms.root(act, 0)

            def group(g, last):
                act.wait_ge(xt_ps, g + 1)
                for j in range(GT):
                    act.copy(m.XT[:, :, j * P:(j + 1) * P], PS[j][:, :].rearrange("p (k n) -> p k n", k=KD))
                act.drain().then_inc(xt_sb, 1)
                if not last:
                    norms.root(act, g + 1)

            with act.Fori(0, NG - 1) as g:
                group(g, False)
            group(NG - 1, True)

        @block.tensor
        def _(pe):
            pe.sem_inc(ps_ready, ONE)

            def transposes(g):
                pe.wait_ge(xs_ready, g + 1)
                for j in range(GT):
                    for k in range(KD):
                        ins = pe.transpose(PS[j][:, k * P:(k + 1) * P], m.XS[:, j, k * P:(k + 1) * P], m.ident[:, :])
                ins.then_inc(xt_ps, 1)

            def group(g, last):
                pe.wait_ge(xt_sb, g + 1)
                for j in range(GT):
                    for r in range(PJ):
                        n = j * PJ + r
                        pe.wait_ge(w_ld[r], 16)
                        pe.wait_ge(ps_used, ONE + g * GT * PJ + max(n - PB + 1, 0))
                        for k in range(KD):
                            w = WR[:, k, r * D:(r + 1) * D] if r < NREL else WS[:, k, :]
                            ins = pe.matmul(PS[2 + n % PB][:, :], m.XT[:, k, j * P:(j + 1) * P], w, start=(k == 0), stop=(k == KD - 1))
                        ins.then_inc(ps_ready, 1)
                if not last:
                    transposes(g + 1)

            transposes(0)
            with pe.Fori(0, NG - 1) as g:
                group(g, False)
            group(NG - 1, True)


def ffn_weights(m):
    take = carver(m)
    W1 = take(KD * FF).rearrange("p (k n) -> p k n", k=KD)
    W2 = take(FF // P * D).rearrange("p (k n) -> p k n", n=D)
    return W1, W2


def load_ffn(m, eng, s):
    W1, W2 = ffn_weights(m)
    eng.dma_start(W1, m.t["L1_gnn_W1"].rearrange("(k p) n -> p k n", p=P)).then_inc(s, 16)
    eng.dma_start(W2, m.t["L1_gnn_W2"].rearrange("(k p) n -> p k n", p=P)).then_inc(s, 16)
    eng.wait_ge(s, 32)


def ffn(nc, m):
    t, PS, sem = m.t, m.PS, m.sem
    MB = 2
    NQ = FF // P // MB
    W1, W2 = ffn_weights(m)
    take = carver(m, WBYTES // 4)
    HS = take(2 * MB * W2N).rearrange("p (r b n) -> p r b n", r=2, b=MB)
    B1 = take(FF // P)
    deg = take(NT)
    Y = take(GT * D).rearrange("p (j d) -> p j d", j=GT)
    ld, xs_ready, xt_ps, xt_sb, h_ps, h_sb, o_ps, o_used = (sem("s7_" + n) for n in (
        "ld", "xs_ready", "xt_ps", "xt_sb", "h_ps", "h_sb", "o_ps", "o_used"))
    norms = Norms(m, "s7")

    with nc.Block() as block:
        @block.sync
        def _(sp):
            sp.dma_start(B1, t["L1_gnn_b1_cols"]).then_inc(ld, 16)
            sp.wait_ge(ld, 16)

        @block.vector
        def _(dve):
            dve.sem_inc(o_used, ONE)

            def front(g, n):
                S = [m.XS[:, j, :] for j in range(GT)]
                for j in range(GT):
                    dve.scalar_tensor_tensor(S[j], tile(m.ACC, g * GT + j), deg[:, bass.ds(g * GT + j, 1)], tile(m.RES, g * GT + j), ALU.mult, ALU.add)
                dve.drain()
                norms.stats(dve, n, S)
                norms.apply(dve, S, S)
                affine(dve, S, m.rows["L1_gnn_ln1_w"], m.rows["L1_gnn_ln1_b"])
                dve.drain().then_inc(xs_ready, 1)
                for j in range(GT):
                    dve.tensor_tensor(tile(m.RES, g * GT + j), S[j], m.rows["L1_gnn_b2"], ALU.add)
                dve.drain()

            def back(g, n):
                O = [Y[:, j, :] for j in range(GT)]
                dve.wait_ge(o_ps, g + 1)
                for j in range(GT):
                    dve.tensor_tensor(O[j], tile(m.RES, g * GT + j), PS[4 + j][:, :], ALU.add)
                dve.drain().then_inc(o_used, 1)
                norms.stats(dve, n, O)
                norms.apply(dve, O, O)
                affine(dve, O, m.rows["L1_gnn_ln2_w"], m.rows["L1_gnn_ln2_b"])
                for j in range(GT):
                    dve.tensor_tensor(tile(m.X, g * GT + j), tile(m.X, g * GT + j), O[j], ALU.add)
                dve.drain()

            dve.tensor_scalar(deg, m.ASUM[:, :, H], 1.0, None, ALU.max)
            dve.drain()
            dve.reciprocal(deg, deg)
            dve.drain()
            front(0, 0)
            with dve.Fori(0, NG - 1) as g:
                dve.wait_ge(xt_ps, g + 1)
                front(g + 1, g * 2 + 1)
                back(g, g * 2 + 2)
            back(NG - 1, NG * 2 - 1)

        @block.scalar
        def _(act):
            act.sem_inc(h_sb, ONE)
            act.wait_ge(ld, 16)

            def group(g, n, last):
                act.wait_ge(xt_ps, g + 1)
                for j in range(GT):
                    act.copy(m.XT[:, :, j * P:(j + 1) * P], PS[j][:, :].rearrange("p (k n) -> p k n", k=KD))
                act.drain().then_inc(xt_sb, 1)
                for q in range(NQ):
                    act.wait_ge(h_ps, g * NQ + q + 1)
                    for b in range(MB):
                        act.activation(HS[:, q % 2, b, :], PS[2 + q % 2][:, b * W2N:(b + 1) * W2N], ACT.Gelu,
                                       bias=B1[:, q * MB + b:q * MB + b + 1])
                    act.drain().then_inc(h_sb, 1)
                    if q == 0 and not last:
                        norms.root(act, n)
                norms.root(act, n + (0 if last else 1))

            norms.root(act, 0)
            with act.Fori(0, NG - 1) as g:
                group(g, g * 2 + 1, False)
            group(NG - 1, NG * 2 - 1, True)

        @block.tensor
        def _(pe):
            def transposes(g):
                pe.wait_ge(xs_ready, g + 1)
                for j in range(GT):
                    for k in range(KD):
                        ins = pe.transpose(PS[j][:, k * P:(k + 1) * P], m.XS[:, j, k * P:(k + 1) * P], m.ident[:, :])
                ins.then_inc(xt_ps, 1)

            def hidden(g, q):
                pe.wait_ge(h_sb, ONE + g * NQ + max(q - 1, 0))
                for b in range(MB):
                    at = (q * MB + b) * P
                    for k in range(KD):
                        ins = pe.matmul(PS[2 + q % 2][:, b * W2N:(b + 1) * W2N], W1[:, k, at:at + P], m.XT[:, k, :],
                                        start=(k == 0), stop=(k == KD - 1))
                ins.then_inc(h_ps, 1)

            def group(g, last):
                pe.wait_ge(xt_sb, g + 1)
                hidden(g, 0)
                hidden(g, 1)
                pe.wait_ge(o_used, ONE + g)
                for q in range(NQ):
                    pe.wait_ge(h_sb, ONE + g * NQ + q + 1)
                    for b in range(MB):
                        for j in range(GT):
                            ins = pe.matmul(PS[4 + j][:, :], HS[:, q % 2, b, j * P:(j + 1) * P], W2[:, q * MB + b, :],
                                            start=(q == 0 and b == 0), stop=(q == NQ - 1 and b == MB - 1))
                    if q == NQ - 1:
                        ins.then_inc(o_ps, 1)
                    if q + 2 < NQ:
                        hidden(g, q + 2)
                    elif q + 2 == NQ and not last:
                        transposes(g + 1)

            transposes(0)
            with pe.Fori(0, NG - 1) as g:
                group(g, False)
            group(NG - 1, True)


ALU_LO, ALU_HI, AX_LO, AX_HI = 16, 32, 48, 64
OPC_ADD, OPC_SUB, OPCODE_BASE, OP_START = 25, 26, 80, 10
OUTPUT_LO, OUTPUT_HI, CARRY = 128, 144, 160
NF = 4
MARK_AX, OP_ADD, OP_SUB = 0, 1, 2


def nibbles(nc, m):
    t, PS, sem = m.t, m.PS, m.sem
    take = carver(m)
    REM = GE - P
    W0 = take(2 * GE)[0:NF, :].rearrange("p (a n) -> p a n", a=2)
    W1a = take(2 * GE).rearrange("p (a n) -> p a n", a=2)
    W1b = take(2 * GE)[0:REM, :].rearrange("p (a n) -> p a n", a=2)
    W2a = take(2 * 2).rearrange("p (a n) -> p a n", a=2)
    W2b = take(2 * 2)[0:REM, :].rearrange("p (a n) -> p a n", a=2)
    Ba = take(2 * 2).rearrange("p (a n) -> p a n", a=2)
    Bb = take(2 * 2)[0:REM, :].rearrange("p (a n) -> p a n", a=2)
    BO = take(2 * 2).rearrange("p (a n) -> p a n", a=2)
    Y = m.RES
    desc = take(16)
    gt = take(NT * 64).rearrange("p (t n) -> p t n", t=NT)
    nib = take(NT * 4).rearrange("p (t n) -> p t n", t=NT)
    msk = take(NT * 4).rearrange("p (t n) -> p t n", t=NT)
    FT = take(NT * 2 * NF).rearrange("p (t s f) -> p t s f", t=NT, s=2)
    mark, op_add, op_sub, adds, subs, active, active2, both = (take(NT).rearrange("p (t n) -> p t n", t=NT) for _ in range(8))
    FS = take(2 * W2N)[0:NF, :]
    FG = take(GT * 2 * NF).rearrange("p (j s f) -> p j s f", j=GT, s=2)
    H1a = take(2 * 2 * W2N).rearrange("p (a n) -> p a n", a=2)
    H1b = take(2 * 2 * W2N)[0:REM, :].rearrange("p (a n) -> p a n", a=2)
    H2a = take(2 * 2 * W2N).rearrange("p (a n) -> p a n", a=2)
    H2b = take(2 * 2 * W2N)[0:REM, :].rearrange("p (a n) -> p a n", a=2)
    RW = GT * 2 * 2 * 2
    res = take(NG * RW)
    y = take(NT * 4).rearrange("p (q n) -> p q n", n=2)
    y2 = take(NT * 4).rearrange("p (q n) -> p q n", n=2)
    oh = take(NT * 32).rearrange("p (t s n) -> p t s n", t=NT, s=2)

    ld, desc_ready, var_ready, sd_ready, f_ready, f_in, f_ps, f_sb, h1_ps, h1_sb, h2_ps, h2_sb, y_ps, y_sb, out_ready, out_dr = (
        sem("s8_" + n) for n in ("ld", "desc_ready", "var_ready", "sd_ready", "f_ready", "f_in", "f_ps", "f_sb", "h1_ps", "h1_sb",
                                 "h2_ps", "h2_sb", "y_ps", "y_sb", "out_ready", "out_dr"))

    with nc.Block() as block:
        @block.sync
        def _(sp):
            for a, (w, b) in enumerate((("L1_ffn_Wa", "L1_ffn_ba"), ("L1_ffn_Ws", "L1_ffn_bs"))):
                wt, bc = t[w + "_T"], t[b + "_cols"]
                sp.dma_start(W0[0:2, a, :], wt[0, 0:2, :]).then_inc(ld, 16)
                sp.dma_start(W0[2:4, a, :], wt[0, OP_START + OPC_ADD:OP_START + OPC_SUB + 1, :]).then_inc(ld, 16)
                sp.dma_start(W1a[:, a, :], wt[1, 0:P, :]).then_inc(ld, 16)
                sp.dma_start(W1b[:, a, :], wt[1, P:GE, :]).then_inc(ld, 16)
                sp.dma_start(W2a[:, a, :], wt[2, 0:P, 100:102]).then_inc(ld, 16)
                sp.dma_start(W2b[:, a, :], wt[2, P:GE, 100:102]).then_inc(ld, 16)
                sp.dma_start(Ba[:, a, :], bc[0:P, 0:2]).then_inc(ld, 16)
                sp.dma_start(Bb[:, a, :], bc[P:GE, 0:2]).then_inc(ld, 16)
                sp.dma_start(BO[:, a, :], t[b][2, 100:102].partition_broadcast(P)).then_inc(ld, 16)
            for i in range(NT):
                rows = P if i < NT - 1 else LAST
                sp.wait_ge(out_ready, i + 1)
                sp.dma_start(t["out"][i * P:i * P + rows, :], m.X[0:rows, i, :]).then_inc(out_dr, 16)
            sp.wait_ge(out_dr, 16 * NT)

        @block.gpsimd
        def _(pool):
            pool.iota(desc, [[-1, 16]], base=16, channel_multiplier=0, allow_small_or_imprecise_dtypes=True).then_inc(desc_ready, 1)

        @block.vector
        def _(dve):
            for i in range(NT):
                dve.bn_stats(m.stats[:, i, :], m.X[:, i, :])
            dve.drain()
            for i in range(NT):
                dve.bn_aggr(m.mv[:, i, :], m.stats[:, i, :])
            dve.drain().then_inc(var_ready, 1)
            dve.wait_ge(sd_ready, 1)
            dve.reciprocal(m.rstd[:, :], m.sd[:, :])
            dve.drain()
            for i in range(NT):
                dve.tensor_scalar(Y[:, i, :], m.X[:, i, :], m.mv[:, i, 0:1], m.rstd[:, i:i + 1], ALU.subtract, ALU.mult)
            dve.drain()
            dve.wait_ge(desc_ready, 1)
            dve.tensor_scalar(gt, Y[:, :, ALU_LO:ALU_LO + 64], 0.5, None, ALU.is_gt)
            dve.tensor_scalar(mark, Y[:, :, MARK_AX:MARK_AX + 1], 0.5, None, ALU.is_gt)
            dve.tensor_scalar(op_add, Y[:, :, OP_ADD:OP_ADD + 1], 0.5, None, ALU.is_gt)
            dve.tensor_scalar(op_sub, Y[:, :, OP_SUB:OP_SUB + 1], 0.5, None, ALU.is_gt)
            dve.drain()
            q = gt.rearrange("p t (q n) -> p (t q) n", q=4)
            dve.tensor_tensor(q, q, desc.unsqueeze(1).to_broadcast((P, NT * 4, 16)), ALU.mult)
            dve.drain()
            dve.tensor_reduce(nib, gt.rearrange("p t (q n) -> p t q n", q=4), AX.X, ALU.max)
            dve.drain()
            dve.tensor_scalar(msk, nib, 0.0, None, ALU.is_gt)
            dve.tensor_scalar(nib, nib, -1.0, 16.0, ALU.mult, ALU.add)
            dve.drain()
            dve.tensor_tensor(nib, nib, msk, ALU.mult)
            dve.drain()
            for s in range(2):
                dve.tensor_copy(FT[:, :, s, 0:1], nib[:, :, s:s + 1])
                dve.tensor_copy(FT[:, :, s, 1:2], nib[:, :, 2 + s:3 + s])
                dve.tensor_copy(FT[:, :, s, 2:4], Y[:, :, OPCODE_BASE + OPC_ADD:OPCODE_BASE + OPC_SUB + 1])
            dve.drain().then_inc(f_ready, 1)
            dve.tensor_tensor(adds, mark, op_add, ALU.mult)
            dve.tensor_tensor(both, mark, op_sub, ALU.mult)
            dve.drain()
            dve.tensor_tensor(subs, both, op_add, ALU.mult)
            dve.drain()
            dve.tensor_tensor(subs, both, subs, ALU.subtract)
            dve.drain()
            dve.tensor_tensor(active, adds, subs, ALU.add)
            dve.drain()
            dve.tensor_scalar(active2, active, 2.0, None, ALU.mult)
            with dve.Fori(0, NG) as g:
                dve.wait_ge(f_ps, ONE + g)
                dve.tensor_copy(FG, FT[:, bass.ds(g * GT, GT), :, :]).then_inc(f_in, 1)
                dve.wait_ge(f_ps, ONE + g + 1)
                dve.tensor_copy(FS, PS[0][0:NF, :]).then_inc(f_sb, 1)
                dve.wait_ge(y_ps, g + 1)
                dve.tensor_copy(res[:, bass.ds(g * RW, RW)], PS[7][:, 0:RW]).then_inc(y_sb, 1)
            dve.drain()
            r4 = res.rearrange("p (q a n) -> p q a n", a=2, n=2)
            rq = res.rearrange("p (q n) -> p q n", n=4)
            dve.tensor_tensor(rq, rq, BO.rearrange("p a n -> p (a n)").unsqueeze(1).to_broadcast((P, 2 * NT, 4)), ALU.add)
            dve.drain()
            w = lambda v: v.to_broadcast((P, NT, 4))
            t4 = lambda v: v.rearrange("p (t s) n -> p t (s n)", s=2)
            dve.tensor_copy(y, r4[:, :, 0, :])
            dve.tensor_copy(y2, r4[:, :, 1, :])
            dve.drain()
            dve.tensor_tensor(t4(y), t4(y), w(adds), ALU.mult)
            dve.tensor_tensor(t4(y2), t4(y2), w(subs), ALU.mult)
            dve.drain()
            dve.tensor_tensor(y, y, y2, ALU.add)
            dve.drain()
            dve.tensor_scalar(y, y, ROUND, ROUND, ALU.add, ALU.subtract)
            dve.drain()
            dve.tensor_scalar(y[:, :, 0:1], y[:, :, 0:1], 0.0, 15.0, ALU.max, ALU.min)
            dve.tensor_scalar(y2[:, :, 1:2], y[:, :, 1:2], 0.5, None, ALU.is_gt)
            dve.drain()
            dve.tensor_tensor(oh.rearrange("p t s n -> p (t s) n"), m.iota_f[:, 0:16].unsqueeze(1).to_broadcast((P, 2 * NT, 16)),
                              y[:, :, 0:1].to_broadcast((P, 2 * NT, 16)), ALU.is_equal)
            carry = y2.rearrange("p (t s) n -> p t s n", s=2)[:, :, 1, 1:2]
            dve.tensor_tensor(carry, carry, active, ALU.mult)
            dve.drain()
            o = oh.rearrange("p t s n -> p t (s n)")
            dve.tensor_tensor(o, o, active2.to_broadcast((P, NT, 32)), ALU.mult)
            dve.drain()
            dve.tensor_tensor(Y[:, :, OUTPUT_LO:CARRY], Y[:, :, OUTPUT_LO:CARRY], o, ALU.add)
            dve.tensor_tensor(Y[:, :, CARRY:CARRY + 1], Y[:, :, CARRY:CARRY + 1], carry, ALU.add)
            dve.drain()
            for i in range(NT):
                dve.tensor_tensor(m.X[:, i, :], m.X[:, i, :], Y[:, i, :], ALU.add).then_inc(out_ready, 1)

        @block.scalar
        def _(act):
            act.wait_ge(var_ready, 1)
            act.activation(m.sd[:, :], m.mv[:, :, 1], ACT.Sqrt, bias=m.eps[:, 0:1]).then_inc(sd_ready, 1)
            act.wait_ge(ld, 16 * 18)
            with act.Fori(0, NG) as g:
                for layer, (ps, sbuf, Ha, Hb) in enumerate(((h1_ps, h1_sb, H1a, H1b), (h2_ps, h2_sb, H2a, H2b))):
                    for a in range(2):
                        act.wait_ge(ps, g * 2 + a + 1)
                        act.activation(Ha[:, a, :], PS[1 + a][:, :], ACT.Relu, bias=Ba[:, a, layer:layer + 1])
                        act.activation(Hb[:, a, :], PS[3 + a][0:REM, :], ACT.Relu, bias=Bb[:, a, layer:layer + 1])
                        act.drain().then_inc(sbuf, 1)

        @block.tensor
        def _(pe):
            pe.sem_inc(f_ps, ONE)
            pe.wait_ge(ld, 16 * 18)
            pe.wait_ge(f_ready, 1)
            with pe.Fori(0, NG) as g:
                pe.wait_ge(f_in, g + 1)
                for j in range(GT):
                    for s in range(2):
                        ins = pe.transpose(PS[0][0:NF, (j * 2 + s) * P:(j * 2 + s + 1) * P], FG[:, j, s, :], m.ident[:, :])
                ins.then_inc(f_ps, 1)
                pe.wait_ge(f_sb, g + 1)
                for a in range(2):
                    pe.matmul(PS[1 + a][:, :], W0[:, a, 0:P], FS, start=True, stop=True)
                    pe.matmul(PS[3 + a][0:REM, :], W0[:, a, P:GE], FS, start=True, stop=True).then_inc(h1_ps, 1)
                for a in range(2):
                    pe.wait_ge(h1_sb, g * 2 + a + 1)
                    for ps, lo, hi in ((PS[1 + a][:, :], 0, P), (PS[3 + a][0:REM, :], P, GE)):
                        pe.matmul(ps, W1a[:, a, lo:hi], H1a[:, a, :], start=True, stop=False)
                        ins = pe.matmul(ps, W1b[:, a, lo:hi], H1b[:, a, :], start=False, stop=True)
                    ins.then_inc(h2_ps, 1)
                pe.wait_ge(h2_sb, g * 2 + 2)
                for q in range(2 * GT):
                    for a in range(2):
                        at = (q * 2 + a) * 2
                        pe.matmul(PS[7][:, at:at + 2], H2a[:, a, q * P:(q + 1) * P], W2a[:, a, :], start=True, stop=False)
                        ins = pe.matmul(PS[7][:, at:at + 2], H2b[:, a, q * P:(q + 1) * P], W2b[:, a, :], start=False, stop=True)
                ins.then_inc(y_ps, 1)


_PLAIN = ["x", "src", "dst", "edge_type_4", "edge_type_8", "edge_weight", "L0_gnn_W", "L0_gnn_a_src", "L0_gnn_a_dst",
          "L0_gnn_et_emb", "L0_ffn_Wg", "L0_ffn_W1", "L0_ffn_W2", "L0_ffn_b2", "L1_gnn_self_W", "L1_gnn_rel_W",
          "L1_gnn_rel_b", "L1_gnn_W1", "L1_gnn_W2", "L1_ffn_ba", "L1_ffn_bs"] + ROW_NAMES


def kernel(**inputs):
    import concourse.bacc as _bacc
    from concourse.bass_utils import run_bass_kernel_spmd as _run

    a = {name: np.ascontiguousarray(inputs[name]) for name in _PLAIN}
    a["L0_gnn_WT"] = np.ascontiguousarray(np.asarray(inputs["L0_gnn_W"]).T)
    a["L0_ffn_b1_cols"] = np.ascontiguousarray(np.asarray(inputs["L0_ffn_b1"]).reshape(-1, P).T)
    a["L1_gnn_b1_cols"] = np.ascontiguousarray(np.asarray(inputs["L1_gnn_b1"]).reshape(-1, P).T)
    for w, b in (("L1_ffn_Wa", "L1_ffn_ba"), ("L1_ffn_Ws", "L1_ffn_bs")):
        a[w + "_T"] = np.ascontiguousarray(np.asarray(inputs[w]).transpose(0, 2, 1))
        a[b + "_cols"] = np.ascontiguousarray(np.asarray(inputs[b]).T)

    nc = _bacc.Bacc("TRN2", target_bir_lowering=False, num_devices=1)
    t = {name: nc.dram_tensor("in_" + name, v.shape, mybir.dt.from_np(v.dtype), kind="ExternalInput").ap() for name, v in a.items()}
    t["out"] = nc.dram_tensor("out", (N, D), F32, kind="ExternalOutput").ap()
    build(nc, t)
    r = _run(nc, [{"in_" + name: v for name, v in a.items()}], core_ids=[0])
    return r.results[0]["out"]
```

```python
from contextlib import ExitStack

import concourse.bass as bass
import numpy as np
from concourse import mybir

ALU = mybir.AluOpType
ACT = mybir.ActivationFunctionType
AX = mybir.AxisListType
F32, F16, BF16 = mybir.dt.float32, mybir.dt.float16, mybir.dt.bfloat16
I32, U32 = mybir.dt.int32, mybir.dt.uint32

P = 128
N = 1250
D = 512
E = 40000
NT = -(-N // P)
NP = NT * P
LAST = N - (NT - 1) * P
KD = D // P
H, HD = 8, 64
NREL = 4
NTYPE = 8
NEXP, HID = 8, 256
FF = 1024
GT = 2
NG = NT // GT
W2N = GT * P

C = -(-E // P)
EP = C * P
CG = 12
NCG = -(-C // CG)
CP = NCG * CG
TAIL = E - (P - 1) * C
CHUNK = 512
CJ = CHUNK // P
STEPS = (EP + NT * (CHUNK - 1)) // CHUNK
RING = 4
R0 = 2 + H + 1
R1 = 2
PARTS = 3
EPS = 1e-5
NEG_SLOPE = 0.2
PAD_DST = NP - 1
ROUND = 12582912.0
GE = 160
ONE = 1
WBYTES = 64 * 1024

ROW_NAMES = ["L0_gnn_ln_gamma", "L0_gnn_ln_beta", "L0_ffn_ln_g", "L0_ffn_ln_b", "L0_ffn_out_g",
             "L0_ffn_out_b", "L1_gnn_self_b", "L1_gnn_ln1_w", "L1_gnn_ln1_b", "L1_gnn_b2",
             "L1_gnn_ln2_w", "L1_gnn_ln2_b"]


class Shared:
    pass


def tile(ap, i):
    return ap[:, bass.ds(i, 1), :].rearrange("p a d -> p (a d)")


def over_heads(ap):
    return ap.unsqueeze(2).to_broadcast((P, H, HD))


def build(nc, t):
    with ExitStack() as ctx:
        m = Shared()
        m.t = t

        def sb(name, shape, dt=F32):
            return ctx.enter_context(nc.sbuf_tensor(name, shape, dt))

        def sem(name):
            return ctx.enter_context(nc.semaphore(name))

        def dram(name, shape, dt=F32):
            return nc.dram_tensor(name, shape, dt, kind="Internal").ap()

        m.sb, m.sem = sb, sem
        m.h_rows = dram("h_rows", [NP, D])
        m.rel_rows = dram("rel_rows", [NP * NREL, D])
        m.rec0 = dram("rec0", [EP + CHUNK, R0])
        m.rec1 = dram("rec1", [EP + CHUNK, R1])
        m.src_cp = dram("src_cp", [CP, P], F16)
        m.dst_cp = dram("dst_cp", [CP, P], F16)

        m.X = sb("X", [P, NT, D])
        m.ACC = sb("ACC", [P, NT, D])
        m.ASUM = sb("ASUM", [P, NT, H + 1])
        m.RES = sb("RES", [P, NT, D])
        m.XS = sb("XS", [P, GT, D])
        m.XT = sb("XT", [P, KD, W2N])
        m.U = sb("U", [P, GT, D])
        m.ident = sb("ident", [P, P])
        m.iota_f = sb("iota_f", [P, P])
        m.iota_k = sb("iota_k", [P, NT])
        m.ones = sb("ones", [P, P])
        m.eps = sb("eps", [P, 1])
        m.half = sb("half", [P, NT])
        m.ROWS = sb("ROWS", [P, len(ROW_NAMES), D])
        m.rows = {name: m.ROWS[:, n, :] for n, name in enumerate(ROW_NAMES)}
        m.stats = sb("stats", [P, NT, 6])
        m.mv = sb("mv", [P, NT, 2])
        m.sd = sb("sd", [P, NT])
        m.rstd = sb("rstd", [P, NT])
        m.TAB = sb("TAB", [P, 2, PARTS, NT, H], BF16)
        m.woff = sb("woff", [P, STEPS])
        m.step_off = sb("step_off", [P, STEPS], I32)
        m.step_win = sb("step_win", [P, STEPS], I32)
        m.arena_words = 26 * 1024 + 512
        m.arena = sb("arena", [P, m.arena_words])
        m.PS = [ctx.enter_context(nc.psum_tensor(f"PS{i}", [P, 512], F32)) for i in range(8)]

        load_inputs(nc, m)
        sort_edges(nc, m)
        node_scores(nc, m)
        edge_weights(nc, m)
        messages(nc, m, "m0", m.rec0, R0, m.h_rows, True, load_experts)
        experts(nc, m)
        relations(nc, m)
        messages(nc, m, "m1", m.rec1, R1, m.rel_rows, False, load_ffn)
        ffn(nc, m)
        nibbles(nc, m)


def carver(m, start=0, end=None):
    at = [start]
    end = m.arena_words if end is None else end

    def take(words):
        at[0] += words
        assert at[0] <= end, at
        return m.arena[:, at[0] - words:at[0]]
    return take


FIELDS = ("src", "dst", "edge_type_4", "edge_type_8", "edge_weight")
NODE_AT = 10 * 1024


def edge_arrays(m):
    top = m.arena[:, m.arena_words - 12 * CP:]
    EDG = top.rearrange("p (n c) -> p n c", n=12)
    return EDG, [EDG[:, n, :].bitcast(I32) for n in range(4)] + [EDG[:, 4, :]], EDG[:, 10, :].bitcast(I32), EDG[:, 11, :]


def factor_arrays(m):
    top = m.arena_words - 12 * CP
    MUL = m.arena[:, top - H * CP:top].rearrange("p (h c) -> p h c", h=H)
    return MUL, m.arena[:, top - H * CP - NTYPE * H:top - H * CP]


def node_arrays(m):
    take = carver(m, NODE_AT)
    WT = take(KD * D).rearrange("p (k d) -> p k d", k=KD)
    WR = take(KD * D).rearrange("p (k d) -> p k d", k=KD)
    AB = take(KD * 2 * H).rearrange("p (k d) -> p k d", k=KD)
    return WT, WR, AB, take


def load_inputs(nc, m):
    t, PS, sem = m.t, m.PS, m.sem
    EDG, fields, next_i, down = edge_arrays(m)
    MUL, emb = factor_arrays(m)
    WT, WR, AB, _ = node_arrays(m)
    m.flag = m.sb("flag", [P, 1], I32)
    down_n = m.sb("down_n", [P, 1])
    edg_zero, edg_pad, e_ld, x_zero, ab_zero, down_ready, down_ps, mv_ready = (sem("s1_" + n) for n in (
        "edg_zero", "edg_pad", "e_ld", "x_zero", "ab_zero", "down_ready", "down_ps", "mv_ready"))
    m.x_ld, m.w_ld, m.a_ld, m.emb_ld, m.consts = (sem("s1_" + n) for n in ("x_ld", "w_ld", "a_ld", "emb_ld", "consts"))

    with nc.Block() as block:
        @block.sync
        def _(sp):
            sp.wait_ge(edg_pad, 1)
            full = (P - 1) * C
            for dst, name in zip(fields, FIELDS):
                sp.dma_start(dst[0:P - 1, 0:C], t[name][0:full].rearrange("(p c) -> p c", c=C)).then_inc(e_ld, 16)
                sp.dma_start(dst[P - 1:P, 0:TAIL], t[name][full:E].unsqueeze(0)).then_inc(e_ld, 16)
            sp.dma_start(next_i[0:P - 1, 0:C], t["dst"][1:full + 1].rearrange("(p c) -> p c", c=C)).then_inc(e_ld, 16)
            sp.dma_start(next_i[P - 1:P, 0:TAIL - 1], t["dst"][full + 1:E].unsqueeze(0)).then_inc(e_ld, 16)

        @block.scalar
        def _(act):
            act.dma_start(m.X[:, 0:NT - 1, :], t["x"][0:(NT - 1) * P, :].rearrange("(t p) d -> p t d", p=P)).then_inc(m.x_ld, 16)
            act.wait_ge(x_zero, 1)
            act.dma_start(m.X[0:LAST, NT - 1, :], t["x"][(NT - 1) * P:N, :]).then_inc(m.x_ld, 16)
            act.wait_ge(ab_zero, 1)
            for s, name in enumerate(("L0_gnn_a_src", "L0_gnn_a_dst")):
                for odd in range(P // HD):
                    act.dma_start(AB.rearrange("p k d -> p (k d)")[odd * HD:(odd + 1) * HD, s * H + odd::2 * H + P // HD],
                                  t[name][odd::P // HD, :].rearrange("a d -> d a"), allow_slow_non_contiguous=True).then_inc(m.a_ld, 16)
            act.dma_start(WR, t["L0_gnn_W"].rearrange("(k p) d -> p k d", p=P)).then_inc(m.w_ld, 16)
            act.dma_start(WT, t["L0_gnn_WT"].rearrange("(k p) d -> p k d", p=P)).then_inc(m.w_ld, 16)
            act.dma_start(emb, t["L0_gnn_et_emb"].rearrange("t h -> (t h)").partition_broadcast(P)).then_inc(m.emb_ld, 16)

        @block.gpsimd
        def _(pool):
            pool.memset(EDG[:, 0:len(FIELDS), :], 0.0).then_inc(edg_zero, 1)
            pool.memset(AB, 0.0).then_inc(ab_zero, 1)
            pool.memset(m.eps[:, :], EPS)
            pool.memset(m.half[:, :], -0.5)
            pool.memset(m.ones[:, :], 1.0)
            pool.memset(m.ident[:, :], 0.0)
            pool.iota(m.iota_f[:, :], [[1, P]], base=0, channel_multiplier=0, allow_small_or_imprecise_dtypes=True)
            pool.iota(m.iota_k[:, :], [[P, NT]], base=0, channel_multiplier=1, allow_small_or_imprecise_dtypes=True)
            pool.drain()
            pool.affine_select(out=m.ident[:, :], in_=m.ident[:, :], compare_op=ALU.not_equal, fill=1.0, base=0,
                               pattern=[[-1, P]], channel_multiplier=1).then_inc(m.consts, 1)
            pool.memset(MUL, 0.0)
            pool.wait_ge(mv_ready, 1)
            pool.tensor_tensor(m.sd[:, :], m.mv[:, :, 1], m.eps[:, 0:1].to_broadcast((P, NT)), ALU.add)
            pool.drain()
            pool.tensor_tensor(m.rstd[:, :], m.sd[:, :], m.half[:, :], ALU.pow)

        @block.vector
        def _(dve):
            dve.memset(m.X[:, NT - 1, :], 0.0).then_inc(x_zero, 1)
            dve.memset(next_i, PAD_DST)
            dve.wait_ge(edg_zero, 1)
            dve.memset(fields[1], PAD_DST)
            dve.drain().then_inc(edg_pad, 1)
            dve.memset(m.ACC[:, :, :], 0.0)
            dve.memset(m.ASUM[:, :, :], 0.0)
            dve.wait_ge(m.x_ld, 32)
            for i in range(NT):
                dve.bn_stats(m.stats[:, i, :], m.X[:, i, :])
            dve.drain()
            for i in range(NT):
                dve.bn_aggr(m.mv[:, i, :], m.stats[:, i, :])
            dve.drain().then_inc(mv_ready, 1)
            dve.wait_ge(e_ld, 32 * (len(FIELDS) + 1))
            dve.tensor_tensor(down, next_i, fields[1], ALU.is_lt)
            dve.drain()
            dve.tensor_reduce(down_n[:, :], down[:, 0:C], AX.X, ALU.add)
            dve.drain().then_inc(down_ready, 1)
            dve.wait_ge(down_ps, 1)
            dve.tensor_copy(m.flag[:, :], PS[0][:, 0:1])
            dve.drain()

        @block.tensor
        def _(pe):
            pe.wait_ge(m.consts, 1)
            pe.wait_ge(down_ready, 1)
            pe.matmul(PS[0][:, 0:1], m.ones[:, :], down_n[:, :], start=True, stop=True).then_inc(down_ps, 1)


def sort_edges(nc, m):
    PS, sem = m.PS, m.sem
    take = carver(m, end=NODE_AT)
    EDG, fields, _, _ = edge_arrays(m)
    REC5 = take(C * 5).rearrange("p (c f) -> p c f", f=5)
    REC5_i = REC5.bitcast(I32)
    iota_n = take(NP)
    OHD = take(NP // 2).bitcast(BF16)
    prod = take(NP)
    starts = take(NP)
    rank, add, pos = take(CP), take(CP), take(CP)
    dst_f = take(CP)
    pos_i = take(CP).bitcast(I32)
    BEFORE = take(P // 2).bitcast(BF16)
    OTHERS = take(P // 2).bitcast(BF16)
    ZERO = take(P // 2).bitcast(BF16)
    ones_n = take(NP)
    idx1 = take(1).bitcast(I32)
    rec_1 = take(5)
    sorted5 = nc.dram_tensor("sorted5", [EP, 5], F32, kind="Internal").ap()
    ready, oh_ready, before_ps, rank_read, all_ps, pos_ready, staged, scattered, back = (sem("s2_" + n) for n in (
        "ready", "oh_ready", "before_ps", "rank_read", "all_ps", "pos_ready", "staged", "scattered", "back"))
    SPAN = [(0, 512), (512, 1024), (1024, NP)]

    def out_of_order(eng):
        return eng.value_load(m.flag[0:1, 0:1], min_val=0, max_val=E)

    with nc.Block() as block:
        @block.vector
        def _(dve):
            with dve.If(out_of_order(dve) > 0):
                dve.wait_ge(ready, 1)
                dve.tensor_copy(dst_f, fields[1])
                for f in range(4):
                    dve.tensor_copy(REC5_i[:, :, f], fields[f][:, 0:C])
                dve.tensor_copy(REC5[:, :, 4], fields[4][:, 0:C])
                dve.tensor_scalar(BEFORE, m.iota_f[:, :], m.iota_k[:, 0:1], None, ALU.is_gt)
                dve.tensor_scalar(OTHERS, m.iota_f[:, :], m.iota_k[:, 0:1], None, ALU.is_le)
                dve.memset(ZERO, 0.0)
                dve.memset(ones_n, 1.0)
                dve.drain()
                dve.tensor_scalar(OHD, iota_n, dst_f[:, 0:1], None, ALU.is_equal)
                dve.drain().then_inc(oh_ready, 1)
                with dve.Fori(0, C) as c:
                    dve.wait_ge(before_ps, c + 1)
                    for b, (lo, hi) in enumerate(SPAN):
                        dve.tensor_tensor(prod[:, lo:hi], OHD[:, lo:hi], PS[b][:, 0:hi - lo], ALU.mult)
                    dve.drain()
                    dve.tensor_reduce(rank[:, bass.ds(c, 1)], prod, AX.X, ALU.add)
                    dve.drain().then_inc(rank_read, 1)
                    dve.wait_ge(all_ps, c + 1)
                    dve.tensor_scalar(OHD, iota_n, dst_f[:, bass.ds(c + 1, 1)], None, ALU.is_equal)
                    dve.drain().then_inc(oh_ready, 1)
                for b, (lo, hi) in enumerate(SPAN):
                    dve.tensor_copy(prod[:, lo:hi], PS[b][:, 0:hi - lo])
                dve.drain()
                dve.tensor_tensor_scan(starts, ones_n, prod, 0.0, ALU.mult, ALU.add)
                dve.drain()
                dve.tensor_tensor(starts, starts, prod, ALU.subtract)
                dve.drain()
                with dve.Fori(0, C) as c:
                    dve.tensor_scalar(OHD, iota_n, dst_f[:, bass.ds(c, 1)], None, ALU.is_equal)
                    dve.drain()
                    dve.tensor_tensor(prod, OHD, starts, ALU.mult)
                    dve.drain()
                    dve.tensor_reduce(add[:, bass.ds(c, 1)], prod, AX.X, ALU.add)
                    dve.drain()
                dve.tensor_tensor(pos_i[:, 0:C], rank[:, 0:C], add[:, 0:C], ALU.add)
                dve.drain().then_inc(pos_ready, 1)
                dve.wait_ge(back, 16)
                for f in range(4):
                    dve.tensor_copy(fields[f][:, 0:C], REC5_i[:, :, f])
                dve.tensor_copy(fields[4][:, 0:C], REC5[:, :, 4])
                dve.drain()

        @block.gpsimd
        def _(pool):
            with pool.If(out_of_order(pool) > 0):
                pool.iota(iota_n, [[1, NP]], base=0, channel_multiplier=0, allow_small_or_imprecise_dtypes=True)
                pool.drain().then_inc(ready, 1)
                pool.wait_ge(pos_ready, 1)
                with pool.Fori(0, C) as c:
                    pool.tensor_copy(idx1, pos_i[:, bass.ds(c, 1)])
                    pool.tensor_copy(rec_1, tile(REC5, c))
                    pool.drain().then_inc(staged, 1)
                    pool.wait_ge(staged, c + 1)
                    pool.sem_inc(pos_ready, 1)
                    pool.indirect_dma_start(sorted5, bass.IndirectOffsetOnAxis(ap=idx1, axis=0), rec_1, None).then_inc(scattered, 16)
                    pool.wait_ge(scattered, c * 16 + 16)
                pool.dma_start(REC5.rearrange("p c f -> p (c f)"), sorted5.rearrange("(p c) f -> p (c f)", c=C)).then_inc(back, 16)

        @block.tensor
        def _(pe):
            with pe.If(out_of_order(pe) > 0):
                pe.wait_ge(oh_ready, 1)
                for b, (lo, hi) in enumerate(SPAN):
                    pe.matmul(PS[b][:, 0:hi - lo], ZERO, OHD[:, lo:hi], start=True, stop=False, skip_group_check=True)
                with pe.Fori(0, C) as c:
                    pe.wait_ge(oh_ready, c + 1)
                    for b, (lo, hi) in enumerate(SPAN):
                        ins = pe.matmul(PS[b][:, 0:hi - lo], BEFORE, OHD[:, lo:hi], start=False, stop=False, skip_group_check=True)
                    ins.then_inc(before_ps, 1)
                    pe.wait_ge(rank_read, c + 1)
                    for b, (lo, hi) in enumerate(SPAN):
                        ins = pe.matmul(PS[b][:, 0:hi - lo], OTHERS, OHD[:, lo:hi], start=False, stop=False, skip_group_check=True)
                    ins.then_inc(all_ps, 1)


def node_scores(nc, m):
    PS, sem = m.PS, m.sem
    WT, WR, AB, take = node_arrays(m)
    WA = take(KD * 2 * H).rearrange("p (k d) -> p k d", k=KD)
    STG = take(GT * D).rearrange("p (j d) -> p j d", j=GT)
    SV = take(NT * 2 * H).rearrange("p (t s) -> p t s", t=NT)
    SR = take(NT * 2 * H).rearrange("p (t s) -> p t s", t=NT)
    EDG, fields, _, _ = edge_arrays(m)
    MUL, emb = factor_arrays(m)
    src_f, dst_f, t8_f, mask, same = (EDG[:, n, :] for n in range(5, 10))
    tile_f = EDG[:, 10:12, :]
    low = carver(m, end=NODE_AT)
    q_f = low(2 * CP).rearrange("p (s c) -> p s c", s=2)
    tile_i = low(2 * CP).rearrange("p (s c) -> p s c", s=2).bitcast(I32)
    cp16 = low(2 * 3 * P // 2).bitcast(F16).rearrange("p (s b e) -> p s b e", s=2, b=3)
    cnt, tot, sst = low(NT + 1), low(NT + 1), low(NT + 1)
    nst, nst_i, adj, dadj = low(NT), low(NT).bitcast(I32), low(NT), low(NT)
    iota_s, off_f = low(STEPS), low(STEPS)
    begun = low(STEPS * (NT - 1)).rearrange("p (s w) -> p s w", w=NT - 1)
    floats, q_ready, mul_ready, cnt_ready, cp_zero, cp_ps, cp_sb, cp_dr, tot_ps = (sem("s3_" + n) for n in (
        "floats", "q_ready", "mul_ready", "cnt_ready", "cp_zero", "cp_ps", "cp_sb", "cp_dr", "tot_ps"))
    wa_ps, wa_sb, xs_ready, xt_ps, xt_sb, res_sb, h_ps, h_sb, h_dr, row_ld = (sem("s3_" + n) for n in (
        "wa_ps", "wa_sb", "xs_ready", "xt_ps", "xt_sb", "res_sb", "h_ps", "h_sb", "h_dr", "row_ld"))
    TYPES = NTYPE // (NG - 1)

    with nc.Block() as block:
        @block.sync
        def _(sp):
            sp.sem_inc(h_dr, ONE)
            for name in ROW_NAMES:
                sp.dma_start(m.rows[name], m.t[name].partition_broadcast(P)).then_inc(row_ld, 16)
            with sp.Fori(0, NG) as g:
                sp.wait_ge(h_sb, ONE + g * GT + GT)
                sp.dma_start(m.h_rows[bass.ds(g * W2N, W2N), :].rearrange("(j p) d -> p j d", p=P), STG).then_inc(h_dr, 16)
            sp.wait_ge(cp_sb, 2)
            for s, cp in enumerate((m.src_cp, m.dst_cp)):
                sp.dma_start(cp[0:2 * P, :].rearrange("(b c) p -> c b p", c=P), cp16[:, s, 0:2, :]).then_inc(cp_dr, 16)
                sp.dma_start(cp[2 * P:CP, :], cp16[0:CP - 2 * P, s, 2, :]).then_inc(cp_dr, 16)
            sp.wait_ge(cp_dr, 64)
            sp.wait_ge(h_dr, ONE + 16 * NG)
            sp.wait_ge(row_ld, 16 * len(ROW_NAMES))

        @block.gpsimd
        def _(pool):
            pool.iota(iota_s, [[1, STEPS]], base=0, channel_multiplier=0, allow_small_or_imprecise_dtypes=True)
            pool.tensor_copy(dst_f, fields[1])
            pool.tensor_copy(src_f, fields[0])
            pool.tensor_copy(t8_f, fields[3])
            pool.drain().then_inc(floats, 1)
            pool.memset(cp16, 0.0).then_inc(cp_zero, 1)
            pool.wait_ge(mul_ready, 1)
            pool.tensor_tensor(MUL, MUL, fields[4].unsqueeze(1).to_broadcast((P, H, CP)), ALU.mult)

        @block.vector
        def _(dve):
            def normalise(g):
                dve.wait_ge(xt_ps, ONE + g * GT)
                dve.wait_ge(res_sb, ONE + g * GT)
                for j in range(GT):
                    dve.tensor_scalar(m.XS[:, j, :], tile(m.X, g * GT + j), tile(m.mv, g * GT + j)[:, 0:1],
                                      m.rstd[:, bass.ds(g * GT + j, 1)], ALU.subtract, ALU.mult).then_inc(xs_ready, 1)

            normalise(0)
            dve.wait_ge(wa_ps, 1)
            dve.tensor_copy(WA, PS[7][:, 0:KD * 2 * H].rearrange("p (k d) -> p k d", k=KD)).then_inc(wa_sb, 1)
            dve.wait_ge(m.emb_ld, 16)
            dve.tensor_scalar(emb, emb, 1.0, None, ALU.add)
            for s, v in enumerate(fields[0:2]):
                dve.tensor_scalar(tile_i[:, s, :], v, P.bit_length() - 1, None, ALU.arith_shift_right)
            dve.drain()
            dve.tensor_copy(tile_f, tile_i)
            dve.drain()
            dve.wait_ge(floats, 1)
            for s, v in enumerate((src_f, dst_f)):
                dve.scalar_tensor_tensor(q_f[:, s, :], tile_f[:, s, :], -float(P), v, ALU.mult, ALU.add)
            dve.drain().then_inc(q_ready, 1)
            with dve.Fori(0, NG - 1) as g:
                normalise(g + 1)
                for n in range(TYPES):
                    ty = g * TYPES + n
                    dve.tensor_scalar(mask, t8_f, m.iota_f[:, bass.ds(ty, 1)], None, ALU.is_equal)
                    dve.drain()
                    for h in range(H):
                        dve.scalar_tensor_tensor(MUL[:, h, :], mask, emb[:, bass.ds(ty * H + h, 1)], MUL[:, h, :], ALU.mult, ALU.add)
                    dve.drain()
            dve.drain().then_inc(mul_ready, 1)
            dve.memset(cnt[:, 0:1], 0.0)
            dve.drain()
            for w in range(1, NT + 1):
                dve.tensor_scalar(mask[:, 0:C], dst_f[:, 0:C], float(P * w), 0.0, ALU.is_lt, ALU.add, accum_out=cnt[:, w:w + 1])
                dve.drain()
            dve.drain().then_inc(cnt_ready, 1)
            dve.memset(same[:, 0:1], 1.0)
            dve.tensor_tensor(same[:, 1:C], dst_f[:, 1:C], dst_f[:, 0:C - 1], ALU.is_equal)
            dve.memset(same[:, C:C + 1], 1.0)
            dve.wait_ge(tot_ps, 1)
            dve.tensor_copy(tot, PS[0][:, 0:NT + 1])
            dve.drain()
            dve.tensor_tensor(nst, tot[:, 1:NT + 1], tot[:, 0:NT], ALU.subtract)
            dve.drain()
            dve.tensor_scalar(nst_i, nst, float(CHUNK - 1), None, ALU.add)
            dve.drain()
            dve.tensor_scalar(nst_i, nst_i, CHUNK.bit_length() - 1, None, ALU.arith_shift_right)
            dve.drain()
            dve.tensor_copy(nst, nst_i)
            dve.memset(sst, 0.0)
            dve.drain()
            dve.tensor_tensor_scan(sst[:, 1:NT + 1], m.ones[:, 0:NT], nst, 0.0, ALU.mult, ALU.add)
            dve.drain()
            dve.scalar_tensor_tensor(adj, sst[:, 0:NT], -float(CHUNK), tot[:, 0:NT], ALU.mult, ALU.add)
            dve.drain()
            dve.tensor_tensor(dadj[:, 1:NT], adj[:, 1:NT], adj[:, 0:NT - 1], ALU.subtract)
            shape = (P, STEPS, NT - 1)
            dve.tensor_tensor(begun, iota_s.unsqueeze(2).to_broadcast(shape), sst[:, 1:NT].unsqueeze(1).to_broadcast(shape), ALU.is_ge)
            dve.drain()
            dve.tensor_reduce(m.woff[:, :], begun, AX.X, ALU.add)
            dve.drain()
            dve.tensor_tensor(begun, begun, dadj[:, 1:NT].unsqueeze(1).to_broadcast(shape), ALU.mult)
            dve.drain()
            dve.tensor_reduce(off_f, begun, AX.X, ALU.add)
            dve.drain()
            dve.scalar_tensor_tensor(off_f, iota_s, float(CHUNK), off_f, ALU.mult, ALU.add)
            dve.drain()
            dve.tensor_scalar(m.step_off[:, :], off_f, float(EP), None, ALU.min)
            dve.tensor_copy(m.step_win[:, :], m.woff[:, :])
            dve.drain()
            dve.tensor_scalar(m.woff[:, :], m.woff[:, :], float(P), None, ALU.mult)
            dve.wait_ge(h_sb, ONE + NT)
            for s in range(2):
                left = SV[:, :, s * H:(s + 1) * H]
                for part in range(PARTS):
                    dve.tensor_copy(m.TAB[:, s, part, :, :], left)
                    dve.drain()
                    if part < PARTS - 1:
                        rest = SR[:, :, part * H:(part + 1) * H]
                        dve.tensor_tensor(rest, left, m.TAB[:, s, part, :, :], ALU.subtract)
                        dve.drain()
                        left = rest

        @block.scalar
        def _(act):
            act.sem_inc(res_sb, ONE)
            act.sem_inc(xt_sb, ONE)
            act.sem_inc(h_sb, ONE)

            def keep(g):
                for j in range(GT):
                    act.wait_ge(xs_ready, g * GT + j + 1)
                    act.copy(tile(m.RES, g * GT + j), m.XS[:, j, :]).then_inc(res_sb, 1)

            def transposed(g, j):
                act.wait_ge(xt_ps, ONE + g * GT + j + 1)
                act.copy(m.XT[:, :, j * P:(j + 1) * P], PS[j][:, :].rearrange("p (k n) -> p k n", k=KD)).then_inc(xt_sb, 1)

            def products(g, last):
                for j in range(GT):
                    act.wait_ge(h_ps, ONE + g * GT + j + 1)
                    if not last:
                        transposed(g + 1, j)
                    act.wait_ge(h_dr, ONE + g * 16)
                    act.copy(STG[:, j, :], PS[4 + j][:, :])
                    act.copy(tile(SV, g * GT + j), PS[2 + j][:, 0:2 * H])
                    act.drain().then_inc(h_sb, 1)

            keep(0)
            for j in range(GT):
                transposed(0, j)
            with act.Fori(0, NG - 1) as g:
                keep(g + 1)
                products(g, False)
            act.wait_ge(cp_zero, 1)
            for s in range(2):
                act.wait_ge(cp_ps, s + 1)
                act.copy(cp16[:, s, 0:2, :], PS[6 + s][:, 0:2 * P].rearrange("p (b c) -> p b c", b=2))
                act.copy(cp16[0:C - 2 * P, s, 2, :], PS[6 + s][0:C - 2 * P, 2 * P:3 * P])
                act.drain().then_inc(cp_sb, 1)
            products(NG - 1, True)

        @block.tensor
        def _(pe):
            pe.sem_inc(xt_ps, ONE)
            pe.sem_inc(h_ps, ONE)

            def transposes(g):
                pe.wait_ge(xt_sb, ONE + g * GT)
                for j in range(GT):
                    pe.wait_ge(xs_ready, g * GT + j + 1)
                    for k in range(KD):
                        ins = pe.transpose(PS[j][:, k * P:(k + 1) * P], m.XS[:, j, k * P:(k + 1) * P], m.ident[:, :])
                    ins.then_inc(xt_ps, 1)

            def products(g):
                for j in range(GT):
                    pe.wait_ge(xt_sb, ONE + g * GT + j + 1)
                    pe.wait_ge(h_sb, ONE + g * GT)
                    for k in range(KD):
                        pe.matmul(PS[2 + j][:, 0:2 * H], m.XT[:, k, j * P:(j + 1) * P], WA[:, k, :],
                                  start=(k == 0), stop=(k == KD - 1))
                    for k in range(KD):
                        ins = pe.matmul(PS[4 + j][:, :], m.XT[:, k, j * P:(j + 1) * P], WT[:, k, :],
                                        start=(k == 0), stop=(k == KD - 1))
                    ins.then_inc(h_ps, 1)

            pe.wait_ge(m.w_ld, 32)
            pe.wait_ge(m.a_ld, 16 * 2 * P // HD)
            for k in range(KD):
                for b in range(KD):
                    ins = pe.matmul(PS[7][:, k * 2 * H:(k + 1) * 2 * H], WR[:, b, k * P:(k + 1) * P], AB[:, b, :],
                                    start=(b == 0), stop=(b == KD - 1))
            ins.then_inc(wa_ps, 1)
            pe.wait_ge(m.consts, 1)
            transposes(0)
            pe.wait_ge(wa_sb, 1)
            with pe.Fori(0, NG - 1) as g:
                transposes(g + 1)
                products(g)
            pe.wait_ge(q_ready, 1)
            for s in range(2):
                for b in range(3):
                    n = min(P, C - b * P)
                    ins = pe.transpose(PS[6 + s][0:n, b * P:(b + 1) * P], q_f[:, s, b * P:b * P + n], m.ident[:, :])
                ins.then_inc(cp_ps, 1)
            products(NG - 1)
            pe.wait_ge(cnt_ready, 1)
            pe.matmul(PS[0][:, 0:NT + 1], m.ones[:, :], cnt, start=True, stop=True).then_inc(tot_ps, 1)


def edge_weights(nc, m):
    t, PS, sem = m.t, m.PS, m.sem
    UNITS = 4
    BANK = CG // 2
    assert BANK * NT * H <= 512 and NCG % 2 == 1
    take = carver(m, end=m.arena_words - (12 + H) * CP - NTYPE * H)
    BC = take(2 * 2 * CG * P // 2).bitcast(F16).rearrange("p (r s e) -> p r s e", r=2, s=2)
    OT = take(UNITS * CG * P // 2).bitcast(BF16).rearrange("p (r e) -> p r e", r=UNITS)
    FOUND = [v[:, 0:CG * NT * H] for v in (m.XS.rearrange("p a d -> p (a d)"), m.XT.rearrange("p a d -> p (a d)"),
                                           m.U.rearrange("p a d -> p (a d)"), take(CG * NT * H))]
    MINE = take(UNITS * CG * NT).rearrange("p (r c k) -> p r c k", r=UNITS, k=NT)
    SC = take(H * CP).rearrange("p (h c) -> p h c", h=H)
    MUL, emb = factor_arrays(m)
    FW = take(H * CP).rearrange("p (h c) -> p h c", h=H)
    EDG, (src_i, _, t4_i, _, _), _, _ = edge_arrays(m)
    src_f, dst_f, _, _, same = (EDG[:, n, :] for n in range(5, 10))
    tile_f = EDG[:, 10:12, :]
    REC0 = take(C * R0).rearrange("p (c r) -> p c r", r=R0)
    REC1 = take(C * R1).rearrange("p (c r) -> p c r", r=R1)
    lv_in = take(4 * H).rearrange("p (n h) -> p n h", n=4)
    lv = take(4 * 2 * P).rearrange("p (n e s) -> p n e s", n=4, e=P)
    lv_same = take(2 * P + 1)[0:H, :]
    g_first, g_last = take(H), take(H)
    tail = take(CJ * R0).rearrange("p (c r) -> p c r", r=R0)

    tails = sem("s4_tails")
    bc_ld = [sem(f"s4_bc_ld{i}") for i in range(2)]
    mine_ready, bc_free, ot_ready, looked_up, copied, chosen, found_free = (sem("s4_" + n) for n in (
        "mine_ready", "bc_free", "ot_ready", "looked_up", "copied", "chosen", "found_free"))
    lv_ready, lv_ps, lv_done, gb_ps, diff, rec1_ready, rec_ready, rec_dr = (sem("s4_" + n) for n in (
        "lv_ready", "lv_ps", "lv_done", "gb_ps", "diff", "rec1_ready", "rec_ready", "rec_dr"))

    with nc.Block() as block:
        @block.sync
        def _(sp):
            def load(g, r):
                sp.wait_ge(bc_free, g + 1)
                for s, cp in enumerate((m.src_cp, m.dst_cp)):
                    sp.dma_start(BC[:, r, s, :], cp[bass.ds(g * CG, CG), :].rearrange("c p -> (c p)").partition_broadcast(P)).then_inc(bc_ld[r], 16)

            with sp.Fori(0, NCG // 2) as i:
                for r in range(2):
                    load(i * 2 + r, r)
            load(NCG - 1, 0)
            sp.wait_ge(rec1_ready, 1)
            sp.dma_start(m.rec1[0:EP, :].rearrange("(p c) r -> p (c r)", c=C), REC1.rearrange("p c r -> p (c r)")).then_inc(rec_dr, 16)
            sp.wait_ge(tails, 1)
            sp.dma_start(m.rec0[EP:EP + CHUNK, :].rearrange("(p c) r -> p c r", c=CJ), tail).then_inc(rec_dr, 16)
            sp.dma_start(m.rec1[EP:EP + CHUNK, :].rearrange("(p c) r -> p c r", c=CJ), tail[:, :, 0:R1]).then_inc(rec_dr, 16)
            sp.wait_ge(rec_ready, 1)
            sp.dma_start(m.rec0[0:EP, :].rearrange("(p c) r -> p (c r)", c=C), REC0.rearrange("p c r -> p (c r)")).then_inc(rec_dr, 16)
            sp.wait_ge(rec_dr, 64)

        @block.gpsimd
        def _(pool):
            pool.memset(tail, 0.0)
            pool.drain()
            pool.memset(tail[:, :, 1:2], -1.0).then_inc(tails, 1)

            def choose(g, b):
                s = b % 2
                pool.wait_ge(mine_ready, g * 2 + s + 1)
                pool.wait_ge(copied, UNITS + g * 2 + s + 1)
                f = FOUND[b].rearrange("p (c k h) -> p c k h", c=CG, k=NT)
                pool.tensor_tensor(f, f, MINE[:, b, :, :].unsqueeze(3).to_broadcast((P, CG, NT, H)), ALU.mult)
                pool.drain().then_inc(chosen, 1)

            with pool.Fori(0, NCG // 2) as i:
                for b in range(UNITS):
                    choose(i * 2 + b // 2, b)
            for b in range(2):
                choose(NCG - 1, b)

        @block.vector
        def _(dve):
            dve.sem_inc(bc_free, 2)
            dve.sem_inc(found_free, UNITS)
            dve.scalar_tensor_tensor(REC1[:, :, 0].bitcast(I32), src_f[:, 0:C], float(NREL), t4_i[:, 0:C], ALU.mult, ALU.add)
            dve.tensor_copy(REC1[:, :, 1], dst_f[:, 0:C])
            dve.tensor_copy(REC0[:, :, 0].bitcast(I32), src_i[:, 0:C])
            dve.tensor_copy(REC0[:, :, 1], dst_f[:, 0:C])
            dve.memset(REC0[:, :, R0 - 1], 1.0)
            dve.drain().then_inc(rec1_ready, 1)

            def one_hots(g, r, waits):
                dve.wait_ge(bc_ld[r], waits)
                for s in range(2):
                    dve.wait_ge(looked_up, g * 2 + s + 1)
                    dve.tensor_scalar(OT[:, r * 2 + s, :], BC[:, r, s, :], m.iota_k[:, 0:1], None, ALU.is_equal).then_inc(ot_ready, 1)
                    dve.tensor_tensor(MINE[:, r * 2 + s, :, :], m.iota_f[:, 0:NT].unsqueeze(1).to_broadcast((P, CG, NT)),
                                      tile_f[:, s, bass.ds(g * CG, CG)].unsqueeze(2).to_broadcast((P, CG, NT)), ALU.is_equal).then_inc(mine_ready, 1)
                dve.drain().then_inc(bc_free, 1)

            def collect(g, r):
                for s, out in enumerate((SC, FW)):
                    dve.wait_ge(chosen, g * 2 + s + 1)
                    dve.tensor_reduce(out[:, :, bass.ds(g * CG, CG)].rearrange("p h c -> p c h"),
                                      FOUND[r * 2 + s].rearrange("p (c k h) -> p c h k", c=CG, k=NT), AX.X, ALU.add).then_inc(found_free, 1)

            one_hots(0, 0, 32)
            with dve.Fori(0, NCG // 2) as i:
                for r in range(2):
                    one_hots(i * 2 + r + 1, 1 - r, i * 32 + 32 * (r + 1))
                    collect(i * 2 + r, r)
            collect(NCG - 1, 0)
            dve.drain()
            dve.tensor_tensor(SC, SC, FW, ALU.add)
            dve.drain()
            dve.scalar_tensor_tensor(SC, SC, NEG_SLOPE, SC, ALU.mult, ALU.max)
            dve.drain()
            dve.tensor_tensor(SC, SC, MUL, ALU.mult)
            dve.drain()

            def segment_max(first, last):
                for h in range(H):
                    dve.tensor_tensor_scan(FW[:, h, 0:C], same[:, 0:C], SC[:, h, 0:C], first(h), ALU.mult, ALU.max)
                dve.drain()
                for h in range(H):
                    dve.tensor_tensor_scan(MUL[:, h, 0:C][:, ::-1], same[:, 1:C + 1][:, ::-1], FW[:, h, 0:C][:, ::-1],
                                           last(h), ALU.mult, ALU.max)
                dve.drain()

            segment_max(lambda h: 0.0, lambda h: 0.0)
            dve.tensor_copy(lv_in[:, 0, :], MUL[:, :, 0])
            dve.tensor_copy(lv_in[:, 1, :], FW[:, :, C - 1])
            dve.tensor_copy(lv_in[:, 2, :], dst_f[:, 0:1].to_broadcast((P, H)))
            dve.tensor_copy(lv_in[:, 3, :], dst_f[:, C - 1:C].to_broadcast((P, H)))
            dve.memset(lv_same, 0.0)
            dve.drain().then_inc(lv_ready, 1)
            dve.wait_ge(lv_ps, 1)
            for n in range(4):
                dve.tensor_copy(lv[0:H, n // 2, :, n % 2], PS[3][0:H, n * P:(n + 1) * P])
            dve.drain()
            val, key, fwd, bwd = (lv[0:H, n, :, :].rearrange("h e s -> h (e s)") for n in range(4))
            dve.tensor_tensor(lv_same[:, 1:2 * P], key[:, 1:2 * P], key[:, 0:2 * P - 1], ALU.is_equal)
            dve.drain()
            dve.tensor_tensor_scan(fwd, lv_same[:, 0:2 * P], val, 0.0, ALU.mult, ALU.max)
            dve.drain()
            dve.tensor_tensor_scan(bwd[:, ::-1], lv_same[:, 1:2 * P + 1][:, ::-1], fwd[:, ::-1], 0.0, ALU.mult, ALU.max).then_inc(lv_done, 1)
            dve.wait_ge(gb_ps, 1)
            dve.tensor_copy(g_first, PS[2][:, 0:H])
            dve.tensor_copy(g_last, PS[2][:, H:2 * H])
            dve.drain()
            segment_max(lambda h: g_first[:, h:h + 1], lambda h: g_last[:, h:h + 1])
            dve.tensor_tensor(FW, SC, MUL, ALU.subtract)
            dve.drain().then_inc(diff, 1)

        @block.scalar
        def _(act):
            def copy(g, b):
                act.wait_ge(looked_up, UNITS + g * 2 + b % 2 + 1)
                act.wait_ge(found_free, g * 2 + b % 2 + 1)
                for n in range(2):
                    act.copy(FOUND[b][:, n * BANK * NT * H:(n + 1) * BANK * NT * H], PS[2 * b + n][:, 0:BANK * NT * H])
                act.drain().then_inc(copied, 1)

            with act.Fori(0, NCG // 2) as i:
                for b in range(UNITS):
                    copy(i * 2 + b // 2, b)
            for b in range(2):
                copy(NCG - 1, b)
            act.wait_ge(diff, 1)
            act.activation(REC0[:, :, 2:2 + H].rearrange("p c h -> p h c"), FW[:, :, 0:C], ACT.Exp).then_inc(rec_ready, 1)

        @block.tensor
        def _(pe):
            pe.sem_inc(looked_up, UNITS)
            pe.sem_inc(copied, UNITS)

            def look_up(g, b):
                pe.wait_ge(ot_ready, g * 2 + b % 2 + 1)
                pe.wait_ge(copied, g * 2 + b % 2 + 1)
                for c in range(CG):
                    at = c % BANK * NT * H
                    for part in range(PARTS):
                        ins = pe.matmul(PS[2 * b + c // BANK][:, at:at + NT * H], OT[:, b, c * P:(c + 1) * P],
                                        m.TAB[:, b % 2, part, :, :].rearrange("p t h -> p (t h)"),
                                        start=(part == 0), stop=(part == PARTS - 1))
                ins.then_inc(looked_up, 1)

            with pe.Fori(0, NCG // 2) as i:
                for b in range(UNITS):
                    look_up(i * 2 + b // 2, b)
            for b in range(2):
                look_up(NCG - 1, b)
            pe.wait_ge(lv_ready, 1)
            for n in range(4):
                ins = pe.transpose(PS[3][0:H, n * P:(n + 1) * P], lv_in[:, n, :], m.ident[:, :])
            ins.then_inc(lv_ps, 1)
            pe.wait_ge(lv_done, 1)
            for n in range(2):
                ins = pe.transpose(PS[2][:, n * H:(n + 1) * H], lv[0:H, 3, :, n], m.ident[0:H, 0:H])
            ins.then_inc(gb_ps, 1)


def messages(nc, m, tag, rec, R, table, weighted, load_next):
    PS, sem = m.PS, m.sem
    take = carver(m, WBYTES // 4)
    G = take(RING * CJ * D).rearrange("p (r j d) -> p r j d", r=RING, j=CJ)
    OH = take(RING * CJ * P).rearrange("p (r j d) -> p r j d", r=RING, j=CJ)
    RC = take(RING * CJ * R).rearrange("p (r j c) -> p r j c", r=RING, j=CJ)
    DR = take(RING * CJ).rearrange("p (r j) -> p r j", r=RING)
    rec_ld = [sem(f"{tag}_rec_ld{i}") for i in range(RING)]
    g_ld = [sem(f"{tag}_g_ld{i}") for i in range(RING)]
    msg_ready, slot_free, oh_ready, ps_free = (sem(f"{tag}_{n}") for n in ("msg_ready", "slot_free", "oh_ready", "ps_free"))
    next_ld = sem(f"{tag}_next_ld")
    gather_steps = sem(f"{tag}_gather_steps")
    ROUNDS = STEPS // RING
    assert STEPS % RING == 0
    SELF_FROM, SELF_TO = ROUNDS // 3, ROUNDS // 3 + NT
    assert SELF_TO < ROUNDS and RING == KD
    if not weighted:
        WS, XA = self_arrays(m)
        self_in, self_ps, self_used = (sem(f"{tag}_{n}") for n in ("self_in", "self_ps", "self_used"))

    with nc.Block() as block:
        @block.sync
        def _(sp):
            with sp.Fori(0, ROUNDS) as i:
                for r in range(RING):
                    off = sp.value_load(m.step_off[0:1, bass.ds(i * RING + r, 1)], min_val=0, max_val=EP)
                    sp.wait_ge(slot_free, i * RING + r + 1)
                    sp.dma_start(RC[:, r, :, :].rearrange("p j c -> p (j c)"),
                                 rec[bass.ds(off, CHUNK), :].rearrange("(p j) c -> p (j c)", j=CJ)).then_inc(rec_ld[r], 16)

        @block.gpsimd
        def _(pool):
            with pool.Fori(0, ROUNDS) as i:
                for r in range(RING):
                    pool.wait_ge(rec_ld[r], i * 16 + 16)
                    pool.sem_inc(gather_steps, 1)
                    for j in range(CJ):
                        pool.indirect_dma_start(G[:, r, j, :], None, table,
                                                bass.IndirectOffsetOnAxis(ap=RC[:, r, j, 0:1].bitcast(I32), axis=0)).then_inc(g_ld[r], 16)

        @block.vector
        def _(dve):
            def front(i, r):
                dve.wait_ge(slot_free, i * RING + r + 1)
                dve.wait_ge(rec_ld[r], i * 16 + 16)
                dve.tensor_scalar(DR[:, r, :], RC[:, r, :, 1], m.woff[:, bass.ds(i * RING + r, 1)], None, ALU.subtract)
                dve.drain()
                dve.tensor_tensor(OH[:, r, :, :], m.iota_f[:, :].unsqueeze(1).to_broadcast((P, CJ, P)),
                                  DR[:, r, :].unsqueeze(2).to_broadcast((P, CJ, P)), ALU.is_equal).then_inc(oh_ready, 1)
                if weighted:
                    dve.wait_ge(g_ld[r], i * 16 * CJ + 16 * CJ)
                    g = G[:, r, :, :].rearrange("p j (h d) -> p j h d", h=H)
                    dve.tensor_tensor(g, g, RC[:, r, :, 2:2 + H].unsqueeze(3).to_broadcast((P, CJ, H, HD)), ALU.mult).then_inc(msg_ready, 1)

            def back(i, r):
                win = dve.value_load(m.step_win[0:1, bass.ds(i * RING + r, 1)], min_val=0, max_val=NT - 1)
                dve.wait_ge(slot_free, i * RING + r + RING + 1)
                dve.tensor_tensor(tile(m.ACC, win), tile(m.ACC, win), PS[r][:, :], ALU.add)
                if weighted:
                    dve.tensor_tensor(tile(m.ASUM, win), tile(m.ASUM, win), PS[RING + r][:, 0:H + 1], ALU.add)
                dve.drain().then_inc(ps_free, 1)

            LAG = 2
            dve.sem_inc(ps_free, RING)
            for r in range(LAG):
                front(0, r)

            def round_(i):
                for r in range(RING):
                    front(i + (r + LAG) // RING, (r + LAG) % RING)
                    back(i, r)

            if weighted:
                with dve.Fori(0, ROUNDS - 1) as i:
                    round_(i)
            else:
                dve.sem_inc(self_used, ONE)
                with dve.Fori(0, SELF_FROM) as i:
                    round_(i)
                with dve.Fori(0, NT) as n:
                    round_(n + SELF_FROM)
                    dve.wait_ge(self_ps, ONE + n + 1)
                    dve.tensor_tensor(tile(m.RES, n), tile(m.RES, n), PS[RING][:, :], ALU.add).then_inc(self_used, 1)
                with dve.Fori(SELF_TO, ROUNDS - 1) as i:
                    round_(i)
            for r in range(RING):
                if r + LAG < RING:
                    front(ROUNDS - 1, r + LAG)
                back(ROUNDS - 1, r)

        @block.scalar
        def _(act):
            load_next(m, act, next_ld, lambda n: act.wait_ge(slot_free, RING + 2 + 2 * n))
            if not weighted:
                with act.Fori(0, NT) as n:
                    act.wait_ge(self_ps, ONE + n)
                    act.copy(m.XT[:, :, 0:P], XA[:, :, bass.ds(n * P, P)]).then_inc(self_in, 1)

        @block.tensor
        def _(pe):
            pe.sem_inc(slot_free, RING)

            def self_product(n, k):
                if k == 0:
                    pe.wait_ge(self_in, n + 1)
                    pe.wait_ge(self_used, ONE + n)
                ins = pe.matmul(PS[RING][:, :], m.XT[:, k, 0:P], WS[:, k, :], start=(k == 0), stop=(k == KD - 1))
                if k == KD - 1:
                    ins.then_inc(self_ps, 1)

            def round_(i, n=None):
                for r in range(RING):
                    pe.wait_ge(oh_ready, i * RING + r + 1)
                    if weighted:
                        pe.wait_ge(msg_ready, i * RING + r + 1)
                    else:
                        pe.wait_ge(g_ld[r], i * 16 * CJ + 16 * CJ)
                    pe.wait_ge(ps_free, i * RING + r + 1)
                    for j in range(CJ):
                        if weighted:
                            pe.matmul(PS[RING + r][:, 0:H + 1], OH[:, r, j, :], RC[:, r, j, 2:R], start=(j == 0), stop=(j == CJ - 1))
                        ins = pe.matmul(PS[r][:, :], OH[:, r, j, :], G[:, r, j, :], start=(j == 0), stop=(j == CJ - 1))
                    ins.then_inc(slot_free, 1)
                    if n is not None:
                        self_product(n, r)

            if weighted:
                with pe.Fori(0, ROUNDS) as i:
                    round_(i)
            else:
                pe.sem_inc(self_ps, ONE)
                with pe.Fori(0, SELF_FROM) as i:
                    round_(i)
                with pe.Fori(0, NT) as n:
                    round_(n + SELF_FROM, n)
                with pe.Fori(SELF_TO, ROUNDS) as i:
                    round_(i)


class Norms:

    def __init__(self, m, tag):
        self.m = m
        self.var_ready, self.rstd_ready = m.sem(tag + "_var_ready"), m.sem(tag + "_rstd_ready")

    def stats(self, dve, n, tiles):
        m = self.m
        for j, x in enumerate(tiles):
            dve.bn_stats(m.stats[:, j, :], x)
        dve.drain()
        for j in range(len(tiles)):
            dve.bn_aggr(m.mv[:, j, :], m.stats[:, j, :])
        dve.drain().then_inc(self.var_ready, 1)
        dve.wait_ge(self.rstd_ready, n + 1)

    def apply(self, dve, out, x):
        m = self.m
        for j in range(len(x)):
            dve.tensor_scalar(out[j], x[j], m.mv[:, j, 0:1], m.rstd[:, j:j + 1], ALU.subtract, ALU.mult)
        dve.drain()

    def roots(self, pool, count):
        m = self.m
        with pool.Fori(0, count) as n:
            pool.wait_ge(self.var_ready, n + 1)
            pool.tensor_tensor(m.sd[:, 0:GT], m.mv[:, 0:GT, 1], m.eps[:, 0:1].to_broadcast((P, GT)), ALU.add)
            pool.drain()
            pool.tensor_tensor(m.rstd[:, 0:GT], m.sd[:, 0:GT], m.half[:, 0:GT], ALU.pow).then_inc(self.rstd_ready, 1)


def affine(dve, x, scale, shift):
    for a in x:
        dve.tensor_tensor(a, a, scale, ALU.mult)
    dve.drain()
    for a in x:
        dve.tensor_tensor(a, a, shift, ALU.add)
    dve.drain()


def expert_weights(m):
    take = carver(m)
    W1 = take(KD * NEXP * HID).rearrange("p (k n) -> p k n", k=KD)
    W2 = take(NEXP * HID // P * D).rearrange("p (k n) -> p k n", n=D)
    return W1, W2


def load_experts(m, eng, s, pace):
    W1, W2 = expert_weights(m)
    for k in range(KD):
        for half in range(2):
            e = slice(half * NEXP // 2, (half + 1) * NEXP // 2)
            pace(2 * k + half)
            eng.dma_start(W1[:, k, :].rearrange("p (e h) -> p e h", e=NEXP)[:, e, :],
                          m.t["L0_ffn_W1"].rearrange("e (k p) h -> k p e h", p=P)[k][:, e, :]).then_inc(s, 16)
    for e in range(NEXP):
        pace(2 * KD + e)
        eng.dma_start(W2[:, e * HID // P:(e + 1) * HID // P, :], m.t["L0_ffn_W2"][e].rearrange("(k p) n -> p k n", p=P)).then_inc(s, 16)
    eng.wait_ge(s, 16 * (2 * KD + NEXP))


def relation_input(dve, m, norms, n, g):
    X = [tile(m.X, g * GT + j) for j in range(GT)]
    norms.stats(dve, n, X)
    norms.apply(dve, [m.XS[:, j, :] for j in range(GT)], X)
    for j in range(GT):
        dve.tensor_tensor(tile(m.RES, g * GT + j), m.XS[:, j, :], m.rows["L1_gnn_self_b"], ALU.add)


def experts(nc, m):
    t, PS, sem = m.t, m.PS, m.sem
    MH = HID // P
    W1, W2 = expert_weights(m)
    take = carver(m, WBYTES // 4)
    HS = take(2 * MH * W2N).rearrange("p (r b n) -> p r b n", r=2, b=MH)
    WG = take(KD * NEXP).rearrange("p (k e) -> p k e", k=KD)
    B1 = take(NEXP * MH)
    B2 = take(D)[0:NEXP, :]
    O = take(GT * D).rearrange("p (j d) -> p j d", j=GT)
    lg = take(GT * NEXP).rearrange("p (j e) -> p j e", j=GT)
    pr = take(GT * NEXP).rearrange("p (j e) -> p j e", j=GT)
    top = take(GT * NEXP).rearrange("p (j e) -> p j e", j=GT)
    top_i = take(GT * NEXP).bitcast(U32).rearrange("p (j e) -> p j e", j=GT)
    idx = take(GT * NEXP).rearrange("p (j e) -> p j e", j=GT)
    hot = take(GT * NEXP).rearrange("p (j e) -> p j e", j=GT)
    conf = take(GT * NEXP).rearrange("p (j e) -> p j e", j=GT)
    conf_t = take(W2N)[0:NEXP, :]
    red = take(GT * 4).rearrange("p (j e) -> p j e", j=GT)
    rs = take(GT * H).rearrange("p (j e) -> p j e", j=GT)

    ld, xs_ready, xt_ps, xt_sb, lg_ps, lg_ready, pr_ready, conf_ready, ct_ps, ct_sb = (sem("s6_" + n) for n in (
        "ld", "xs_ready", "xt_ps", "xt_sb", "lg_ps", "lg_ready", "pr_ready", "conf_ready", "ct_ps", "ct_sb"))
    h_ps, h_sb, o_ps, o_used = (sem("s6_" + n) for n in ("h_ps", "h_sb", "o_ps", "o_used"))
    norms = Norms(m, "s6")
    PO = NEXP + 1

    with nc.Block() as block:
        @block.sync
        def _(sp):
            sp.dma_start(WG, t["L0_ffn_Wg"].rearrange("(k p) e -> p k e", p=P)).then_inc(ld, 16)
            sp.dma_start(B1, t["L0_ffn_b1_cols"]).then_inc(ld, 16)
            sp.dma_start(B2, t["L0_ffn_b2"]).then_inc(ld, 16)
            sp.wait_ge(ld, 48)

        FRONT = 3
        AFTER = (1, 3, 5)

        @block.vector
        def _(dve):
            dve.sem_inc(o_used, ONE)

            def tiles(b, g):
                return [tile(b, g * GT + j) for j in range(GT)]

            def front(g, part, n):
                A, R, X = tiles(m.ACC, g), tiles(m.RES, g), tiles(m.X, g)
                U, S = ([b[:, j, :] for j in range(GT)] for b in (m.U, m.XS))
                if part == 0:
                    for j in range(GT):
                        dve.tensor_scalar(rs[:, j, :], tile(m.ASUM, g * GT + j)[:, 0:H], 1e-10, None, ALU.add)
                    dve.drain()
                    dve.reciprocal(rs, rs)
                    dve.drain()
                    for j in range(GT):
                        a = A[j].rearrange("p (h d) -> p h d", h=H)
                        dve.tensor_tensor(a, a, over_heads(rs[:, j, :]), ALU.mult)
                    dve.drain()
                    for j in range(GT):
                        dve.tensor_tensor(A[j], A[j], R[j], ALU.add)
                    dve.drain()
                    norms.stats(dve, n, A)
                    norms.apply(dve, A, A)
                elif part == 1:
                    affine(dve, A, m.rows["L0_gnn_ln_gamma"], m.rows["L0_gnn_ln_beta"])
                    for j in range(GT):
                        dve.tensor_tensor(X[j], X[j], A[j], ALU.add)
                    dve.drain()
                    norms.stats(dve, n, X)
                    norms.apply(dve, U, X)
                else:
                    norms.stats(dve, n, U)
                    norms.apply(dve, S, U)
                    affine(dve, S, m.rows["L0_ffn_ln_g"], m.rows["L0_ffn_ln_b"])
                    dve.drain().then_inc(xs_ready, 1)

            def route(g):
                dve.wait_ge(lg_ps, g + 1)
                dve.tensor_reduce(red[:, :, 0:1], PS[0][:, 0:GT * NEXP].rearrange("p (j e) -> p j e", j=GT), AX.X, ALU.max)
                dve.drain()
                dve.tensor_tensor(lg, PS[0][:, 0:GT * NEXP].rearrange("p (j e) -> p j e", j=GT),
                                  red[:, :, 0:1].to_broadcast((P, GT, NEXP)), ALU.subtract)
                dve.drain().then_inc(lg_ready, 1)
                dve.wait_ge(pr_ready, g + 1)
                dve.tensor_reduce(red[:, :, 1:2], pr, AX.X, ALU.add)
                dve.drain()
                dve.reciprocal(red[:, :, 2:3], red[:, :, 1:2])
                dve.drain()
                dve.tensor_tensor(pr, pr, red[:, :, 2:3].to_broadcast((P, GT, NEXP)), ALU.mult)
                dve.drain()
                for j in range(GT):
                    dve.max(top[:, j, :], pr[:, j, :])
                dve.drain()
                for j in range(GT):
                    dve.max_index(top_i[:, j, :], top[:, j, :], pr[:, j, :])
                dve.tensor_reduce(red[:, :, 0:1], top[:, :, 0:2], AX.X, ALU.add)
                dve.drain()
                dve.reciprocal(red[:, :, 1:2], red[:, :, 0:1])
                dve.tensor_copy(idx, top_i)
                dve.drain()
                dve.tensor_tensor(top[:, :, 0:2], top[:, :, 0:2], red[:, :, 1:2].to_broadcast((P, GT, 2)), ALU.mult)
                dve.drain()
                for j in range(GT):
                    dve.tensor_scalar(conf[:, j, :], m.iota_f[:, 0:NEXP], idx[:, j, 0:1], top[:, j, 0:1], ALU.is_equal, ALU.mult)
                    dve.tensor_scalar(hot[:, j, :], m.iota_f[:, 0:NEXP], idx[:, j, 1:2], top[:, j, 1:2], ALU.is_equal, ALU.mult)
                dve.drain()
                dve.tensor_tensor(conf, conf, hot, ALU.add)
                dve.drain().then_inc(conf_ready, 1)
                dve.wait_ge(ct_ps, g + 1)
                dve.tensor_copy(conf_t, PS[1][0:NEXP, 0:W2N]).then_inc(ct_sb, 1)

            def group(g, n, last):
                route(g)
                out = [O[:, j, :] for j in range(GT)]
                for e in range(PO):
                    dve.wait_ge(o_ps, ONE + g * PO + e + 1)
                    for j in range(GT):
                        ps = PS[4 + 2 * (e % 2) + j][:, :]
                        if e < NEXP:
                            dve.scalar_tensor_tensor(out[j], ps, conf[:, j, e:e + 1], m.U[:, j, :] if e == 0 else out[j], ALU.mult, ALU.add)
                        else:
                            dve.tensor_tensor(out[j], out[j], ps, ALU.add)
                    dve.drain().then_inc(o_used, 1)
                    if e in AFTER and not last:
                        front(g + 1, AFTER.index(e), n + AFTER.index(e))
                    if e == AFTER[0] and last:
                        relation_input(dve, m, norms, n, 0)
                norms.stats(dve, n + (1 if last else FRONT), out)
                norms.apply(dve, out, out)
                affine(dve, out, m.rows["L0_ffn_out_g"], m.rows["L0_ffn_out_b"])
                for x, o in zip(tiles(m.X, g), out):
                    dve.tensor_tensor(x, x, o, ALU.add)
                dve.drain()

            for part in range(FRONT):
                front(0, part, part)
            with dve.Fori(0, NG - 1) as g:
                group(g, FRONT + g * (FRONT + 1), False)
            group(NG - 1, FRONT + (NG - 1) * (FRONT + 1), True)

        @block.scalar
        def _(act):
            act.sem_inc(h_sb, ONE)
            act.wait_ge(ld, 48)

            def transposed(g):
                act.wait_ge(xt_ps, ONE + g * GT + GT)
                for j in range(GT):
                    act.copy(m.XT[:, :, j * P:(j + 1) * P], PS[j][:, :].rearrange("p (k n) -> p k n", k=KD))
                act.drain().then_inc(xt_sb, 1)

            def group(g, last):
                act.wait_ge(lg_ready, g + 1)
                act.activation(pr, lg, ACT.Exp).then_inc(pr_ready, 1)
                for e in range(NEXP):
                    act.wait_ge(h_ps, g * NEXP + e + 1)
                    act.wait_ge(o_ps, ONE + g * PO + max(e - 1, 0))
                    for b in range(MH):
                        act.activation(HS[:, e % 2, b, :], PS[2 + e % 2][:, b * W2N:(b + 1) * W2N], ACT.Gelu_apprx_tanh,
                                       bias=B1[:, e * MH + b:e * MH + b + 1])
                    act.drain().then_inc(h_sb, 1)
                if not last:
                    transposed(g + 1)

            transposed(0)
            with act.Fori(0, NG - 1) as g:
                group(g, False)
            group(NG - 1, True)

        @block.gpsimd
        def _(pool):
            norms.roots(pool, NG * (FRONT + 1) + 1)

        @block.tensor
        def _(pe):
            pe.sem_inc(xt_ps, ONE)
            pe.sem_inc(o_ps, ONE)
            pe.wait_ge(ld, 48)

            def transposes(g):
                pe.wait_ge(xs_ready, g + 1)
                for j in range(GT):
                    for k in range(KD):
                        ins = pe.transpose(PS[j][:, k * P:(k + 1) * P], m.XS[:, j, k * P:(k + 1) * P], m.ident[:, :])
                    ins.then_inc(xt_ps, 1)

            def hidden(g, e):
                pe.wait_ge(h_sb, ONE + g * NEXP + max(e - 1, 0))
                for b in range(MH):
                    for k in range(KD):
                        at = e * HID + b * P
                        ins = pe.matmul(PS[2 + e % 2][:, b * W2N:(b + 1) * W2N], W1[:, k, at:at + P], m.XT[:, k, :],
                                        start=(k == 0), stop=(k == KD - 1))
                ins.then_inc(h_ps, 1)

            def output(g, e):
                pe.wait_ge(h_sb, ONE + g * NEXP + e + 1)
                pe.wait_ge(o_used, ONE + g * PO + max(e - 1, 0))
                for j in range(GT):
                    for b in range(MH):
                        ins = pe.matmul(PS[4 + 2 * (e % 2) + j][:, :], HS[:, e % 2, b, j * P:(j + 1) * P], W2[:, e * MH + b, :],
                                        start=(b == 0), stop=(b == MH - 1))
                ins.then_inc(o_ps, 1)

            def group(g, last):
                pe.wait_ge(xt_sb, g + 1)
                for j in range(GT):
                    for k in range(KD):
                        ins = pe.matmul(PS[0][:, j * NEXP:(j + 1) * NEXP], m.XT[:, k, j * P:(j + 1) * P], WG[:, k, :],
                                        start=(k == 0), stop=(k == KD - 1))
                ins.then_inc(lg_ps, 1)
                hidden(g, 0)
                for e in range(NEXP):
                    if e + 1 < NEXP:
                        hidden(g, e + 1)
                    if e == 1:
                        pe.wait_ge(conf_ready, g + 1)
                        for j in range(GT):
                            ins = pe.transpose(PS[1][0:NEXP, j * P:(j + 1) * P], conf[:, j, :], m.ident[:, :])
                        ins.then_inc(ct_ps, 1)
                    if e == NEXP - 1:
                        pe.wait_ge(ct_sb, g + 1)
                        if not last:
                            transposes(g + 1)
                    output(g, e)
                pe.wait_ge(o_used, ONE + g * PO + NEXP - 1)
                for j in range(GT):
                    ins = pe.matmul(PS[4 + j][:, :], conf_t[:, j * P:(j + 1) * P], B2, start=True, stop=True)
                ins.then_inc(o_ps, 1)

            transposes(0)
            with pe.Fori(0, NG - 1) as g:
                group(g, False)
            group(NG - 1, True)


def self_arrays(m):
    take = carver(m, KD * FF + FF // P * D, WBYTES // 4)
    return take(KD * D).rearrange("p (k n) -> p k n", k=KD), take(KD * NP).rearrange("p (k n) -> p k n", k=KD)


def relations(nc, m):
    t, PS, sem = m.t, m.PS, m.sem
    WR = carver(m, end=KD * FF + FF // P * D)(KD * NREL * D).rearrange("p (k n) -> p k n", k=KD)
    WS, XA = self_arrays(m)
    take = carver(m, WBYTES // 4)
    RB = take(NREL * D)
    STG = take(GT * NREL * D).rearrange("p (j n) -> p j n", j=GT)
    b_ld, xs_ready, xt_ps, xt_sb, ps_ready, ps_used, rows_dr = (sem("s7_" + n) for n in (
        "b_ld", "xs_ready", "xt_ps", "xt_sb", "ps_ready", "ps_used", "rows_dr"))
    norms = Norms(m, "s7")
    PB = 4
    assert GT * NREL % PB == 0
    w_ld = [sem(f"s7_w_ld{r}") for r in range(NREL + 1)]

    with nc.Block() as block:
        @block.sync
        def _(sp):
            sp.sem_inc(rows_dr, ONE)
            for r in range(NREL):
                sp.dma_start(WR[:, :, r * D:(r + 1) * D], t["L1_gnn_rel_W"][r].rearrange("(k p) f -> p k f", p=P)).then_inc(w_ld[r], 16)
                if r == 0:
                    sp.dma_start(RB, t["L1_gnn_rel_b"].rearrange("r f -> (r f)").partition_broadcast(P)).then_inc(b_ld, 16)
            sp.dma_start(WS, t["L1_gnn_self_W"].rearrange("(k p) f -> p k f", p=P)).then_inc(w_ld[NREL], 16)
            with sp.Fori(0, NG) as g:
                for j in range(GT):
                    sp.wait_ge(ps_used, PB + (g * GT + j + 1) * NREL)
                    sp.dma_start(m.rel_rows[bass.ds((g * GT + j) * P * NREL, P * NREL), :].rearrange("(p r) f -> p (r f)", r=NREL),
                                 STG[:, j, :]).then_inc(rows_dr, 16)
            sp.wait_ge(rows_dr, ONE + 16 * NT)
            sp.wait_ge(w_ld[NREL], 16)

        @block.vector
        def _(dve):
            dve.sem_inc(ps_used, PB)

            def group(g, last):
                for j in range(GT):
                    dve.wait_ge(rows_dr, ONE + g * 16 * GT)
                    for r in range(NREL):
                        n = j * NREL + r
                        dve.wait_ge(ps_ready, g * GT * NREL + n + 1)
                        dve.tensor_tensor(STG[:, j, r * D:(r + 1) * D], PS[2 + n % PB][:, :], RB[:, r * D:(r + 1) * D], ALU.add).then_inc(ps_used, 1)
                    if j == 0 and not last:
                        relation_input(dve, m, norms, g, g + 1)
                        dve.drain().then_inc(xs_ready, 1)

            dve.sem_inc(xs_ready, 1)
            dve.memset(m.ACC[:, :, :], 0.0)
            dve.wait_ge(b_ld, 16)
            with dve.Fori(0, NG - 1) as g:
                group(g, False)
            group(NG - 1, True)

        @block.scalar
        def _(act):
            def group(g):
                act.wait_ge(xt_ps, g + 1)
                for j in range(GT):
                    act.copy(m.XT[:, :, j * P:(j + 1) * P], PS[j][:, :].rearrange("p (k n) -> p k n", k=KD))
                act.drain().then_inc(xt_sb, 1)
                for j in range(GT):
                    act.copy(XA[:, :, bass.ds((g * GT + j) * P, P)], m.XT[:, :, j * P:(j + 1) * P])
                act.drain()

            with act.Fori(0, NG) as g:
                group(g)

        @block.gpsimd
        def _(pool):
            norms.roots(pool, NG - 1)

        @block.tensor
        def _(pe):
            def transposes(g):
                pe.wait_ge(xs_ready, g + 1)
                for j in range(GT):
                    for k in range(KD):
                        ins = pe.transpose(PS[j][:, k * P:(k + 1) * P], m.XS[:, j, k * P:(k + 1) * P], m.ident[:, :])
                ins.then_inc(xt_ps, 1)

            def group(g, last):
                pe.wait_ge(xt_sb, g + 1)
                for j in range(GT):
                    for r in range(NREL):
                        n = j * NREL + r
                        pe.wait_ge(w_ld[r], 16)
                        pe.wait_ge(ps_used, g * GT * NREL + n + 1)
                        for k in range(KD):
                            ins = pe.matmul(PS[2 + n % PB][:, :], m.XT[:, k, j * P:(j + 1) * P], WR[:, k, r * D:(r + 1) * D], start=(k == 0), stop=(k == KD - 1))
                        ins.then_inc(ps_ready, 1)
                if not last:
                    transposes(g + 1)

            transposes(0)
            with pe.Fori(0, NG - 1) as g:
                group(g, False)
            group(NG - 1, True)


def ffn_weights(m):
    take = carver(m)
    W1 = take(KD * FF).rearrange("p (k n) -> p k n", k=KD)
    W2 = take(FF // P * D).rearrange("p (k n) -> p k n", n=D)
    return W1, W2


def load_ffn(m, eng, s, pace):
    W1, W2 = ffn_weights(m)
    for k in range(KD):
        pace(k)
        eng.dma_start(W1[:, k, :], m.t["L1_gnn_W1"][k * P:(k + 1) * P, :]).then_inc(s, 16)
    for k in range(0, FF // P, 2):
        pace(KD + k // 2)
        eng.dma_start(W2[:, k:k + 2, :], m.t["L1_gnn_W2"][k * P:(k + 2) * P, :].rearrange("(k p) n -> p k n", p=P)).then_inc(s, 16)
    eng.wait_ge(s, 16 * (KD + FF // P // 2))


def ffn(nc, m):
    t, PS, sem = m.t, m.PS, m.sem
    MB = 2
    NQ = FF // P // MB
    W1, W2 = ffn_weights(m)
    take = carver(m, WBYTES // 4)
    HS = take(2 * MB * W2N).rearrange("p (r b n) -> p r b n", r=2, b=MB)
    B1 = take(FF // P)
    deg = take(NT)
    Y = take(GT * D).rearrange("p (j d) -> p j d", j=GT)
    ld, xs_ready, xt_ps, xt_sb, h_ps, h_sb, o_ps, o_used = (sem("s9_" + n) for n in (
        "ld", "xs_ready", "xt_ps", "xt_sb", "h_ps", "h_sb", "o_ps", "o_used"))
    norms = Norms(m, "s9")
    next_ld, next_zero = sem("s9_next_ld"), sem("s9_next_zero")

    with nc.Block() as block:
        @block.sync
        def _(sp):
            sp.dma_start(B1, t["L1_gnn_b1_cols"]).then_inc(ld, 16)
            sp.wait_ge(ld, 16)
            sp.wait_ge(next_zero, 1)
            load_nibbles(m, sp, next_ld)

        @block.gpsimd
        def _(pool):
            for w in nibble_weights(m)[2:]:
                pool.memset(w, 0.0)
            pool.drain().then_inc(next_zero, 1)
            norms.roots(pool, NG * 3)

        @block.vector
        def _(dve):
            dve.sem_inc(o_used, ONE)

            def front(g, n):
                S = [m.XS[:, j, :] for j in range(GT)]
                for j in range(GT):
                    dve.scalar_tensor_tensor(S[j], tile(m.ACC, g * GT + j), deg[:, bass.ds(g * GT + j, 1)], tile(m.RES, g * GT + j), ALU.mult, ALU.add)
                dve.drain()
                norms.stats(dve, n, S)
                norms.apply(dve, S, S)
                affine(dve, S, m.rows["L1_gnn_ln1_w"], m.rows["L1_gnn_ln1_b"])
                dve.drain().then_inc(xs_ready, 1)
                for j in range(GT):
                    dve.tensor_tensor(tile(m.RES, g * GT + j), S[j], m.rows["L1_gnn_b2"], ALU.add)
                dve.drain()

            def back(g, n):
                O = [Y[:, j, :] for j in range(GT)]
                dve.wait_ge(o_ps, g + 1)
                for j in range(GT):
                    dve.tensor_tensor(O[j], tile(m.RES, g * GT + j), PS[4 + j][:, :], ALU.add)
                dve.drain().then_inc(o_used, 1)
                norms.stats(dve, n, O)
                norms.apply(dve, O, O)
                affine(dve, O, m.rows["L1_gnn_ln2_w"], m.rows["L1_gnn_ln2_b"])
                for j in range(GT):
                    dve.tensor_tensor(tile(m.X, g * GT + j), tile(m.X, g * GT + j), O[j], ALU.add)
                dve.drain()
                X = [tile(m.X, g * GT + j) for j in range(GT)]
                norms.stats(dve, n + 1, X)
                norms.apply(dve, [tile(m.RES, g * GT + j) for j in range(GT)], X)

            dve.tensor_scalar(deg, m.ASUM[:, :, H], 1.0, None, ALU.max)
            dve.drain()
            dve.reciprocal(deg, deg)
            dve.drain()
            front(0, 0)
            with dve.Fori(0, NG - 1) as g:
                dve.wait_ge(xt_ps, g + 1)
                front(g + 1, g * 3 + 1)
                back(g, g * 3 + 2)
            back(NG - 1, NG * 3 - 2)

        @block.scalar
        def _(act):
            act.sem_inc(h_sb, ONE)
            act.wait_ge(ld, 16)

            def transposed(g):
                act.wait_ge(xt_ps, g + 1)
                for j in range(GT):
                    act.copy(m.XT[:, :, j * P:(j + 1) * P], PS[j][:, :].rearrange("p (k n) -> p k n", k=KD))
                act.drain().then_inc(xt_sb, 1)

            def group(g, last):
                for q in range(NQ):
                    act.wait_ge(h_ps, g * NQ + q + 1)
                    for b in range(MB):
                        act.activation(HS[:, q % 2, b, :], PS[2 + q % 2][:, b * W2N:(b + 1) * W2N], ACT.Gelu,
                                       bias=B1[:, q * MB + b:q * MB + b + 1])
                    act.drain().then_inc(h_sb, 1)
                if not last:
                    transposed(g + 1)

            transposed(0)
            with act.Fori(0, NG - 1) as g:
                group(g, False)
            group(NG - 1, True)

        @block.tensor
        def _(pe):
            def transposes(g):
                pe.wait_ge(xs_ready, g + 1)
                for j in range(GT):
                    for k in range(KD):
                        ins = pe.transpose(PS[j][:, k * P:(k + 1) * P], m.XS[:, j, k * P:(k + 1) * P], m.ident[:, :])
                ins.then_inc(xt_ps, 1)

            def hidden(g, q):
                pe.wait_ge(h_sb, ONE + g * NQ + max(q - 1, 0))
                for b in range(MB):
                    at = (q * MB + b) * P
                    for k in range(KD):
                        ins = pe.matmul(PS[2 + q % 2][:, b * W2N:(b + 1) * W2N], W1[:, k, at:at + P], m.XT[:, k, :],
                                        start=(k == 0), stop=(k == KD - 1))
                ins.then_inc(h_ps, 1)

            def group(g, last):
                pe.wait_ge(xt_sb, g + 1)
                hidden(g, 0)
                hidden(g, 1)
                pe.wait_ge(o_used, ONE + g)
                for q in range(NQ):
                    pe.wait_ge(h_sb, ONE + g * NQ + q + 1)
                    for b in range(MB):
                        for j in range(GT):
                            ins = pe.matmul(PS[4 + j][:, :], HS[:, q % 2, b, j * P:(j + 1) * P], W2[:, q * MB + b, :],
                                            start=(q == 0 and b == 0), stop=(q == NQ - 1 and b == MB - 1))
                    if q == NQ - 1:
                        ins.then_inc(o_ps, 1)
                    if q + 2 < NQ:
                        hidden(g, q + 2)
                    elif q + 2 == NQ and not last:
                        transposes(g + 1)

            transposes(0)
            with pe.Fori(0, NG - 1) as g:
                group(g, False)
            group(NG - 1, True)


ALU_LO, ALU_HI, AX_LO, AX_HI = 16, 32, 48, 64
OPC_ADD, OPC_SUB, OPCODE_BASE, OP_START = 25, 26, 80, 10
OUTPUT_LO, OUTPUT_HI, CARRY = 128, 144, 160
NF = 4
MARK_AX, OP_ADD, OP_SUB = 0, 1, 2


REM = GE - P
NIB_AT = 20 * 1024


def nibble_weights(m):
    take = carver(m, NIB_AT)
    W0 = take(2 * P)[0:NF, :].rearrange("p (a n) -> p a n", a=2)
    W0r = take(2 * REM)[0:NF, :]
    W1aa = take(2 * P).rearrange("p (a n) -> p a n", a=2)
    W1ar = take(2 * 2 * REM).rearrange("p (a n) -> p a n", a=2)
    W1ra = take(2 * P)[0:2 * REM, :].rearrange("p (a n) -> p a n", a=2)
    W1rr = take(2 * REM)[0:2 * REM, :]
    W2a = take(2 * 2)
    W2r = take(2 * 2)[0:2 * REM, :]
    Ba = take(2 * 2).rearrange("p (a n) -> p a n", a=2)
    Br = take(2)[0:2 * REM, :]
    BO = take(2 * 2).rearrange("p (a n) -> p a n", a=2)
    return W0, W0r, W1aa, W1ar, W1ra, W1rr, W2a, W2r, Ba, Br, BO


def load_nibbles(m, eng, s):
    t = m.t
    W0, W0r, W1aa, W1ar, W1ra, W1rr, W2a, W2r, Ba, Br, BO = nibble_weights(m)
    for a, (w, b) in enumerate((("L1_ffn_Wa", "L1_ffn_ba"), ("L1_ffn_Ws", "L1_ffn_bs"))):
        wt, bc = t[w + "_T"], t[b + "_cols"]
        r = slice(a * REM, (a + 1) * REM)
        for to, lo in ((slice(0, 2), 0), (slice(2, 4), OP_START + OPC_ADD)):
            eng.dma_start(W0[to, a, :], wt[0, lo:lo + 2, 0:P]).then_inc(s, 16)
            eng.dma_start(W0r[to, r], wt[0, lo:lo + 2, P:GE]).then_inc(s, 16)
        eng.dma_start(W1aa[:, a, :], wt[1, 0:P, 0:P]).then_inc(s, 16)
        eng.dma_start(W1ar[:, a, r], wt[1, 0:P, P:GE]).then_inc(s, 16)
        eng.dma_start(W1ra[r, a, :], wt[1, P:GE, 0:P]).then_inc(s, 16)
        eng.dma_start(W1rr[r, r], wt[1, P:GE, P:GE]).then_inc(s, 16)
        eng.dma_start(W2a[:, a * 2:a * 2 + 2], wt[2, 0:P, 100:102]).then_inc(s, 16)
        eng.dma_start(W2r[r, a * 2:a * 2 + 2], wt[2, P:GE, 100:102]).then_inc(s, 16)
        eng.dma_start(Ba[:, a, :], bc[0:P, 0:2]).then_inc(s, 16)
        eng.dma_start(Br[r, :], bc[P:GE, 0:2]).then_inc(s, 16)
        eng.dma_start(BO[:, a, :], t[b][2, 100:102].partition_broadcast(P)).then_inc(s, 16)
    eng.wait_ge(s, 16 * 26)


def nibbles(nc, m):
    t, PS, sem = m.t, m.PS, m.sem
    W0, W0r, W1aa, W1ar, W1ra, W1rr, W2a, W2r, Ba, Br, BO = nibble_weights(m)
    take = carver(m)
    Y = m.RES
    desc = take(16)
    gt = take(NT * 64).rearrange("p (t n) -> p t n", t=NT)
    nib = take(NT * 4).rearrange("p (t n) -> p t n", t=NT)
    msk = take(NT * 4).rearrange("p (t n) -> p t n", t=NT)
    FT = take(NT * 2 * NF).rearrange("p (t s f) -> p t s f", t=NT, s=2)
    mark, op_add, op_sub, adds, subs, active, active2, both = (take(NT).rearrange("p (t n) -> p t n", t=NT) for _ in range(8))
    FG = take(2 * NF).rearrange("p (s f) -> p s f", s=2)
    FS = take(2 * P)[0:NF, :]
    H1a = take(4 * P)
    H1r = take(2 * P)[0:2 * REM, :]
    H2a = take(4 * P)
    H2r = take(2 * P)[0:2 * REM, :]
    RW = 2 * 2 * 2
    res = take(NT * RW)
    y = take(NT * 4).rearrange("p (q n) -> p q n", n=2)
    y2 = take(NT * 4).rearrange("p (q n) -> p q n", n=2)
    oh = take(NT * 32).rearrange("p (t s n) -> p t s n", t=NT, s=2)

    desc_ready, f_in, f_ps, f_sb, h1_ps, h1_sb, h2_ps, h2_sb, y_ps, y_sb, out_ready, out_dr = (
        sem("s10_" + n) for n in ("desc_ready", "f_in", "f_ps", "f_sb", "h1_ps", "h1_sb", "h2_ps", "h2_sb",
                                 "y_ps", "y_sb", "out_ready", "out_dr"))

    with nc.Block() as block:
        @block.sync
        def _(sp):
            for i in range(NT):
                rows = P if i < NT - 1 else LAST
                sp.wait_ge(out_ready, i + 1)
                sp.dma_start(t["out"][i * P:i * P + rows, :], m.X[0:rows, i, :]).then_inc(out_dr, 16)
            sp.wait_ge(out_dr, 16 * NT)

        @block.gpsimd
        def _(pool):
            pool.iota(desc, [[-1, 16]], base=16, channel_multiplier=0, allow_small_or_imprecise_dtypes=True).then_inc(desc_ready, 1)

        @block.vector
        def _(dve):
            dve.wait_ge(desc_ready, 1)
            dve.tensor_scalar(gt, Y[:, :, ALU_LO:ALU_LO + 64], 0.5, None, ALU.is_gt)
            dve.tensor_scalar(mark, Y[:, :, MARK_AX:MARK_AX + 1], 0.5, None, ALU.is_gt)
            dve.tensor_scalar(op_add, Y[:, :, OP_ADD:OP_ADD + 1], 0.5, None, ALU.is_gt)
            dve.tensor_scalar(op_sub, Y[:, :, OP_SUB:OP_SUB + 1], 0.5, None, ALU.is_gt)
            dve.drain()
            q = gt.rearrange("p t (q n) -> p (t q) n", q=4)
            dve.tensor_tensor(q, q, desc.unsqueeze(1).to_broadcast((P, NT * 4, 16)), ALU.mult)
            dve.drain()
            dve.tensor_reduce(nib, gt.rearrange("p t (q n) -> p t q n", q=4), AX.X, ALU.max)
            dve.drain()
            dve.tensor_scalar(msk, nib, 0.0, None, ALU.is_gt)
            dve.tensor_scalar(nib, nib, -1.0, 16.0, ALU.mult, ALU.add)
            dve.drain()
            dve.tensor_tensor(nib, nib, msk, ALU.mult)
            dve.drain()
            for s in range(2):
                dve.tensor_copy(FT[:, :, s, 0:1], nib[:, :, s:s + 1])
                dve.tensor_copy(FT[:, :, s, 1:2], nib[:, :, 2 + s:3 + s])
                dve.tensor_copy(FT[:, :, s, 2:4], Y[:, :, OPCODE_BASE + OPC_ADD:OPCODE_BASE + OPC_SUB + 1])
            dve.drain()

            def features(g):
                dve.tensor_copy(FG, FT[:, bass.ds(g, 1), :, :].rearrange("p a s f -> p (a s) f")).then_inc(f_in, 1)
                dve.wait_ge(f_ps, g + 1)
                dve.tensor_copy(FS, PS[0][0:NF, 0:2 * P]).then_inc(f_sb, 1)

            def results(g):
                dve.wait_ge(y_ps, g + 1)
                dve.tensor_copy(res[:, bass.ds(g * RW, RW)], PS[7][:, 0:RW]).then_inc(y_sb, 1)

            dve.sem_inc(y_sb, ONE)
            features(0)
            dve.tensor_tensor(adds, mark, op_add, ALU.mult)
            dve.tensor_tensor(both, mark, op_sub, ALU.mult)
            dve.drain()
            dve.tensor_tensor(subs, both, op_add, ALU.mult)
            dve.drain()
            dve.tensor_tensor(subs, both, subs, ALU.subtract)
            dve.drain()
            dve.tensor_tensor(active, adds, subs, ALU.add)
            dve.drain()
            dve.tensor_scalar(active2, active, 2.0, None, ALU.mult)
            with dve.Fori(0, NT - 1) as g:
                features(g + 1)
                results(g)
            results(NT - 1)
            dve.drain()
            r4 = res.rearrange("p (q a n) -> p q a n", a=2, n=2)
            rq = res.rearrange("p (q n) -> p q n", n=4)
            dve.tensor_tensor(rq, rq, BO.rearrange("p a n -> p (a n)").unsqueeze(1).to_broadcast((P, 2 * NT, 4)), ALU.add)
            dve.drain()
            w = lambda v: v.to_broadcast((P, NT, 4))
            t4 = lambda v: v.rearrange("p (t s) n -> p t (s n)", s=2)
            dve.tensor_copy(y, r4[:, :, 0, :])
            dve.tensor_copy(y2, r4[:, :, 1, :])
            dve.drain()
            dve.tensor_tensor(t4(y), t4(y), w(adds), ALU.mult)
            dve.tensor_tensor(t4(y2), t4(y2), w(subs), ALU.mult)
            dve.drain()
            dve.tensor_tensor(y, y, y2, ALU.add)
            dve.drain()
            dve.tensor_scalar(y, y, ROUND, ROUND, ALU.add, ALU.subtract)
            dve.drain()
            dve.tensor_scalar(y[:, :, 0:1], y[:, :, 0:1], 0.0, 15.0, ALU.max, ALU.min)
            dve.tensor_scalar(y2[:, :, 1:2], y[:, :, 1:2], 0.5, None, ALU.is_gt)
            dve.drain()
            dve.tensor_tensor(oh.rearrange("p t s n -> p (t s) n"), m.iota_f[:, 0:16].unsqueeze(1).to_broadcast((P, 2 * NT, 16)),
                              y[:, :, 0:1].to_broadcast((P, 2 * NT, 16)), ALU.is_equal)
            carry = y2.rearrange("p (t s) n -> p t s n", s=2)[:, :, 1, 1:2]
            dve.tensor_tensor(carry, carry, active, ALU.mult)
            dve.drain()
            o = oh.rearrange("p t s n -> p t (s n)")
            dve.tensor_tensor(o, o, active2.to_broadcast((P, NT, 32)), ALU.mult)
            dve.drain()
            dve.tensor_tensor(Y[:, :, OUTPUT_LO:CARRY], Y[:, :, OUTPUT_LO:CARRY], o, ALU.add)
            dve.tensor_tensor(Y[:, :, CARRY:CARRY + 1], Y[:, :, CARRY:CARRY + 1], carry, ALU.add)
            dve.drain()
            for i in range(NT):
                dve.tensor_tensor(m.X[:, i, :], m.X[:, i, :], Y[:, i, :], ALU.add).then_inc(out_ready, 1)

        @block.scalar
        def _(act):
            def relu(g, layer):
                ps, sbuf, first, rest = ((h1_ps, h1_sb, H1a, H1r), (h2_ps, h2_sb, H2a, H2r))[layer]
                act.wait_ge(ps, g + 1)
                for a in range(2):
                    half = slice(a * 2 * P, (a + 1) * 2 * P)
                    act.activation(first[:, half], PS[1 + 2 * layer][:, half], ACT.Relu, bias=Ba[:, a, layer:layer + 1])
                act.activation(rest, PS[2 + 2 * layer][0:2 * REM, 0:2 * P], ACT.Relu, bias=Br[:, layer:layer + 1])
                act.drain().then_inc(sbuf, 1)

            relu(0, 0)
            with act.Fori(0, NT - 1) as g:
                relu(g, 1)
                relu(g + 1, 0)
            relu(NT - 1, 1)

        @block.tensor
        def _(pe):
            def transposes(g):
                pe.wait_ge(f_in, g + 1)
                for s in range(2):
                    ins = pe.transpose(PS[0][0:NF, s * P:(s + 1) * P], FG[:, s, :], m.ident[:, :])
                ins.then_inc(f_ps, 1)

            def layer1(g):
                pe.wait_ge(f_sb, g + 1)
                for a in range(2):
                    pe.matmul(PS[1][:, a * 2 * P:(a + 1) * 2 * P], W0[:, a, :], FS, start=True, stop=True)
                pe.matmul(PS[2][0:2 * REM, 0:2 * P], W0r, FS, start=True, stop=True).then_inc(h1_ps, 1)

            def layer2(g):
                pe.wait_ge(h1_sb, g + 1)
                for a in range(2):
                    half = slice(a * 2 * P, (a + 1) * 2 * P)
                    pe.matmul(PS[3][:, half], W1aa[:, a, :], H1a[:, half], start=True, stop=False)
                    pe.matmul(PS[3][:, half], W1ra[:, a, :], H1r, start=False, stop=True)
                rest = PS[4][0:2 * REM, 0:2 * P]
                pe.matmul(rest, W1rr, H1r, start=True, stop=False)
                pe.matmul(rest, W1ar[:, 0, :], H1a[:, 0:2 * P], start=False, stop=False)
                pe.matmul(rest, W1ar[:, 1, :], H1a[:, 2 * P:4 * P], start=False, stop=True).then_inc(h2_ps, 1)

            def layer3(g):
                pe.wait_ge(h2_sb, g + 1)
                pe.wait_ge(y_sb, ONE + g)
                for s in range(2):
                    pe.matmul(PS[7][:, s * 4:s * 4 + 4], H2r[:, s * P:(s + 1) * P], W2r, start=True, stop=False, skip_group_check=True)
                    for a in range(2):
                        at, q = (s * 2 + a) * 2, (a * 2 + s) * P
                        ins = pe.matmul(PS[7][:, at:at + 2], H2a[:, q:q + P], W2a[:, a * 2:a * 2 + 2], start=False, stop=True, skip_group_check=True)
                ins.then_inc(y_ps, 1)

            transposes(0)
            layer1(0)
            with pe.Fori(0, NT - 1) as g:
                transposes(g + 1)
                layer2(g)
                layer1(g + 1)
                layer3(g)
            layer2(NT - 1)
            layer3(NT - 1)


_PLAIN = ["x", "src", "dst", "edge_type_4", "edge_type_8", "edge_weight", "L0_gnn_W", "L0_gnn_a_src", "L0_gnn_a_dst",
          "L0_gnn_et_emb", "L0_ffn_Wg", "L0_ffn_W1", "L0_ffn_W2", "L0_ffn_b2", "L1_gnn_self_W", "L1_gnn_rel_W",
          "L1_gnn_rel_b", "L1_gnn_W1", "L1_gnn_W2", "L1_ffn_ba", "L1_ffn_bs"] + ROW_NAMES


def kernel(**inputs):
    import concourse.bacc as _bacc
    from concourse.bass_utils import run_bass_kernel_spmd as _run

    a = {name: np.ascontiguousarray(inputs[name]) for name in _PLAIN}
    a["L0_gnn_WT"] = np.ascontiguousarray(np.asarray(inputs["L0_gnn_W"]).T)
    a["L0_ffn_b1_cols"] = np.ascontiguousarray(np.asarray(inputs["L0_ffn_b1"]).reshape(-1, P).T)
    a["L1_gnn_b1_cols"] = np.ascontiguousarray(np.asarray(inputs["L1_gnn_b1"]).reshape(-1, P).T)
    for w, b in (("L1_ffn_Wa", "L1_ffn_ba"), ("L1_ffn_Ws", "L1_ffn_bs")):
        a[w + "_T"] = np.ascontiguousarray(np.asarray(inputs[w]).transpose(0, 2, 1))
        a[b + "_cols"] = np.ascontiguousarray(np.asarray(inputs[b]).T)

    nc = _bacc.Bacc("TRN2", target_bir_lowering=False, num_devices=1)
    t = {name: nc.dram_tensor("in_" + name, v.shape, mybir.dt.from_np(v.dtype), kind="ExternalInput").ap() for name, v in a.items()}
    t["out"] = nc.dram_tensor("out", (N, D), F32, kind="ExternalOutput").ap()
    build(nc, t)
    r = _run(nc, [{"in_" + name: v for name, v in a.items()}], core_ids=[0])
    return r.results[0]["out"]
```
